# Optimizing a Trainium2 kernel written in Bass

```python
import numpy as np
import jax
import jax.numpy as jnp

def _softmax(x, axis=-1):
    return jax.nn.softmax(x, axis=axis)

def _gelu(x):
    return jax.nn.gelu(x, approximate=True)

def _silu(x):
    return jax.nn.silu(x)

def _sigmoid(x):
    return jax.nn.sigmoid(x)

def _layernorm(x, axis=-1, eps=1e-05):
    m = jnp.mean(x, axis=axis, keepdims=True)
    v = jnp.var(x, axis=axis, keepdims=True)
    return (x - m) / jnp.sqrt(v + eps)

def _scatter_add(tgt, idx, src, axis=0):
    return tgt.at[idx].add(src)

def _segment_sum(src, seg, n):
    return jax.ops.segment_sum(src, seg, n)
kernel_name = 'mk_seq_preln_d2_jaxref_r4_617ecc'

def setup_inputs(seed: int=0):
    np.random.seed(seed)
    _w = jnp.asarray

    def _L0_attn_setup():
        import jax, jax.numpy as jnp
        import numpy as np
        N_HEADS = 16
        BUCKETS = 64
        MAX_REL = 128
        ATT_SPAN = BUCKETS
        LN_EPS = 1e-07

        def make_log_bucket_position(relative_pos, bucket_size, max_position):
            sign = jnp.sign(relative_pos)
            mid = bucket_size // 2
            abs_pos = jnp.where((relative_pos < mid) & (relative_pos > -mid), mid - 1, jnp.abs(relative_pos))
            log_pos = jnp.ceil(jnp.log(abs_pos / mid) / jnp.log((max_position - 1) / mid) * (mid - 1)) + mid
            bucket_pos = jnp.where(abs_pos <= mid, abs_pos, log_pos * sign)
            return bucket_pos.astype(jnp.int32)

        def build_relative_position(q_size, k_size, bucket_size, max_position):
            rel = jnp.arange(q_size)[:, None] - jnp.arange(k_size)[None, :]
            rel = make_log_bucket_position(rel, bucket_size, max_position)
            return rel.astype(jnp.int32)
        key = jax.random.key(seed)
        ks = jax.random.split(key, 16)
        B, S, H = (4, 256, 256)
        std = 0.02
        inp = {'hidden_states': jax.random.normal(ks[0], (B, S, H), jnp.float32), 'attention_mask': jnp.ones((B, S), jnp.float32), 'rel_embeddings': jax.random.normal(ks[1], (2 * ATT_SPAN, H), jnp.float32) * std, 'Wq': jax.random.normal(ks[2], (H, H), jnp.float32) * std, 'bq': jnp.zeros((H,), jnp.float32), 'Wk': jax.random.normal(ks[3], (H, H), jnp.float32) * std, 'bk': jnp.zeros((H,), jnp.float32), 'Wv': jax.random.normal(ks[4], (H, H), jnp.float32) * std, 'bv': jnp.zeros((H,), jnp.float32), 'Wo': jax.random.normal(ks[5], (H, H), jnp.float32) * std, 'bo': jnp.zeros((H,), jnp.float32), 'ln_scale': jnp.ones((H,), jnp.float32), 'ln_bias': jnp.zeros((H,), jnp.float32)}
        return inp
    _L0_attn_in = _L0_attn_setup()

    def _L0_ffn_setup():
        import jax, jax.numpy as jnp
        import numpy as np
        LORA_DIM = 16
        LORA_TOKEN_INDEX = 1
        B, S, D, H = (4, 512, 256, 1024)
        key = jax.random.key(seed)
        ks = jax.random.split(key, 6)
        x = jax.random.normal(ks[0], (B, S, D), dtype=jnp.float32)
        W1 = jax.random.normal(ks[1], (H, D), dtype=jnp.float32) * 0.02
        b1 = jnp.zeros((H,), dtype=jnp.float32)
        W2 = jax.random.normal(ks[2], (D, H), dtype=jnp.float32) * 0.02
        b2 = jnp.zeros((D,), dtype=jnp.float32)
        scale = jnp.asarray(0.001, dtype=jnp.float32)
        return {'x': x, 'W1': W1, 'b1': b1, 'W2': W2, 'b2': b2, 'scale': scale}
    _L0_ffn_in = _L0_ffn_setup()

    def _L1_attn_setup():
        import jax, jax.numpy as jnp
        import numpy as np
        N, B, C = (72, 64, 256)
        H = 16
        P_PER_TASK = 4
        NUM_TASKS = 7

        def _prompt_mask(n, p, num_tasks, dtype):
            P = (num_tasks + 1) * p
            r = jnp.arange(n)[:, None]
            c = jnp.arange(n)[None, :]
            blocked = (c < P) & ~((r < P) & (r >= c // p * p))
            return jnp.where(blocked, -jnp.inf, 0.0).astype(dtype)
        key = jax.random.key(seed)
        k1, k2, k3 = jax.random.split(key, 3)
        x = jax.random.normal(k1, (N, B, C), dtype=jnp.float32)
        Wqkv = jax.random.normal(k2, (3 * C, C), dtype=jnp.float32) * 0.02
        bqkv = jnp.zeros((3 * C,), dtype=jnp.float32)
        Wproj = jax.random.normal(k3, (C, C), dtype=jnp.float32) * 0.02
        bproj = jnp.zeros((C,), dtype=jnp.float32)
        return {'x': x, 'Wqkv': Wqkv, 'bqkv': bqkv, 'Wproj': Wproj, 'bproj': bproj}
    _L1_attn_in = _L1_attn_setup()

    def _L1_ffn_setup():
        import jax, jax.numpy as jnp
        import numpy as np
        from jax import lax
        B, S, H = (2, 256, 256)
        I = 128
        E = 32
        TOP_K = 4
        N_GROUP = 4
        TOPK_GROUP = 2
        SCALE = 2.5
        N_SHARED = 2
        SH_I = I * N_SHARED

        def _route(tokens, router_weight, router_bias):
            logits = tokens.astype(jnp.float32) @ router_weight.astype(jnp.float32).T
            scores = jax.nn.sigmoid(logits)
            sfc = scores + router_bias[None, :]
            T = tokens.shape[0]
            grp = sfc.reshape(T, N_GROUP, E // N_GROUP)
            group_scores = lax.top_k(grp, 2)[0].sum(-1)
            _, gidx = lax.top_k(group_scores, TOPK_GROUP)
            gmask = jax.nn.one_hot(gidx, N_GROUP, dtype=sfc.dtype).sum(1)
            smask = jnp.broadcast_to(gmask[:, :, None], (T, N_GROUP, E // N_GROUP)).reshape(T, E)
            tmp = jnp.where(smask > 0, sfc, 0.0)
            _, topk_idx = lax.top_k(tmp, TOP_K)
            topk_w = jnp.take_along_axis(scores, topk_idx, axis=1)
            topk_w = topk_w / (topk_w.sum(-1, keepdims=True) + 1e-20)
            topk_w = topk_w * SCALE
            return (topk_idx, topk_w)
        key = jax.random.key(seed)
        ks = jax.random.split(key, 10)
        std = 0.02
        return {'hidden_states': jax.random.normal(ks[0], (B, S, H), jnp.float32), 'router_weight': jax.random.normal(ks[1], (E, H), jnp.float32) * std, 'router_bias': jnp.zeros((E,), jnp.float32), 'gate_w': jax.random.normal(ks[2], (E, I, H), jnp.float32) * std, 'up_w': jax.random.normal(ks[3], (E, I, H), jnp.float32) * std, 'down_w': jax.random.normal(ks[4], (E, H, I), jnp.float32) * std, 'shared_gate_w': jax.random.normal(ks[5], (SH_I, H), jnp.float32) * std, 'shared_up_w': jax.random.normal(ks[6], (SH_I, H), jnp.float32) * std, 'shared_down_w': jax.random.normal(ks[7], (H, SH_I), jnp.float32) * std}
    _L1_ffn_in = _L1_ffn_setup()
    _d = {'L0_attn_hidden_states': _L0_attn_in['hidden_states'], 'L0_attn_attention_mask': _L0_attn_in['attention_mask'], 'L0_attn_rel_embeddings': _L0_attn_in['rel_embeddings'], 'L0_attn_Wq': _L0_attn_in['Wq'], 'L0_attn_bq': _L0_attn_in['bq'], 'L0_attn_Wk': _L0_attn_in['Wk'], 'L0_attn_bk': _L0_attn_in['bk'], 'L0_attn_Wv': _L0_attn_in['Wv'], 'L0_attn_bv': _L0_attn_in['bv'], 'L0_attn_Wo': _L0_attn_in['Wo'], 'L0_attn_bo': _L0_attn_in['bo'], 'L0_attn_ln_scale': _L0_attn_in['ln_scale'], 'L0_attn_ln_bias': _L0_attn_in['ln_bias'], 'L0_ffn_W1': _L0_ffn_in['W1'], 'L0_ffn_b1': _L0_ffn_in['b1'], 'L0_ffn_W2': _L0_ffn_in['W2'], 'L0_ffn_b2': _L0_ffn_in['b2'], 'L0_ffn_scale': _L0_ffn_in['scale'], 'L1_attn_Wqkv': _L1_attn_in['Wqkv'], 'L1_attn_bqkv': _L1_attn_in['bqkv'], 'L1_attn_Wproj': _L1_attn_in['Wproj'], 'L1_attn_bproj': _L1_attn_in['bproj'], 'L1_ffn_router_weight': _L1_ffn_in['router_weight'], 'L1_ffn_router_bias': _L1_ffn_in['router_bias'], 'L1_ffn_gate_w': _L1_ffn_in['gate_w'], 'L1_ffn_up_w': _L1_ffn_in['up_w'], 'L1_ffn_down_w': _L1_ffn_in['down_w'], 'L1_ffn_shared_gate_w': _L1_ffn_in['shared_gate_w'], 'L1_ffn_shared_up_w': _L1_ffn_in['shared_up_w'], 'L1_ffn_shared_down_w': _L1_ffn_in['shared_down_w']}
    _x0 = _d['L0_attn_hidden_states']
    _d['L0_attn_hidden_states'] = jax.random.normal(jax.random.fold_in(jax.random.key(seed), 1), (8, 512, 256), dtype=_x0.dtype)
    del _x0
    return _d

def reference(L0_attn_hidden_states, L0_attn_attention_mask, L0_attn_rel_embeddings, L0_attn_Wq, L0_attn_bq, L0_attn_Wk, L0_attn_bk, L0_attn_Wv, L0_attn_bv, L0_attn_Wo, L0_attn_bo, L0_attn_ln_scale, L0_attn_ln_bias, L0_ffn_W1, L0_ffn_b1, L0_ffn_W2, L0_ffn_b2, L0_ffn_scale, L1_attn_Wqkv, L1_attn_bqkv, L1_attn_Wproj, L1_attn_bproj, L1_ffn_router_weight, L1_ffn_router_bias, L1_ffn_gate_w, L1_ffn_up_w, L1_ffn_down_w, L1_ffn_shared_gate_w, L1_ffn_shared_up_w, L1_ffn_shared_down_w):

    def _L0_attn_ref(hidden_states, attention_mask, rel_embeddings, Wq, bq, Wk, bk, Wv, bv, Wo, bo, ln_scale, ln_bias):
        import jax, jax.numpy as jnp
        import numpy as np
        N_HEADS = 16
        BUCKETS = 64
        MAX_REL = 128
        ATT_SPAN = BUCKETS
        LN_EPS = 1e-07

        def make_log_bucket_position(relative_pos, bucket_size, max_position):
            sign = jnp.sign(relative_pos)
            mid = bucket_size // 2
            abs_pos = jnp.where((relative_pos < mid) & (relative_pos > -mid), mid - 1, jnp.abs(relative_pos))
            log_pos = jnp.ceil(jnp.log(abs_pos / mid) / jnp.log((max_position - 1) / mid) * (mid - 1)) + mid
            bucket_pos = jnp.where(abs_pos <= mid, abs_pos, log_pos * sign)
            return bucket_pos.astype(jnp.int32)

        def build_relative_position(q_size, k_size, bucket_size, max_position):
            rel = jnp.arange(q_size)[:, None] - jnp.arange(k_size)[None, :]
            rel = make_log_bucket_position(rel, bucket_size, max_position)
            return rel.astype(jnp.int32)
        B, S, H = hidden_states.shape
        nH = N_HEADS
        d = H // nH

        def split_heads(x):
            return jnp.transpose(x.reshape(B, S, nH, d), (0, 2, 1, 3))
        q = split_heads(hidden_states @ Wq + bq)
        k = split_heads(hidden_states @ Wk + bk)
        v = split_heads(hidden_states @ Wv + bv)
        scale_factor = 3
        scale = jnp.sqrt(jnp.asarray(d * scale_factor, hidden_states.dtype))
        scores = jnp.einsum('bhqd,bhkd->bhqk', q, k) / scale
        rel = build_relative_position(S, S, BUCKETS, MAX_REL)
        pos_k = (rel_embeddings @ Wk + bk).reshape(2 * ATT_SPAN, nH, d)
        pos_k = jnp.transpose(pos_k, (1, 0, 2))
        c2p_att = jnp.einsum('bhqd,hpd->bhqp', q, pos_k)
        c2p_pos = jnp.clip(rel + ATT_SPAN, 0, 2 * ATT_SPAN - 1)
        c2p = jnp.take_along_axis(c2p_att, jnp.broadcast_to(c2p_pos[None, None], (B, nH, S, S)), axis=-1)
        p2c_pos = jnp.clip(-rel + ATT_SPAN, 0, 2 * ATT_SPAN - 1)
        p2c_att = jnp.einsum('bhkd,hpd->bhkp', k, pos_k)
        p2c = jnp.take_along_axis(p2c_att, jnp.broadcast_to(p2c_pos[None, None], (B, nH, S, S)), axis=-1)
        p2c = jnp.swapaxes(p2c, -1, -2)
        scores = scores + (c2p + p2c) / scale
        probs = jax.nn.softmax(scores, axis=-1)
        ctx = jnp.einsum('bhqk,bhkd->bhqd', probs, v)
        ctx = jnp.transpose(ctx, (0, 2, 1, 3)).reshape(B, S, H)
        out = ctx @ Wo + bo + hidden_states
        mu = jnp.mean(out, axis=-1, keepdims=True)
        var = jnp.mean(jnp.square(out - mu), axis=-1, keepdims=True)
        out = (out - mu) * jax.lax.rsqrt(var + LN_EPS) * ln_scale + ln_bias
        return out

    def _L0_ffn_ref(x, W1, b1, W2, b2, scale):
        import jax, jax.numpy as jnp
        import numpy as np
        LORA_DIM = 16
        LORA_TOKEN_INDEX = 1
        B, S, D, H = (4, 512, 256, 1024)
        Bx, Sx, Dx = x.shape
        Hx = W1.shape[0]
        lt = jax.lax.dynamic_slice_in_dim(x, LORA_TOKEN_INDEX, LORA_DIM, axis=1)
        even = lt[:, ::2, :]
        odd = lt[:, 1::2, :]
        m1 = (even[:, :4, :, None] * odd[:, :4, None, :]).reshape(Bx, Hx, Dx)
        m2 = (even[:, 4:, :, None] * odd[:, 4:, None, :]).reshape(Bx, Dx, Hx)
        h = jnp.einsum('bsd,hd->bsh', x, W1) + scale * jnp.einsum('bsd,bhd->bsh', x, m1) + b1
        h = jax.nn.gelu(h, approximate=False)
        out = jnp.einsum('bsh,oh->bso', h, W2) + scale * jnp.einsum('bsh,boh->bso', h, m2) + b2
        return out

    def _L1_attn_ref(x, Wqkv, bqkv, Wproj, bproj):
        import jax, jax.numpy as jnp
        import numpy as np
        N, B, C = (72, 64, 256)
        H = 16
        P_PER_TASK = 4
        NUM_TASKS = 7

        def _prompt_mask(n, p, num_tasks, dtype):
            P = (num_tasks + 1) * p
            r = jnp.arange(n)[:, None]
            c = jnp.arange(n)[None, :]
            blocked = (c < P) & ~((r < P) & (r >= c // p * p))
            return jnp.where(blocked, -jnp.inf, 0.0).astype(dtype)
        n, b, ch = x.shape
        hd = ch // H
        scale = hd ** (-0.5)
        qkv = x @ Wqkv.T + bqkv
        q, k, v = jnp.split(qkv, 3, axis=-1)
        to_heads = lambda t: t.reshape(n, b * H, hd).transpose(1, 0, 2)
        q, k, v = (to_heads(q), to_heads(k), to_heads(v))
        mask = _prompt_mask(n, P_PER_TASK, NUM_TASKS, x.dtype)
        scores = mask + scale * jnp.einsum('bnd,bmd->bnm', q, k)
        attn = jax.nn.softmax(scores, axis=-1)
        out = jnp.einsum('bnm,bmd->bnd', attn, v)
        out = out.transpose(1, 0, 2).reshape(n, b, ch)
        return out @ Wproj.T + bproj

    def _L1_ffn_ref(hidden_states, router_weight, router_bias, gate_w, up_w, down_w, shared_gate_w, shared_up_w, shared_down_w):
        import jax, jax.numpy as jnp
        import numpy as np
        from jax import lax
        B, S, H = (2, 256, 256)
        I = 128
        E = 32
        TOP_K = 4
        N_GROUP = 4
        TOPK_GROUP = 2
        SCALE = 2.5
        N_SHARED = 2
        SH_I = I * N_SHARED

        def _route(tokens, router_weight, router_bias):
            logits = tokens.astype(jnp.float32) @ router_weight.astype(jnp.float32).T
            scores = jax.nn.sigmoid(logits)
            sfc = scores + router_bias[None, :]
            T = tokens.shape[0]
            grp = sfc.reshape(T, N_GROUP, E // N_GROUP)
            group_scores = lax.top_k(grp, 2)[0].sum(-1)
            _, gidx = lax.top_k(group_scores, TOPK_GROUP)
            gmask = jax.nn.one_hot(gidx, N_GROUP, dtype=sfc.dtype).sum(1)
            smask = jnp.broadcast_to(gmask[:, :, None], (T, N_GROUP, E // N_GROUP)).reshape(T, E)
            tmp = jnp.where(smask > 0, sfc, 0.0)
            _, topk_idx = lax.top_k(tmp, TOP_K)
            topk_w = jnp.take_along_axis(scores, topk_idx, axis=1)
            topk_w = topk_w / (topk_w.sum(-1, keepdims=True) + 1e-20)
            topk_w = topk_w * SCALE
            return (topk_idx, topk_w)
        tokens = hidden_states.reshape(-1, H)
        topk_idx, topk_w = _route(tokens, router_weight, router_bias)
        gate_vals = jax.nn.silu(jnp.einsum('th,eih->tei', tokens, gate_w))
        up_vals = jnp.einsum('th,eih->tei', tokens, up_w)
        hidden_vals = gate_vals * up_vals
        expert_out = jnp.einsum('tei,ehi->teh', hidden_vals, down_w)
        sel = jnp.take_along_axis(expert_out, topk_idx[:, :, None], axis=1)
        mixed = (sel * topk_w[:, :, None].astype(sel.dtype)).sum(1)
        mixed = mixed.reshape(hidden_states.shape)
        sg = jax.nn.silu(jnp.einsum('bsh,ih->bsi', hidden_states, shared_gate_w))
        su = jnp.einsum('bsh,ih->bsi', hidden_states, shared_up_w)
        shared = jnp.einsum('bsi,hi->bsh', sg * su, shared_down_w)
        return mixed + shared
    x = L0_attn_hidden_states
    x = x + _L0_attn_ref(_layernorm(x, axis=-1), L0_attn_attention_mask, L0_attn_rel_embeddings, L0_attn_Wq, L0_attn_bq, L0_attn_Wk, L0_attn_bk, L0_attn_Wv, L0_attn_bv, L0_attn_Wo, L0_attn_bo, L0_attn_ln_scale, L0_attn_ln_bias)
    x = x + _L0_ffn_ref(_layernorm(x, axis=-1), L0_ffn_W1, L0_ffn_b1, L0_ffn_W2, L0_ffn_b2, L0_ffn_scale)
    x = x + _L1_attn_ref(_layernorm(x, axis=-1), L1_attn_Wqkv, L1_attn_bqkv, L1_attn_Wproj, L1_attn_bproj)
    x = x + _L1_ffn_ref(_layernorm(x, axis=-1), L1_ffn_router_weight, L1_ffn_router_bias, L1_ffn_gate_w, L1_ffn_up_w, L1_ffn_down_w, L1_ffn_shared_gate_w, L1_ffn_shared_up_w, L1_ffn_shared_down_w)
    return x

_drawn_inputs = setup_inputs


def setup_inputs(seed=0):
    import zlib

    import numpy as np

    out = dict(_drawn_inputs(seed))
    spreads = {'L0_attn_bq': (0.0, 0.8),
     'L0_attn_bk': (0.0, 0.8),
     'L0_attn_bv': (0.0, 0.487),
     'L0_attn_bo': (0.0, 0.1),
     'L0_attn_ln_scale': (1.0, 0.2),
     'L0_attn_ln_bias': (0.0, 0.1),
     'L0_ffn_b1': (0.0, 0.447),
     'L0_ffn_b2': (0.0, 0.1),
     'L1_attn_bqkv': (0.0, 0.521),
     'L1_attn_bproj': (0.0, 0.1),
     'L1_ffn_router_bias': (0.0, 0.8)}
    factors = {'L0_attn_rel_embeddings': 8.0,
     'L0_attn_Wq': 8.0,
     'L0_attn_Wk': 8.0,
     'L0_attn_Wv': 8.0,
     'L0_attn_Wo': 3.618,
     'L1_ffn_router_weight': 8.0,
     'L1_ffn_gate_w': 7.665,
     'L1_ffn_up_w': 7.591,
     'L1_ffn_down_w': 7.584,
     'L1_ffn_shared_gate_w': 6.852,
     'L1_ffn_shared_up_w': 6.798,
     'L1_ffn_shared_down_w': 6.802}
    for name, (base, spread) in spreads.items():
        noise = np.random.default_rng([zlib.crc32(name.encode()), seed]).standard_normal(out[name].shape)
        drawn = base * np.exp(spread * noise) if base else spread * noise
        out[name] = jnp.asarray(drawn.astype(out[name].dtype))
    for name, factor in factors.items():
        out[name] = (out[name] * factor).astype(out[name].dtype)
    return out
```

```python
from contextlib import ExitStack

import numpy as np

B, S, C = 8, 512, 256
P = 128
H, D = 16, 16
TILES = B * S // P
TPB = S // P
CC = C // P
REL = 128
SPAN, MAX_POS = 64, 128
NEAR = 3 * P
DIST = 512
R = 8
KCHUNK = 64
STACK = 6
FFN = 1024
EXPERTS, INNER, TOP_K, GROUPS, TOP_GROUPS = 32, 128, 4, 4, 2
ROUTE_SCALE = 2.5
SHARED = 2
ALL_EXPERTS = EXPERTS + SHARED


def bucket_indices(delta):
    mid = SPAN // 2
    f = np.float32

    def bucket(rel):
        a = np.where((rel < mid) & (rel > -mid), mid - 1, np.abs(rel))
        log = np.ceil(np.log((a / f(mid)).astype(f)) / np.log(f((MAX_POS - 1) / mid)) * f(mid - 1)) + mid
        return np.where(a <= mid, a, log * np.sign(rel)).astype(np.int32)

    c2p = np.clip(bucket(delta) + SPAN, 0, 2 * SPAN - 1)
    p2c = np.clip(-bucket(-delta) + SPAN, 0, 2 * SPAN - 1)
    return c2p, p2c


def one_hot_tables():
    c2p, _ = bucket_indices(DIST // 2 - 1 - np.arange(DIST))
    _, p2c = bucket_indices(np.arange(DIST) - (DIST // 2 - 1))
    rows = np.arange(REL)[:, None]
    return (rows == c2p[None]).astype(np.float32), (rows == p2c[None]).astype(np.float32)


def build(nc, a, out, taps=None):
    import concourse.bass as bass
    from concourse import mybir

    F32, BF16, U32 = mybir.dt.float32, mybir.dt.bfloat16, mybir.dt.uint32
    ACT, ALU, AX = mybir.ActivationFunctionType, mybir.AluOpType, mybir.AxisListType
    ds = bass.ds
    whole = ExitStack()
    with whole:
        def sem(name):
            return whole.enter_context(nc.semaphore(name))

        def sb(stack, name, shape, dt=F32):
            return stack.enter_context(nc.sbuf_tensor(name, shape, dt))

        def dram(name, shape, dt):
            return nc.dram_tensor(name, shape, dt, kind="Internal").ap()

        bank = [whole.enter_context(nc.psum_tensor(f"bank{i}", [P, 512], F32)) for i in range(8)]
        ident = sb(whole, "ident", [P, P])
        spacer = sem("spacer")
        ident_zeroed, ident_ready = sem("ident_zeroed"), sem("ident_ready")

        normed_d = dram("normed_d", [B, P, TPB, C], F32)
        q_stack_d = dram("q_stack_d", [H, STACK, D, B * S], BF16)
        qf_stack_d = dram("qf_stack_d", [H, STACK, D, B * S], BF16)
        k_stack_d = dram("k_stack_d", [H, STACK, D, B * S], BF16)
        c2p_stack_d = dram("c2p_stack_d", [H, STACK, D, DIST], BF16)
        k_by_r_d = dram("k_by_r_d", [C, 3, R, B, S // R], BF16)
        p2c_parts_d = dram("p2c_parts_d", [C, 3, DIST], BF16)
        c2p_d = dram("c2p_d", [2, B, P, DIST], F32)
        ctxT_d = dram("ctxT_d", [C, B, S], F32)

        def batches(eng, body):
            for b in range(2):
                body(b, b)
            with eng.Fori(1, B // 2 - 1) as i:
                for u in range(2):
                    body(2 * i + u, u)
            for u in range(2):
                body(B - 2 + u, u)

        def each_batch(eng, body):
            with eng.Fori(0, B // 2 - 1) as i:
                for u in range(2):
                    body(2 * i + u, u)
            for u in range(2):
                body(B - 2 + u, u)

        def exists(b, ahead):
            return not isinstance(b, int) or b + ahead < B

        def apart(eng):
            eng.sem_inc(spacer, 1)

        def layer_norm(name, stack, tiles):
            n = {"tiles": tiles}
            n["stats"] = sb(stack, name + "_stats", [P, tiles, 6])
            n["mv"] = sb(stack, name + "_mv", [P, tiles, 2])
            for k in ("var", "std", "rstd", "tmp"):
                n[k] = sb(stack, f"{name}_{k}", [P, tiles])
            for k in ("stats_done", "mv_done", "var_done", "std_done", "rstd_step", "normed"):
                n[k] = sem(f"{name}_{k}")
            return n

        def ln_moments(dve, n, k, source, eps):
            T = n["tiles"]
            for s in range(T):
                dve.bn_stats(n["stats"][:, s, :], source(s)).then_inc(n["stats_done"], 1)
            dve.wait_ge(n["stats_done"], T * k + T)
            apart(dve)
            for s in range(T):
                dve.bn_aggr(n["mv"][:, s, :], n["stats"][:, s, :]).then_inc(n["mv_done"], 1)
            dve.wait_ge(n["mv_done"], T * k + T)
            dve.tensor_scalar(n["var"][:], n["mv"][:, :, 1], eps, None, ALU.add).then_inc(n["var_done"], 1)

        def ln_std(act, n, k):
            act.wait_ge(n["var_done"], k + 1)
            act.activation(n["std"][:], n["var"][:], ACT.Sqrt).then_inc(n["std_done"], 1)

        def ln_normalize(dve, n, k, source, dest):
            T, step = n["tiles"], n["rstd_step"]
            dve.wait_ge(n["std_done"], k + 1)
            dve.reciprocal(n["rstd"][:], n["std"][:]).then_inc(step, 1)
            dve.wait_ge(step, 5 * k + 1)
            dve.tensor_tensor(n["tmp"][:], n["rstd"][:], n["rstd"][:], ALU.mult).then_inc(step, 1)
            dve.wait_ge(step, 5 * k + 2)
            dve.tensor_tensor(n["tmp"][:], n["tmp"][:], n["var"][:], ALU.mult).then_inc(step, 1)
            dve.wait_ge(step, 5 * k + 3)
            dve.tensor_scalar(n["tmp"][:], n["tmp"][:], -0.5, 1.5, ALU.mult, ALU.add).then_inc(step, 1)
            dve.wait_ge(step, 5 * k + 4)
            dve.tensor_tensor(n["rstd"][:], n["rstd"][:], n["tmp"][:], ALU.mult).then_inc(step, 1)
            dve.wait_ge(step, 5 * k + 5)
            for s in range(T):
                dve.tensor_scalar(dest(s), source(s), n["mv"][:, s, 0:1], n["rstd"][:, s:s + 1],
                                  ALU.subtract, ALU.mult).then_inc(n["normed"], 1)

        attn = ExitStack()
        v_all = sb(attn, "v_all", [P, TILES, C])

        CH = 3 * CC
        with ExitStack() as st:
            x_in = sb(st, "p1_x", [P, 2, TPB, C])
            normed = sb(st, "p1_normed", [P, 2, TPB, C])
            nT = sb(st, "p1_nT", [P, CC, S])
            wq, wk, wv = [sb(st, n, [P, CC, C]) for n in ("p1_wq", "p1_wk", "p1_wv")]
            bq, bk = sb(st, "p1_bq", [P, CC]), sb(st, "p1_bk", [P, CC])
            bq_far = sb(st, "p1_bq_far", [P, CC, 2])
            bk_row, bv_row = sb(st, "p1_bk_row", [P, C]), sb(st, "p1_bv_row", [P, 2, C])
            relT = sb(st, "p1_relT", [P, CC, REL])
            hot = sb(st, "p1_hot", [P, 2, DIST])
            pos_k = sb(st, "p1_pos_k", [P, C])
            full = sb(st, "p1_full", [P, CH, S])
            rest = sb(st, "p1_rest", [P, CH, S])
            parts = sb(st, "p1_parts", [P, CH, 3, S], BF16)
            k_by_r = sb(st, "p1_k_by_r", [P, CC, 3, R, S // R], BF16)
            tab = sb(st, "p1_tab", [P, 2 * CC, DIST])
            tab_rest = sb(st, "p1_tab_rest", [P, 2 * CC, DIST])
            tab_parts = sb(st, "p1_tab_parts", [P, 2 * CC, 3, DIST], BF16)
            ln = layer_norm("ln1", st, TPB)
            w_loaded, tables_loaded = sem("p1_w_loaded"), sem("p1_tables_loaded")
            x_loaded = [sem("p1_x_loaded0"), sem("p1_x_loaded1")]
            n_stored = [sem("p1_n_stored0"), sem("p1_n_stored1")]
            nT_made, nT_ready, projected, v_projected, v_ready = [sem("p1_" + n) for n in (
                "nT_made", "nT_ready", "projected", "v_projected", "v_ready")]
            full_ready, part1_ready, rest_ready, part2_ready, parts_ready = [sem("p1_" + n) for n in (
                "full_ready", "part1_ready", "rest_ready", "part2_ready", "parts_ready")]
            parts_stored = [sem(f"p1_parts_stored{m}") for m in range(CH)]
            by_r_ready, by_r_stored = sem("p1_by_r_ready"), sem("p1_by_r_stored")
            pos_made, pos_ready, tab_made, tab_ready, tab_part1, tab_left, tab_part2, tab_split, far_bias = [
                sem("p1_" + n) for n in ("pos_made", "pos_ready", "tab_made", "tab_ready", "tab_part1",
                                         "tab_left", "tab_part2", "tab_split", "far_bias")]
            tab_stored = sem("p1_tab_stored")

            def store_stack(eng, stack_d, part_sb, m, cols, done, order):
                heads = H // CC
                for slot, part in enumerate(order):
                    eng.dma_start(stack_d[m * heads:(m + 1) * heads, slot, :, cols], part_sb[:, part, :]
                                  ).then_inc(done, 16)
            Q_ORDER, K_ORDER = (0, 1, 2, 0, 1, 0), (0, 0, 0, 1, 1, 2)

            with nc.Block() as block:
                @block.sync
                def _(sp):
                    for b in range(2):
                        sp.dma_start(x_in[:, b], a["x"][b].rearrange("(s p) c -> p s c", p=P)).then_inc(x_loaded[b], 16)

                    def body(b, u):
                        sp.wait_ge(ln["normed"], TPB * b + TPB)
                        sp.dma_start(normed_d[ds(b, 1)].rearrange("a p s c -> p (a s) c"), normed[:, u]
                                     ).then_inc(n_stored[u], 16)
                        if exists(b, 2):
                            sp.dma_start(x_in[:, u], a["x"][ds(b + 2, 1)].rearrange("a (s p) c -> p (a s) c", p=P)
                                         ).then_inc(x_loaded[u], 16)
                        for m in range(4):
                            sp.wait_ge(parts_ready, CH * b + m + 1)
                            store_stack(sp, (q_stack_d, qf_stack_d)[m // 2], parts[:, m], m % 2,
                                        ds(b * S, S), parts_stored[m], Q_ORDER)
                        for c in range(CC):
                            sp.wait_ge(by_r_ready, CC * (b + 1) + c + 1)
                            sp.dma_start(k_by_r_d[c * P:(c + 1) * P, :, :, ds(b, 1), :].rearrange("p t r b k -> p (t r) (b k)"),
                                         k_by_r[:, c].rearrange("p t r k -> p (t r) k")).then_inc(by_r_stored, 16)
                    each_batch(sp, body)
                    for u in range(2):
                        sp.wait_ge(n_stored[u], 16 * (B // 2 + 1))
                    for m in range(4):
                        sp.wait_ge(parts_stored[m], 16 * STACK * (B + 1))
                    sp.wait_ge(by_r_stored, 16 * CC * (B + 1))

                @block.gpsimd
                def _(pool):
                    pool.memset(ident[:], 0.0).then_inc(ident_zeroed, 1)
                    pool.wait_ge(ident_zeroed, 1)
                    pool.affine_select(out=ident[:], in_=ident[:], compare_op=ALU.not_equal, fill=1.0, base=0,
                                       pattern=[[-1, P]], channel_multiplier=1).then_inc(ident_ready, 1)
                    pool.sem_inc(by_r_stored, 16 * CC)
                    pool.sem_inc(by_r_ready, CC)
                    for w, n in ((wk, "wk"), (wq, "wq"), (wv, "wv")):
                        pool.dma_start(w[:], a[n].rearrange("(c p) n -> p c n", p=P)).then_inc(w_loaded, 16)
                    for w, n in ((bq, "bq_col"), (bk, "bk_col")):
                        pool.dma_start(w[:], a[n]).then_inc(w_loaded, 16)
                    for j in range(2):
                        pool.dma_start(bv_row[:, j, :], a["bv"].rearrange("(o n) -> o n", o=1).broadcast_to([P, C])
                                       ).then_inc(w_loaded, 16)
                    pool.dma_start(bk_row[:], a["bk"].rearrange("(o n) -> o n", o=1).broadcast_to([P, C])
                                   ).then_inc(tables_loaded, 16)
                    pool.dma_start(relT[:], a["relT"].rearrange("(c p) n -> p c n", p=P)).then_inc(tables_loaded, 16)
                    pool.dma_start(hot[:, 0], a["hot_c2p"]).then_inc(tables_loaded, 16)
                    pool.dma_start(hot[:, 1], a["hot_p2c"]).then_inc(tables_loaded, 16)
                    for m in range(2 * CC):
                        pool.wait_ge(tab_split, m + 1)
                        if m < CC:
                            store_stack(pool, c2p_stack_d, tab_parts[:, m], m, slice(0, DIST), tab_stored, K_ORDER)
                        else:
                            pool.dma_start(p2c_parts_d[(m - CC) * P:(m - CC + 1) * P], tab_parts[:, m]
                                           ).then_inc(tab_stored, 16)

                    def body(b, u):
                        for m in range(4, CH):
                            pool.wait_ge(parts_ready, CH * b + m + 1)
                            store_stack(pool, k_stack_d, parts[:, m], m % 2, ds(b * S, S), parts_stored[m], K_ORDER)
                    each_batch(pool, body)
                    for m in range(4, CH):
                        pool.wait_ge(parts_stored[m], 16 * STACK * B)
                    pool.wait_ge(tab_stored, 16 * CC * (1 + STACK))

                @block.tensor
                def _(pe):
                    pe.sem_inc(v_projected, 2)
                    pe.wait_ge(ident_ready, 1)
                    pe.wait_ge(w_loaded, 16 * 7)
                    pe.wait_ge(tables_loaded, 16 * 4)
                    for c in range(CC):
                        last = pe.matmul(bank[6][:, 0:C], relT[:, c, :], wk[:, c, :], start=c == 0, stop=c == CC - 1)
                    last.then_inc(pos_made, 1)
                    pe.wait_ge(pos_ready, 1)
                    for m in range(2 * CC):
                        c = m % CC
                        pe.matmul(bank[2 + m][:], pos_k[:, c * P:(c + 1) * P], hot[:, m // CC], start=True, stop=True
                                  ).then_inc(tab_made, 1)
                    pe.wait_ge(tab_ready, 2 * CC)

                    def body(b, u):
                        pe.wait_ge(ln["normed"], TPB * b + TPB)
                        pe.wait_ge(nT_ready, CC * (b + 1))
                        for c in range(CC):
                            for s in range(TPB):
                                last = pe.transpose(bank[c][:, s * P:(s + 1) * P], normed[:, u, s, c * P:(c + 1) * P],
                                                    ident[:])
                            last.then_inc(nT_made, 1)
                        pe.wait_ge(nT_ready, CC * (b + 2))
                        for m in range(4):
                            w = (wq, wk)[m // 2]
                            pe.wait_ge(full_ready, CH * b + m + 3)
                            for c in range(CC):
                                last = pe.matmul(bank[2 + m][:], w[:, c, (m % 2) * P:(m % 2 + 1) * P], nT[:, c, :],
                                                 start=c == 0, stop=c == CC - 1)
                            last.then_inc(projected, 1)
                        for j in range(2):
                            pe.wait_ge(v_ready, 2 * b + j + 1)
                            for s in (2 * j, 2 * j + 1):
                                for c in range(CC):
                                    last = pe.matmul(bank[6 + j][:, (s % 2) * C:(s % 2 + 1) * C],
                                                     nT[:, c, s * P:(s + 1) * P], wv[:, c, :],
                                                     start=c == 0, stop=c == CC - 1)
                            last.then_inc(v_projected, 1)
                    each_batch(pe, body)

                @block.scalar
                def _(act):
                    act.sem_inc(nT_ready, CC)
                    act.sem_inc(full_ready, CH)
                    for m in range(4):
                        act.sem_inc(parts_stored[m], 16 * STACK)
                    for m in range(2 * CC):
                        act.wait_ge(tab_made, m + 1)
                        act.copy(tab[:, m, :], bank[2 + m][:]).then_inc(tab_ready, 1)
                    ln_std(act, ln, 0)
                    act.wait_ge(far_bias, 1)

                    def body(b, u):
                        if exists(b, 1):
                            ln_std(act, ln, b + 1)
                        for c in range(CC):
                            act.wait_ge(nT_made, CC * b + c + 1)
                            if c == 0:
                                act.wait_ge(v_projected, 2 * b + 2)
                            act.copy(nT[:, c, :], bank[c][:]).then_inc(nT_ready, 1)
                        for m in range(CH):
                            kind, c = m // 2, m % 2
                            source = bank[(2, 2, 4)[kind] + c]
                            act.wait_ge(projected, 4 * b + (0, 0, 2)[kind] + c + 1)
                            act.wait_ge(rest_ready, CH * b + m + 1)
                            if kind == 1:
                                act.activation(full[:, m, 0:S // 2], source[:, 0:S // 2], ACT.Identity,
                                               bias=bq_far[:, c, 0:1])
                                act.activation(full[:, m, S // 2:S], source[:, S // 2:S], ACT.Identity,
                                               bias=bq_far[:, c, 1:2]).then_inc(full_ready, 1)
                            else:
                                act.activation(full[:, m, :], source[:], ACT.Identity,
                                               bias=(bq if kind == 0 else bk)[:, c:c + 1]).then_inc(full_ready, 1)
                            act.wait_ge(full_ready, CH * (b + 1) + m + 1)
                            if kind < 2:
                                act.wait_ge(parts_stored[m], 16 * STACK * (b + 1))
                            elif not isinstance(b, int) or b > 0:
                                act.wait_ge(parts_stored[m], 16 * STACK * b)
                            if kind == 2:
                                act.wait_ge(by_r_ready, CC * b + c + 1)
                            act.copy(parts[:, m, 0, :], full[:, m, :]).then_inc(part1_ready, 1)
                    batches(act, body)

                @block.vector
                def _(dve):
                    dve.sem_inc(v_ready, 2)
                    dve.sem_inc(rest_ready, CH)
                    for u in range(2):
                        dve.sem_inc(n_stored[u], 16)
                    dve.wait_ge(tables_loaded, 16 * 4)
                    dve.wait_ge(pos_made, 1)
                    dve.tensor_tensor(pos_k[:], bank[6][:, 0:C], bk_row[:], ALU.add).then_inc(pos_ready, 1)

                    def norm(b, u, half):
                        dve.wait_ge(x_loaded[u], 16 * half + 16)
                        ln_moments(dve, ln, b, lambda s: x_in[:, u, s, :], 1e-5)
                        dve.wait_ge(n_stored[u], 16 * half + 16)
                        ln_normalize(dve, ln, b, lambda s: x_in[:, u, s, :], lambda s: normed[:, u, s, :])

                    dve.wait_ge(tab_ready, 2 * CC)
                    for c in range(CC):
                        for side, x in ((0, 0), (1, DIST - 2)):
                            last = dve.tensor_tensor(bq_far[:, c, side:side + 1], bq[:, c:c + 1],
                                                     tab[:, CC + c, x:x + 1], ALU.add)
                    last.then_inc(far_bias, 1)
                    norm(0, 0, 0)
                    for m in range(2 * CC):
                        dve.tensor_copy(tab_parts[:, m, 0, :], tab[:, m, :]).then_inc(tab_part1, 1)
                        dve.wait_ge(tab_part1, m + 1)
                        dve.tensor_tensor(tab_rest[:, m, :], tab[:, m, :], tab_parts[:, m, 0, :], ALU.subtract
                                          ).then_inc(tab_left, 1)
                        dve.wait_ge(tab_left, m + 1)
                        dve.tensor_copy(tab_parts[:, m, 1, :], tab_rest[:, m, :]).then_inc(tab_part2, 1)
                        dve.wait_ge(tab_part2, m + 1)
                        dve.tensor_tensor(tab_parts[:, m, 2, :], tab_rest[:, m, :], tab_parts[:, m, 1, :],
                                          ALU.subtract).then_inc(tab_split, 1)

                    def body(b, u, half):
                        if exists(b, 1):
                            dve.wait_ge(nT_made, CC * b + 1)
                            norm(b + 1, 1 - u, half + u)
                        for m in range(CH):
                            dve.wait_ge(part1_ready, CH * b + m + 1)
                            dve.tensor_tensor(rest[:, m, :], full[:, m, :], parts[:, m, 0, :], ALU.subtract
                                              ).then_inc(rest_ready, 1)
                            dve.wait_ge(rest_ready, CH * (b + 1) + m + 1)
                            dve.tensor_copy(parts[:, m, 1, :], rest[:, m, :]).then_inc(part2_ready, 1)
                            dve.wait_ge(part2_ready, CH * b + m + 1)
                            dve.tensor_tensor(parts[:, m, 2, :], rest[:, m, :], parts[:, m, 1, :], ALU.subtract
                                              ).then_inc(parts_ready, 1)
                            if m >= 4:
                                c = m - 4
                                dve.wait_ge(by_r_stored, 16 * CC * (b + 1))
                                dve.wait_ge(parts_ready, CH * b + m + 1)
                                dve.tensor_copy(k_by_r[:, c].rearrange("p t r k -> p t k r"),
                                                parts[:, m].rearrange("p t (k r) -> p t k r", r=R)
                                                ).then_inc(by_r_ready, 1)
                        for j in range(2):
                            dve.wait_ge(v_projected, 2 * (b + 1) + j + 1)
                            dve.tensor_tensor(v_all[:, ds(b * TPB + 2 * j, 2), :],
                                              bank[6 + j][:].rearrange("p (s c) -> p s c", s=2), bv_row[:], ALU.add
                                              ).then_inc(v_ready, 1)
                    with dve.Fori(0, B // 2 - 1) as i:
                        for u in range(2):
                            body(2 * i + u, u, i)
                    for u in range(2):
                        body(B - 2 + u, u, B // 2 - 1)

        UNITS = H * TPB
        SCALE = float(1.0 / np.sqrt(np.float32(D * 3)))
        WINDOW = DIST - R
        ZERO_X = DIST // 2 - R

        def is_far(t, j):
            return abs(j // 2 - t) > 1

        LEAD = 2
        with ExitStack() as st:
            q6 = sb(st, "q6", [STACK * D, TPB, 2, B, P], BF16)
            k6 = sb(st, "k6", [STACK * D, 2, B * S], BF16)
            tab6 = sb(st, "tab6", [STACK * D, 2, DIST], BF16)
            p2c8 = sb(st, "p2c8", [P, 2, 3, WINDOW], BF16)
            kbd = sb(st, "kbd", [P, 2, 3, R, B, S // R], BF16)
            v_h = sb(st, "v_h", [P, 2, TILES, D])
            c2p_out = sb(st, "c2p_out", [P, 2, 2, DIST])
            c2p = sb(st, "c2p", [P, 2, B, NEAR])
            c2p_far = sb(st, "c2p_far", [P, 2, 2, B])
            probs = sb(st, "probs", [P, 2, B, S])
            probsT = sb(st, "probsT", [P, 2, TPB, P])
            ctxT = sb(st, "ctxT", [D, B, P])
            sums, inv_sums = sb(st, "sums", [P, 2, B]), sb(st, "inv_sums", [P, 2, B])
            row_max, neg_max = sb(st, "row_max", [P, 2, B]), sb(st, "neg_max", [P, 2, B])
            q_loaded = [sem(f"q_loaded{t}") for t in range(TPB)]
            head_loaded = [sem("head_loaded0"), sem("head_loaded1")]
            kbd_loaded = [sem("kbd_loaded0"), sem("kbd_loaded1")]
            HEAD_DMAS, KBD_DMAS = 2, 2 * R
            kbd_zeroed = sem("kbd_zeroed")
            v_copied, far_copied = sem("v_copied"), sem("far_copied")
            c2p_made, c2p_copied = sem("c2p_made"), sem("c2p_copied")
            c2p_written = [sem("c2p_written0"), sem("c2p_written1")]
            c2p_loaded = [sem("c2p_loaded0"), sem("c2p_loaded1")]
            scores_made, scores_added = sem("scores_made"), sem("scores_added")
            max_done, neg_max_done, exp_done = sem("max_done"), sem("neg_max_done"), sem("exp_done")
            inv_done, probs_ready, probs_transposed = sem("inv_done"), sem("probs_ready"), sem("probs_transposed")
            late_probs_ready = sem("late_probs_ready")
            EARLY = 5
            probsT_copied = [sem("probsT_even_copied"), sem("probsT_odd_copied")]
            pv_made, ctx_copied = sem("pv_made"), sem("ctx_copied")
            ctx_written = sem("ctx_written")
            SC, A_BANKS, T_BANKS, CTX_BANKS = 3, (3, 2), (4, 5), (6, 7)

            def each_step(eng, step):
                for w in range(8 - LEAD, 8):
                    step(-1, w)
                for w in range(8):
                    step(0, w)
                with eng.Fori(1, H // 2 - 1) as i:
                    for w in range(8):
                        step(i, w)
                for w in range(8):
                    step(H // 2 - 1, w)
                step(H // 2, 0)

            def is_unit(n):
                return not isinstance(n, int) or 0 <= n < UNITS

            def wait_count(eng, semaphore, count):
                if not isinstance(count, int) or count > 0:
                    eng.wait_ge(semaphore, count)

            with nc.Block() as block:
                @block.sync
                def _(sp):
                    def load_head(h, par):
                        rows = ds(h * D, D)
                        sp.dma_start(k6[:, par, :], k_stack_d[ds(h, 1)].rearrange("h k d n -> (h k d) n")
                                     ).then_inc(head_loaded[par], 16)
                        sp.dma_start(tab6[:, par, :], c2p_stack_d[ds(h, 1)].rearrange("h k d n -> (h k d) n")
                                     ).then_inc(head_loaded[par], 16)

                    def load_kbd(h, par, part):
                        rows = ds(h * D, D)
                        for g in range(part * R // 4, (part + 1) * R // 4):
                            sp.dma_start(kbd[g * D:(g + 1) * D, par, :, R - 1 - g, :, :].rearrange("p t b k -> p t (b k)"),
                                         k_by_r_d[rows, :, R - 1 - g, :, :].rearrange("p t b k -> p t (b k)")
                                         ).then_inc(kbd_loaded[par], 16)
                            sp.dma_start(p2c8[g * D:(g + 1) * D, par, :, :], p2c_parts_d[rows, :, g:g + WINDOW]
                                         ).then_inc(kbd_loaded[par], 16)

                    def load_q(h, t):
                        for far, stack_d in enumerate((q_stack_d, qf_stack_d)):
                            sp.dma_start(q6[:, t, far],
                                         stack_d[ds(h, 1)].rearrange("h k d (b t q) -> (h k d) t b q", t=TPB, q=P)[:, t]
                                         ).then_inc(q_loaded[t], 16)

                    def step(i, w):
                        n = 8 * i + w
                        if is_unit(n + 3) and is_unit(n):
                            wait_count(sp, scores_made, 8 * n)
                            load_q(2 * i + (w + 3) // 4, (w + 3) % 4)
                        if w in (0, 4) and is_unit(n) and is_unit(n + 4):
                            load_head(2 * i + 1 + w // 4, 1 - w // 4)
                        if is_unit(n) and is_unit(n + 4 - w % 4):
                            load_kbd(2 * i + 1 + w // 4, 1 - w // 4, w % 4)
                        if is_unit(n + LEAD):
                            par = w % 2
                            for q in range(4):
                                sp.wait_ge(c2p_copied, 8 * (n + LEAD) + 2 * q + 2)
                                sp.dma_start(c2p_d[par, 2 * q:2 * q + 2].rearrange("b p n -> p b n"),
                                             c2p_out[:, q % 2]).then_inc(c2p_written[q % 2], 16)
                            for q in range(2):
                                sp.wait_ge(c2p_written[q], 16 * 2 * (n + LEAD + 1))
                            wait_count(sp, scores_added, 8 * (n + 1))
                            skew = bass.AP(c2p_d.tensor, par * B * P * DIST + P - 1,
                                           [[DIST - 1, P], [P * DIST, B], [1, NEAR]])
                            sp.dma_start(c2p[:, par], skew).then_inc(c2p_loaded[par], 16)
                        if is_unit(n - 1):
                            t, h = (w - 1) % 4, 2 * i + w // 4 - (w % 4 == 0)
                            sp.wait_ge(ctx_copied, 2 * n)
                            sp.dma_start(ctxT_d[ds(h * D, D), :, t * P:(t + 1) * P], ctxT[:]
                                         ).then_inc(ctx_written, 16)
                    load_head(0, 0)
                    load_q(0, 0)
                    load_q(0, 1)
                    load_q(0, 2)
                    sp.wait_ge(kbd_zeroed, 2)
                    for part in range(4):
                        load_kbd(0, 0, part)
                    each_step(sp, step)
                    sp.wait_ge(ctx_written, 16 * UNITS)

                @block.gpsimd
                def _(pool):
                    pool.memset(kbd[:, 1], 0.0).then_inc(kbd_zeroed, 1)

                    def copy_v(h, par):
                        pool.tensor_copy(v_h[:, par], v_all[:, :, ds(h * D, D)]).then_inc(v_copied, 1)

                    def step(i, w):
                        n = 8 * i + w
                        if w in (1, 5) and is_unit(n) and is_unit(n + 3):
                            wait_count(pool, pv_made, 8 * (n - 1))
                            apart(pool)
                            copy_v(2 * i + 1 + w // 4, 1 - w // 4)
                        if is_unit(n + LEAD):
                            wait_count(pool, scores_added, 8 * (n + 1))
                            for q in range(4):
                                pool.wait_ge(c2p_copied, 8 * (n + LEAD) + 2 * q + 2)
                                apart(pool)
                                pool.tensor_copy(c2p_far[:, w % 2, :, 2 * q:2 * q + 2],
                                                 c2p_out[:, q % 2, :, 0:DIST - 1:DIST - 2].rearrange("p b s -> p s b")
                                                 ).then_inc(far_copied, 1)
                    copy_v(0, 0)
                    each_step(pool, step)

                @block.tensor
                def _(pe):
                    def step(i, w):
                        n = 8 * i + w
                        t, par = w % 4, w // 4
                        cur, nxt, prev = is_unit(n), is_unit(n + LEAD), is_unit(n - 1)
                        tn = (w + LEAD) % 4
                        i_n, par_n = (i + 1, 0) if w + LEAD > 7 else (i, (w + LEAD) // 4)
                        par_p = ((w - 1) % 8) // 4
                        if cur:
                            if t == 0:
                                pe.wait_ge(kbd_loaded[par], 16 * KBD_DMAS * (i + 1))
                            for j in range(8):
                                if j == A_BANKS[1]:
                                    wait_count(pe, c2p_copied, 8 * (n + min(LEAD, UNITS - n) if isinstance(n, int)
                                                                    else n + LEAD))
                                wait_count(pe, scores_added, 8 * n + j - 2 if j >= SC else 8 * (n - 1) + (7, 8, 6)[j])
                                sc, far = bank[j % SC], is_far(t, j)
                                for b in range(B):
                                    last = pe.matmul(sc[:, b * KCHUNK:(b + 1) * KCHUNK], q6[:, t, int(far), b, :],
                                                     k6[:, par, b * S + j * KCHUNK:b * S + (j + 1) * KCHUNK],
                                                     start=b == 0, stop=far and b == B - 1, skip_group_check=True)
                                cols = sc[:].rearrange("p (b k r) -> p b k r", b=B, r=R)
                                for k in range(0 if far else KCHUNK // R):
                                    x0 = t * P - (j * KCHUNK + k * R) + ZERO_X
                                    for tp, kp in ((0, 0), (0, 1), (0, 2), (1, 0), (1, 1), (2, 0)):
                                        last = pe.matmul(
                                            cols[:, :, k, :], p2c8[:, par, tp, x0:x0 + P],
                                            kbd[:, par, kp, :, :, j * (KCHUNK // R) + k].rearrange("p r b -> p b r"),
                                            start=False, stop=k == KCHUNK // R - 1 and tp == 2, skip_group_check=True)
                                last.then_inc(scores_made, 1)
                        if nxt:
                            pe.wait_ge(q_loaded[tn], 32 * (2 * i_n + par_n + 1))
                            if tn == 0:
                                pe.wait_ge(head_loaded[par_n], 16 * HEAD_DMAS * (i_n + 1))

                        def pv(j, k):
                            if k == 0:
                                pe.wait_ge(probsT_copied[j % 2], 4 * (n - 1) + j // 2 + 1)
                                if j % 4 == 0:
                                    wait_count(pe, ctx_copied, 2 * (n - 1) + j // 4 - 1)
                                if j == 0:
                                    pe.wait_ge(v_copied, 2 * i + w // 4 + (w % 4 > 0))
                            last = pe.matmul(bank[CTX_BANKS[j // 4]][0:D, (j % 4) * P:(j % 4 + 1) * P],
                                             v_h[:, par_p, j * TPB + k, :], probsT[:, j % 2, k, :],
                                             start=k == 0, stop=k == TPB - 1)
                            if k == TPB - 1:
                                last.then_inc(pv_made, 1)

                        for j in range(8 + 2):
                            if prev and j < 8:
                                if j < EARLY:
                                    pe.wait_ge(probs_ready, EARLY * (n - 1) + j + 1)
                                else:
                                    pe.wait_ge(late_probs_ready, (B - EARLY) * (n - 1) + j - EARLY + 1)
                                wait_count(pe, probsT_copied[j % 2], 4 * (n - 1) + j // 2)
                            for k in range(TPB if prev else 0):
                                if j < 8:
                                    last = pe.transpose(bank[T_BANKS[j % 2]][:, k * P:(k + 1) * P],
                                                        probs[:, (w - 1) % 2, j, k * P:(k + 1) * P], ident[:])
                                    if k == TPB - 1:
                                        last.then_inc(probs_transposed, 1)
                                if j >= 2:
                                    pv(j - 2, k)
                            if nxt and j < 8:
                                if j == 1 and cur:
                                    pe.wait_ge(scores_added, 8 * n + 6)
                                wait_count(pe, c2p_copied, 8 * (n + LEAD) + j - 1)
                                pe.matmul(bank[A_BANKS[j % 2]][:], q6[:, tn, 0, j, :], tab6[:, par_n, :], start=True, stop=True
                                          ).then_inc(c2p_made, 1)
                    each_step(pe, step)

                def copy_probsT(eng, copy, n, j):
                    eng.wait_ge(probs_transposed, 8 * n + j + 1)
                    wait_count(eng, pv_made, 8 * n + j - 1)
                    copy(probsT[:, j % 2], bank[T_BANKS[j % 2]][:].rearrange("p (k q) -> p k q", k=TPB)
                         ).then_inc(probsT_copied[j % 2], 1)

                @block.scalar
                def _(act):
                    def step(i, w):
                        n = 8 * i + w
                        nxt, prev = is_unit(n + LEAD), is_unit(n - 1)
                        pp = (w - 1) % 2
                        if prev:
                            act.wait_ge(neg_max_done, n)
                            wait_count(act, inv_done, 2 * (n - 2))
                            for j in range(B):
                                act.activation(probs[:, pp, j, :], probs[:, pp, j, :], ACT.Exp,
                                               bias=neg_max[:, pp, j:j + 1], scale=SCALE,
                                               accum_out=sums[:, pp, j:j + 1]).then_inc(exp_done, 1)
                            for j in range(EARLY, B):
                                act.wait_ge(inv_done, 2 * (n - 1) + 2)
                                act.activation(probs[:, pp, j, :], probs[:, pp, j, :], ACT.Copy,
                                               scale=inv_sums[:, pp, j:j + 1]).then_inc(late_probs_ready, 1)
                        for j in range(8):
                            if prev and j % 2 == 0:
                                copy_probsT(act, act.copy, n - 1, j)
                            if nxt:
                                act.wait_ge(c2p_made, 8 * (n + LEAD) + j + 1)
                                if j % 2 == 0:
                                    q = j // 2
                                    wait_count(act, c2p_written[q % 2], 16 * (2 * (n + LEAD) + q // 2))
                                    wait_count(act, far_copied, 4 * (n + LEAD) + q - 1)
                                act.copy(c2p_out[:, (j // 2) % 2, j % 2, :], bank[A_BANKS[j % 2]][:]).then_inc(c2p_copied, 1)
                    each_step(act, step)

                @block.vector
                def _(dve):
                    def step(i, w):
                        n = 8 * i + w
                        t, cp, pp = w % 4, w % 2, (w - 1) % 2
                        cur, prev = is_unit(n), is_unit(n - 1)
                        if cur:
                            dve.wait_ge(c2p_loaded[cp], 16 * (4 * i + w // 2 + 1))
                            dve.wait_ge(far_copied, 4 * (n + 1))
                            wait_count(dve, probs_transposed, 8 * (n - 1))
                        for j in range(8):
                            if cur:
                                if is_far(t, j):
                                    side = 0 if j // 2 < t else 1
                                    bias = c2p_far[:, cp, side, :].unsqueeze(2).broadcast_to([P, B, KCHUNK])
                                else:
                                    first = j * KCHUNK - (t - 1) * P
                                    bias = c2p[:, cp, :, first:first + KCHUNK]
                                dve.wait_ge(scores_made, 8 * n + j + 1)
                                dve.tensor_tensor(probs[:, cp, :, j * KCHUNK:(j + 1) * KCHUNK],
                                                  bank[j % SC][:].rearrange("p (b k) -> p b k", b=B), bias, ALU.add
                                                  ).then_inc(scores_added, 1)
                            if j == 1 and is_unit(n - 2):
                                copy_ctx(n - 2, 1)
                            if prev and j in (1, 3):
                                lo, hi = ((0, 2), (2, B))[j // 2]
                                dve.wait_ge(exp_done, 8 * (n - 1) + hi)
                                dve.reciprocal(inv_sums[:, pp, lo:hi], sums[:, pp, lo:hi]).then_inc(inv_done, 1)
                                dve.wait_ge(inv_done, 2 * (n - 1) + j // 2 + 1)
                            if prev and j % 2:
                                for b in range(j - 1, min(j + 1, EARLY)):
                                    dve.tensor_scalar(probs[:, pp, b, :], probs[:, pp, b, :], inv_sums[:, pp, b:b + 1],
                                                      None, ALU.mult).then_inc(probs_ready, 1)
                        if cur:
                            dve.wait_ge(scores_added, 8 * n + 8)
                        for j in range(B):
                            if cur:
                                dve.reduce_max(row_max[:, cp, j:j + 1], probs[:, cp, j, :], axis=AX.X).then_inc(max_done, 1)
                            if prev and j % 2:
                                copy_probsT(dve, dve.tensor_copy, n - 1, j)
                            if prev and j == 6:
                                copy_ctx(n - 1, 0)
                        if cur:
                            dve.wait_ge(max_done, 8 * n + 8)
                            dve.tensor_scalar(neg_max[:, cp, :], row_max[:, cp, :], -SCALE, None, ALU.mult
                                              ).then_inc(neg_max_done, 1)
                        if not cur and prev:
                            copy_ctx(n - 1, 1)

                    def copy_ctx(n, half):
                        dve.wait_ge(pv_made, 8 * n + 4 * half + 4)
                        if half == 0:
                            wait_count(dve, ctx_written, 16 * n)
                        dve.tensor_copy(ctxT[:, 4 * half:4 * half + 4, :],
                                        bank[CTX_BANKS[half]][0:D, :].rearrange("p (b q) -> p b q", b=4)
                                        ).then_inc(ctx_copied, 1)
                    dve.memset(kbd[:, 0], 0.0).then_inc(kbd_zeroed, 1)
                    each_step(dve, step)
        attn.close()

        residual = sb(whole, "residual", [P, TILES, C])

        def row(name):
            return a[name].rearrange("(o n) -> o n", o=1).broadcast_to([P, a[name].shape[0]])

        HID = FFN // P
        LOW = 4
        with ExitStack() as st:
            ctx_in = sb(st, "p3_ctx", [P, 2, CC, S])
            n_in = sb(st, "p3_n", [P, 2, TPB, C])
            x_in = sb(st, "p3_x", [P, 2, TPB, C])
            n_bo, x_lb = sb(st, "p3_n_bo", [P, TPB, C]), sb(st, "p3_x_lb", [P, TPB, C])
            o = sb(st, "p3_o", [P, TPB, C])
            o_norm = sb(st, "p3_o_norm", [P, TPB, C])
            x1 = sb(st, "p3_x1", [P, TPB, C])
            x1_b2 = sb(st, "p3_x1_b2", [P, 2, TPB, C])
            y = sb(st, "p3_y", [P, TPB, C])
            yT = sb(st, "p3_yT", [P, 2, CC, S])
            hT = sb(st, "p3_hT", [P, HID, S])
            wo = sb(st, "p3_wo", [P, CC, C])
            w1, w2 = sb(st, "p3_w1", [P, CC, FFN]), sb(st, "p3_w2", [P, HID, C])
            w1_b, w2_b = sb(st, "p3_w1_b", [P, 2, CC, FFN]), sb(st, "p3_w2_b", [P, 2, HID, C])
            rows3 = sb(st, "p3_rows", [P, 4, C])
            b1 = sb(st, "p3_b1", [P, HID])
            scale = sb(st, "p3_scale", [P, 1])
            pick = sb(st, "p3_pick", [P, 2 * LOW, P])
            odd = sb(st, "p3_odd", [P, CC, 2 * LOW])
            lnA, lnB = layer_norm("ln2", st, TPB), layer_norm("ln3", st, TPB)
            w_loaded, pick_zeroed, pick_ready = sem("p3_w_loaded"), sem("p3_pick_zeroed"), sem("p3_pick_ready")
            in_loaded = [sem("p3_in_loaded0"), sem("p3_in_loaded1")]
            wo_made, n_bo_ready, x_lb_ready, o_ready, scaled, x1_ready, x1_b2_ready = [sem("p3_" + k) for k in (
                "wo_made", "n_bo_ready", "x_lb_ready", "o_ready", "scaled", "x1_ready", "x1_b2_ready")]
            yT_made, yT_ready, even_made, odd_ready, w1_ready, w_ready = [sem("p3_" + k) for k in (
                "yT_made", "yT_ready", "even_made", "odd_ready", "w1_ready", "w_ready")]
            ffn1_made, gelu_done, ffn2_made, x2_ready = [sem("p3_" + k) for k in (
                "ffn1_made", "gelu_done", "ffn2_made", "x2_ready")]
            O_BANKS, Y_BANKS, F_BANKS, G_BANKS = (0, 1), (2, 3), (4, 5), (6, 7)
            EVEN_BANKS = O_BANKS + Y_BANKS
            W_OPS = CC * LOW + HID * LOW

            def wait_count(eng, semaphore, count):
                if not isinstance(count, int) or count > 0:
                    eng.wait_ge(semaphore, count)

            with nc.Block() as block:
                @block.sync
                def _(sp):
                    def load(b, u):
                        wait_count(sp, wo_made, 2 * (b - 1))
                        wait_count(sp, n_bo_ready, b - 1)
                        wait_count(sp, x_lb_ready, b - 1)
                        sp.dma_start(ctx_in[:, u], ctxT_d[:, ds(b, 1), :].rearrange("(c p) b s -> p c (b s)", p=P)
                                     ).then_inc(in_loaded[u], 16)
                        sp.dma_start(n_in[:, u], normed_d[ds(b, 1)].rearrange("b p s c -> p (b s) c")
                                     ).then_inc(in_loaded[u], 16)
                        sp.dma_start(x_in[:, u], a["x"][ds(b, 1)].rearrange("b (s p) c -> p (b s) c", p=P)
                                     ).then_inc(in_loaded[u], 16)
                    batches(sp, load)

                @block.gpsimd
                def _(pool):
                    for k, n in enumerate(("bo", "ln_scale", "ln_bias", "b2")):
                        pool.dma_start(rows3[:, k, :], row(n)).then_inc(w_loaded, 16)
                    pool.dma_start(wo[:], a["wo"].rearrange("(c p) n -> p c n", p=P)).then_inc(w_loaded, 16)
                    pool.dma_start(w1[:], a["w1T"].rearrange("(c p) n -> p c n", p=P)).then_inc(w_loaded, 16)
                    pool.dma_start(w2[:], a["w2T"].rearrange("(c p) n -> p c n", p=P)).then_inc(w_loaded, 16)
                    pool.dma_start(b1[:], a["b1_col"]).then_inc(w_loaded, 16)
                    pool.dma_start(scale[:], row("scale")).then_inc(w_loaded, 16)
                    pool.memset(pick[:], 0.0).then_inc(pick_zeroed, 1)
                    pool.wait_ge(pick_zeroed, 1)
                    pool.affine_select(out=pick[:], in_=pick[:], compare_op=ALU.not_equal, fill=1.0, base=-1,
                                       pattern=[[-2, 2 * LOW], [0, P]], channel_multiplier=1).then_inc(pick_ready, 1)
                    pool.wait_ge(w_loaded, 16 * 9)

                    def across(k):
                        return rows3[:, k, :].unsqueeze(1).broadcast_to([P, TPB, C])

                    def body(b, u):
                        if isinstance(b, int):
                            pool.wait_ge(in_loaded[u], 48 * (b // 2 + 1))
                        else:
                            pool.wait_ge(in_loaded[u], 24 * (b - u) + 48)
                        wait_count(pool, o_ready, 2 * b)
                        apart(pool)
                        pool.tensor_tensor(n_bo[:], n_in[:, u], across(0), ALU.add).then_inc(n_bo_ready, 1)
                        wait_count(pool, x1_ready, b)
                        apart(pool)
                        pool.tensor_tensor(x_lb[:], x_in[:, u], across(2), ALU.add).then_inc(x_lb_ready, 1)
                        wait_count(pool, x2_ready, 2 * (b - 1))
                        pool.wait_ge(x1_ready, b + 1)
                        apart(pool)
                        pool.tensor_tensor(x1_b2[:, u], x1[:], across(3), ALU.add).then_inc(x1_b2_ready, 1)
                    batches(pool, body)

                @block.tensor
                def _(pe):
                    def project(b, u):
                        if isinstance(b, int):
                            pe.wait_ge(in_loaded[u], 48 * (b // 2 + 1))
                        else:
                            pe.wait_ge(in_loaded[u], 24 * (b - u) + 48)
                        wait_count(pe, w_ready, W_OPS * b)
                        for j in range(2):
                            for s in (2 * j, 2 * j + 1):
                                for c in range(CC):
                                    last = pe.matmul(bank[O_BANKS[j]][:, (s % 2) * C:(s % 2 + 1) * C],
                                                     ctx_in[:, u, c, s * P:(s + 1) * P], wo[:, c, :],
                                                     start=c == 0, stop=c == CC - 1)
                            last.then_inc(wo_made, 1)

                    def transpose(b, u):
                        pe.wait_ge(lnB["normed"], TPB * b + TPB)
                        for c in range(CC):
                            for s in range(TPB):
                                last = pe.transpose(bank[Y_BANKS[c]][:, s * P:(s + 1) * P], y[:, s, c * P:(c + 1) * P],
                                                    ident[:])
                            last.then_inc(yT_made, 1)
                        pe.wait_ge(yT_ready, CC * b + CC)
                        pe.wait_ge(o_ready, 2 * b + 2)
                        for i in range(2 * LOW):
                            last = pe.matmul(bank[EVEN_BANKS[i // 2]][:, (i % 2) * C:(i % 2 + 1) * C], pick[:, i, :],
                                             y[:, 0, :], start=True, stop=True)
                        last.then_inc(even_made, 1)

                    pe.wait_ge(w_loaded, 16 * 9)
                    pe.wait_ge(pick_ready, 1)
                    project(0, 0)
                    transpose(0, 0)
                    project(1, 1)

                    def body(b, u):
                        pe.wait_ge(w_ready, W_OPS * b + W_OPS)
                        for m in range(HID):
                            wait_count(pe, gelu_done, HID * b + m - 1)
                            for c in range(CC):
                                last = pe.matmul(bank[F_BANKS[m % 2]][:], w1_b[:, u, c, m * P:(m + 1) * P],
                                                 yT[:, u, c, :], start=c == 0, stop=c == CC - 1)
                            last.then_inc(ffn1_made, 1)
                        if exists(b, 1):
                            transpose(b + 1, 1 - u)
                        pe.wait_ge(gelu_done, HID * b + HID)
                        for j in range(2):
                            wait_count(pe, x2_ready, 2 * b + j - 1)
                            for s in (2 * j, 2 * j + 1):
                                for m in range(HID):
                                    last = pe.matmul(bank[G_BANKS[j]][:, (s % 2) * C:(s % 2 + 1) * C],
                                                     hT[:, m, s * P:(s + 1) * P], w2_b[:, u, m, :],
                                                     start=m == 0, stop=m == HID - 1)
                            last.then_inc(ffn2_made, 1)
                        if exists(b, 2):
                            project(b + 2, u)
                    batches(pe, body)

                @block.scalar
                def _(act):
                    def copy_yT(b, u):
                        wait_count(act, ffn1_made, HID * (b - 1))
                        for c in range(CC):
                            act.wait_ge(yT_made, CC * b + c + 1)
                            act.copy(yT[:, u, c, :], bank[Y_BANKS[c]][:]).then_inc(yT_ready, 1)

                    def gelu(b, m):
                        act.wait_ge(ffn1_made, HID * b + m + 1)
                        if m == 0:
                            wait_count(act, ffn2_made, 2 * b)
                        act.activation(hT[:, m, :], bank[F_BANKS[m % 2]][:], ACT.Gelu, bias=b1[:, m:m + 1]
                                       ).then_inc(gelu_done, 1)
                    ln_std(act, lnA, 0)
                    ln_std(act, lnB, 0)
                    copy_yT(0, 0)
                    act.wait_ge(w_loaded, 16 * 9)

                    def body(b, u):
                        if exists(b, 1):
                            ln_std(act, lnA, b + 1)
                        for m in range(HID // 2):
                            gelu(b, m)
                        if exists(b, 1):
                            ln_std(act, lnB, b + 1)
                        for m in range(HID // 2, HID):
                            gelu(b, m)
                        if exists(b, 1):
                            copy_yT(b + 1, 1 - u)
                    batches(act, body)

                @block.vector
                def _(dve):
                    def norms(b, u):
                        dve.wait_ge(n_bo_ready, b + 1)
                        for j in range(2):
                            dve.wait_ge(wo_made, 2 * b + j + 1)
                            dve.tensor_tensor(o[:, 2 * j:2 * j + 2, :],
                                              bank[O_BANKS[j]][:].rearrange("p (s c) -> p s c", s=2),
                                              n_bo[:, 2 * j:2 * j + 2, :], ALU.add).then_inc(o_ready, 1)
                        dve.wait_ge(o_ready, 2 * b + 2)
                        ln_moments(dve, lnA, b, lambda s: o[:, s, :], 1e-7)
                        ln_normalize(dve, lnA, b, lambda s: o[:, s, :], lambda s: o_norm[:, s, :])
                        dve.wait_ge(lnA["normed"], TPB * b + TPB)
                        dve.tensor_tensor(o_norm[:], o_norm[:], rows3[:, 1, :].unsqueeze(1).broadcast_to([P, TPB, C]),
                                          ALU.mult).then_inc(scaled, 1)
                        dve.wait_ge(scaled, b + 1)
                        dve.wait_ge(x_lb_ready, b + 1)
                        wait_count(dve, x1_b2_ready, b)
                        dve.tensor_tensor(x1[:], o_norm[:], x_lb[:], ALU.add).then_inc(x1_ready, 1)
                        dve.wait_ge(x1_ready, b + 1)
                        ln_moments(dve, lnB, b, lambda s: x1[:, s, :], 1e-5)
                        wait_count(dve, even_made, b)
                        ln_normalize(dve, lnB, b, lambda s: x1[:, s, :], lambda s: y[:, s, :])

                    def weights(b, u):
                        dve.wait_ge(yT_ready, CC * b + CC)
                        dve.tensor_scalar(odd[:], yT[:, u, :, 2:2 + 4 * LOW:2], scale[:], None, ALU.mult
                                          ).then_inc(odd_ready, 1)
                        dve.wait_ge(odd_ready, b + 1)
                        dve.wait_ge(even_made, b + 1)
                        wait_count(dve, ffn2_made, 2 * (b - 1))

                        def even(i):
                            return bank[EVEN_BANKS[i // 2]][:, (i % 2) * C:(i % 2 + 1) * C]
                        for c in range(CC):
                            for i in range(LOW):
                                dve.scalar_tensor_tensor(
                                    w1_b[:, u, c, i * C:(i + 1) * C], even(i), odd[:, c, i:i + 1],
                                    w1[:, c, i * C:(i + 1) * C], op0=ALU.mult, op1=ALU.add).then_inc(w_ready, 1)
                        for m in range(HID):
                            for i in range(LOW):
                                cols = slice(i * C // LOW, (i + 1) * C // LOW)
                                dve.scalar_tensor_tensor(
                                    w2_b[:, u, m, cols], even(LOW + i)[:, m // CC:C:LOW],
                                    odd[:, m % CC, LOW + i:LOW + i + 1], w2[:, m, cols],
                                    op0=ALU.mult, op1=ALU.add).then_inc(w_ready, 1)

                    dve.wait_ge(w_loaded, 16 * 9)
                    norms(0, 0)
                    weights(0, 0)

                    def body(b, u):
                        if exists(b, 1):
                            norms(b + 1, 1 - u)
                            weights(b + 1, 1 - u)
                        dve.wait_ge(x1_b2_ready, b + 1)
                        for j in range(2):
                            dve.wait_ge(ffn2_made, 2 * b + j + 1)
                            dve.tensor_tensor(residual[:, ds(b * TPB + 2 * j, 2), :],
                                              bank[G_BANKS[j]][:].rearrange("p (s c) -> p s c", s=2),
                                              x1_b2[:, u, 2 * j:2 * j + 2, :], ALU.add).then_inc(x2_ready, 1)
                    batches(dve, body)

        def tile_of(n, g):
            return n * TPB + g

        TASK = 4
        QKV = 3 * C
        with ExitStack() as st:
            y = sb(st, "p4_y", [P, B, C])
            yT = sb(st, "p4_yT", [P, CC, B, P])
            qkv = sb(st, "p4_qkv", [P, 2, B, QKV])
            prod = sb(st, "p4_prod", [P, 2, B, C])
            score = sb(st, "p4_score", [P, B, H, B])
            top = sb(st, "p4_top", [P, B, H])
            total = sb(st, "p4_total", [P, B, H])
            attn_out = sb(st, "p4_attn", [P, 2, B, C])
            attnT = sb(st, "p4_attnT", [P, CC, B, P])
            wqkv, wproj = sb(st, "p4_wqkv", [P, CC, QKV]), sb(st, "p4_wproj", [P, CC, C])
            bqkv, bproj = sb(st, "p4_bqkv", [1, QKV]), sb(st, "p4_bproj", [1, C])
            ones = sb(st, "p4_ones", [1, P])
            ln = layer_norm("ln4", st, B)
            w_loaded, ones_ready = sem("p4_w_loaded"), sem("p4_ones_ready")
            yT_made, yT_ready, qkv_made, qkv_ready = [sem("p4_" + k) for k in (
                "yT_made", "yT_ready", "qkv_made", "qkv_ready")]
            q_times_k, scores_ready, top_ready, shifted, exp_done, total_ready, inv_ready, p_ready = [
                sem("p4_" + k) for k in ("q_times_k", "scores_ready", "top_ready", "shifted", "exp_done",
                                         "total_ready", "inv_ready", "p_ready")]
            p_times_v, out_ready, aT_made, aT_ready, proj_made, x3_ready = [sem("p4_" + k) for k in (
                "p_times_v", "out_ready", "aT_made", "aT_ready", "proj_made", "x3_ready")]
            Y_BANKS, QKV_BANKS, PROJ_BANK = (0, 1), ((2, 3), (4, 5)), 6
            BLOCKS = ((slice(0, TASK), slice(0, TASK)), (slice(TASK, B), slice(0, B)))

            def seen(n):
                return TASK if n < TASK else B

            with nc.Block() as block:
                @block.sync
                def _(sp):
                    sp.dma_start(wqkv[:], a["wqkvT"].rearrange("(c p) n -> p c n", p=P)).then_inc(w_loaded, 16)
                    sp.dma_start(wproj[:], a["wprojT"].rearrange("(c p) n -> p c n", p=P)).then_inc(w_loaded, 16)
                    sp.dma_start(bqkv[:], a["bqkv"].rearrange("(o n) -> o n", o=1)).then_inc(w_loaded, 16)
                    sp.dma_start(bproj[:], a["bproj"].rearrange("(o n) -> o n", o=1)).then_inc(w_loaded, 16)
                    sp.wait_ge(w_loaded, 64)

                @block.gpsimd
                def _(pool):
                    pool.memset(ones[:], 1.0).then_inc(ones_ready, 1)

                @block.tensor
                def _(pe):
                    def transposes(source, g, made, ready):
                        for q in range(4):
                            if 4 * g + q >= 2:
                                pe.wait_ge(ready, 4 * g + q - 1)
                            for k in range(4):
                                n, c = 4 * (q % 2) + k, q // 2
                                last = pe.transpose(bank[Y_BANKS[q % 2]][:, k * P:(k + 1) * P],
                                                    source[:, n, c * P:(c + 1) * P], ident[:])
                            last.then_inc(made, 1)

                    def qkv_of(g):
                        pe.wait_ge(ln["normed"], B * g + B)
                        if g:
                            pe.wait_ge(aT_ready, 4 * g - 4)
                        transposes(y, g, yT_made, yT_ready)
                        pe.wait_ge(yT_ready, 4 * g + 4)
                        for n in range(B):
                            if B * g + n >= 2:
                                pe.wait_ge(qkv_ready, 2 * (B * g + n) - 2)
                            for h, (lo, hi) in enumerate(((0, 512), (512, QKV))):
                                dst = bank[QKV_BANKS[n % 2][h]][:, 0:hi - lo]
                                for c in range(CC):
                                    pe.matmul(dst, yT[:, c, n, :], wqkv[:, c, lo:hi], start=c == 0, stop=False)
                                pe.matmul(dst, ones[:], bqkv[:, lo:hi], start=False, stop=True).then_inc(qkv_made, 1)

                    def project(g):
                        pe.wait_ge(out_ready, B * g + B)
                        pe.wait_ge(yT_ready, 4 * min(g + 2, TPB))
                        transposes(attn_out[:, g % 2], g, aT_made, aT_ready)
                        pe.wait_ge(aT_ready, 4 * g + 4)
                        for n in range(B):
                            half = bank[PROJ_BANK + n % 2][:, 0:C]
                            if B * g + n >= 2:
                                pe.wait_ge(x3_ready, B * g + n - 1)
                            for c in range(CC):
                                pe.matmul(half, attnT[:, c, n, :], wproj[:, c, :], start=c == 0, stop=False)
                            pe.matmul(half, ones[:], bproj[:], start=False, stop=True).then_inc(proj_made, 1)

                    pe.wait_ge(w_loaded, 64)
                    pe.wait_ge(ones_ready, 1)
                    qkv_of(0)
                    for g in range(TPB):
                        if g + 1 < TPB:
                            qkv_of(g + 1)
                        project(g)

                @block.scalar
                def _(act):
                    def copy_T(dst, g, made, ready):
                        for q in range(4):
                            act.wait_ge(made, 4 * g + q + 1)
                            act.copy(dst[:, q // 2, 4 * (q % 2):4 * (q % 2) + 4, :],
                                     bank[Y_BANKS[q % 2]][:].rearrange("p (n s) -> p n s", n=4)).then_inc(ready, 1)

                    def qkv_of(g):
                        ln_std(act, ln, g)
                        if g:
                            act.wait_ge(qkv_made, 2 * B * g)
                        copy_T(yT, g, yT_made, yT_ready)
                        if g >= 2:
                            act.wait_ge(out_ready, B * (g - 1))
                        for n in range(B):
                            for h, (lo, hi) in enumerate(((0, 512), (512, QKV))):
                                act.wait_ge(qkv_made, 2 * (B * g + n) + h + 1)
                                act.copy(qkv[:, g % 2, n, lo:hi], bank[QKV_BANKS[n % 2][h]][:, 0:hi - lo]
                                         ).then_inc(qkv_ready, 1)

                    def exponentials(g):
                        for k, (ns, ms) in enumerate(BLOCKS):
                            act.wait_ge(shifted, 2 * g + k + 1)
                            act.activation(score[:, ns, :, ms], score[:, ns, :, ms], ACT.Exp, scale=float(D) ** -0.5
                                           ).then_inc(exp_done, 1)

                    qkv_of(0)
                    for g in range(TPB):
                        exponentials(g)
                        if g + 1 < TPB:
                            qkv_of(g + 1)
                        if g:
                            act.wait_ge(proj_made, B * g)
                        copy_T(attnT, g, aT_made, aT_ready)

                @block.vector
                def _(dve):
                    def norm(g):
                        def source(n):
                            return residual[:, tile_of(n, g), :]
                        ln_moments(dve, ln, g, source, 1e-5)
                        if g:
                            dve.wait_ge(yT_made, 4 * g)
                        ln_normalize(dve, ln, g, source, lambda n: y[:, n, :])

                    def heads(x, m):
                        return x.rearrange("p m (h d) -> p m h d", h=H)

                    def attention(g):
                        u = g % 2
                        dve.wait_ge(qkv_ready, 2 * B * (g + 1))
                        q, k, v = (qkv[:, u, :, i * C:(i + 1) * C] for i in range(3))
                        for n in range(B):
                            m = seen(n)
                            if B * g + n >= 2:
                                dve.wait_ge(scores_ready, B * g + n - 1)
                            dve.tensor_tensor(prod[:, n % 2, 0:m, :], k[:, 0:m, :],
                                              q[:, n, :].unsqueeze(1).broadcast_to([P, m, C]), ALU.mult
                                              ).then_inc(q_times_k, 1)
                            dve.wait_ge(q_times_k, B * g + n + 1)
                            dve.reduce_sum(score[:, n, :, 0:m].rearrange("p h m -> p m h"),
                                           heads(prod[:, n % 2, 0:m, :], m), axis=AX.X).then_inc(scores_ready, 1)
                        dve.wait_ge(scores_ready, B * g + B)
                        for j, (ns, ms) in enumerate(BLOCKS):
                            size = [P, TASK, H, ms.stop]
                            dve.reduce_max(top[:, ns, :], score[:, ns, :, ms], axis=AX.X).then_inc(top_ready, 1)
                            dve.wait_ge(top_ready, 2 * g + j + 1)
                            dve.tensor_tensor(score[:, ns, :, ms], score[:, ns, :, ms],
                                              top[:, ns, :].unsqueeze(3).broadcast_to(size), ALU.subtract
                                              ).then_inc(shifted, 1)
                        if g:
                            add(g - 1)
                        if g + 1 < TPB:
                            norm(g + 1)
                        for j, (ns, ms) in enumerate(BLOCKS):
                            size = [P, TASK, H, ms.stop]
                            dve.wait_ge(exp_done, 2 * g + j + 1)
                            dve.reduce_sum(total[:, ns, :], score[:, ns, :, ms], axis=AX.X).then_inc(total_ready, 1)
                            dve.wait_ge(total_ready, 2 * g + j + 1)
                            dve.reciprocal(total[:, ns, :], total[:, ns, :]).then_inc(inv_ready, 1)
                            dve.wait_ge(inv_ready, 2 * g + j + 1)
                            dve.tensor_tensor(score[:, ns, :, ms], score[:, ns, :, ms],
                                              total[:, ns, :].unsqueeze(3).broadcast_to(size), ALU.mult
                                              ).then_inc(p_ready, 1)
                        dve.wait_ge(p_ready, 2 * g + 2)
                        if g >= 2:
                            dve.wait_ge(aT_made, 4 * (g - 1))
                        for n in range(B):
                            m = seen(n)
                            dve.tensor_tensor(heads(prod[:, n % 2, 0:m, :], m), heads(v[:, 0:m, :], m),
                                              score[:, n, :, 0:m].rearrange("p h m -> p m h").unsqueeze(3)
                                              .broadcast_to([P, m, H, D]), ALU.mult).then_inc(p_times_v, 1)
                            dve.wait_ge(p_times_v, B * g + n + 1)
                            dve.reduce_sum(attn_out[:, u, n, :], prod[:, n % 2, 0:m, :].rearrange("p m c -> p c m"),
                                           axis=AX.X).then_inc(out_ready, 1)

                    def add(g):
                        for n in range(B):
                            t = tile_of(n, g)
                            dve.wait_ge(proj_made, B * g + n + 1)
                            dve.tensor_tensor(residual[:, t, :], bank[PROJ_BANK + n % 2][:, 0:C], residual[:, t, :],
                                              ALU.add).then_inc(x3_ready, 1)
                    norm(0)
                    for g in range(TPB):
                        attention(g)
                    add(TPB - 1)

        HALF = TILES // 2
        with ExitStack() as st:
            yT = sb(st, "p5_yT", [P, CC, B * S])
            cw = sb(st, "p5_cw", [P, TILES, ALL_EXPERTS])
            with ExitStack() as pre:
                y = sb(pre, "p5_y", [P, 2, TPB, C])
                router = sb(pre, "p5_router", [P, CC, EXPERTS])
                bias = sb(pre, "p5_bias", [P, EXPERTS])
                before = sb(pre, "p5_before", [P, GROUPS, GROUPS])
                index = sb(pre, "p5_index", [P, EXPERTS])
                score = sb(pre, "p5_score", [P, TILES, EXPERTS])
                sfc = sb(pre, "p5_sfc", [P, TILES, EXPERTS])
                best = sb(pre, "p5_best", [P, TILES, GROUPS, 8])
                pair = sb(pre, "p5_pair", [P, TILES, GROUPS])
                wins, ties = [sb(pre, n, [P, TILES, GROUPS, GROUPS]) for n in ("p5_wins", "p5_ties")]
                rank = sb(pre, "p5_rank", [P, TILES, GROUPS])
                top8 = sb(pre, "p5_top8", [P, TILES, 8])
                where = sb(pre, "p5_where", [P, TILES, 8], U32)
                where_f = sb(pre, "p5_where_f", [P, TILES, 8])
                hit = sb(pre, "p5_hit", [P, TOP_K, TILES, EXPERTS])
                norm_w = sb(pre, "p5_norm_w", [P, TILES])
                ln = layer_norm("ln5", pre, TPB)
                c_loaded, yT_made, yT_ready, logits_made, score_ready, step = [
                    sem("p5_" + k) for k in ("c_loaded", "yT_made", "yT_ready", "logits_made", "score_ready",
                                             "route_step")]
                cw_ready = sem("p5_cw_ready")
                Y_BANKS, L_BANKS = ((0, 1), (2, 3)), (4, 5)

                with nc.Block() as block:
                    @block.sync
                    def _(sp):
                        sp.dma_start(router[:], a["routerT"].rearrange("(c p) n -> p c n", p=P)).then_inc(c_loaded, 16)
                        sp.dma_start(bias[:], row("router_bias")).then_inc(c_loaded, 16)
                        sp.dma_start(before[:].rearrange("p g h -> p (g h)"), row("group_before")).then_inc(c_loaded, 16)
                        sp.dma_start(index[:], row("expert_index")).then_inc(c_loaded, 16)
                        sp.wait_ge(c_loaded, 64)

                    @block.tensor
                    def _(pe):
                        pe.wait_ge(c_loaded, 64)
                        for b in range(B + 1):
                            if b < B:
                                u = b % 2
                                pe.wait_ge(ln["normed"], TPB * b + TPB)
                                if b >= 2:
                                    pe.wait_ge(yT_ready, CC * (b - 1))
                                for c in range(CC):
                                    for s in range(TPB):
                                        last = pe.transpose(bank[Y_BANKS[u][c]][:, s * P:(s + 1) * P],
                                                            y[:, u, s, c * P:(c + 1) * P], ident[:])
                                    last.then_inc(yT_made, 1)
                            if b:
                                pe.wait_ge(yT_ready, CC * b)
                                for t in range((b - 1) * TPB, b * TPB):
                                    for c in range(CC):
                                        last = pe.matmul(bank[L_BANKS[t // HALF]][:, (t % HALF) * EXPERTS:
                                                                                  (t % HALF + 1) * EXPERTS],
                                                         yT[:, c, t * P:(t + 1) * P], router[:, c, :],
                                                         start=c == 0, stop=c == CC - 1)
                                last.then_inc(logits_made, 1)

                    @block.scalar
                    def _(act):
                        for b in range(B):
                            ln_std(act, ln, b)
                            for c in range(CC):
                                act.wait_ge(yT_made, CC * b + c + 1)
                                act.copy(yT[:, c, b * S:(b + 1) * S], bank[Y_BANKS[b % 2][c]][:]).then_inc(yT_ready, 1)
                        for half in range(2):
                            act.wait_ge(logits_made, B // 2 * (half + 1))
                            act.activation(score[:, half * HALF:(half + 1) * HALF, :],
                                           bank[L_BANKS[half]][:].rearrange("p (t e) -> p t e", e=EXPERTS), ACT.Sigmoid
                                           ).then_inc(score_ready, 1)

                    @block.vector
                    def _(dve):
                        for b in range(B):
                            def source(s):
                                return residual[:, b * TPB + s, :]
                            ln_moments(dve, ln, b, source, 1e-5)
                            if b >= 2:
                                dve.wait_ge(yT_made, CC * (b - 1))
                            ln_normalize(dve, ln, b, source, lambda s: y[:, b % 2, s, :])
                        dve.wait_ge(c_loaded, 64)
                        dve.wait_ge(score_ready, 2)
                        count = [0]

                        def then(ins):
                            ins.then_inc(step, 1)
                            count[0] += 1
                            dve.wait_ge(step, count[0])
                        then(dve.tensor_tensor(sfc[:], score[:], bias[:].unsqueeze(1).broadcast_to([P, TILES, EXPERTS]),
                                               ALU.add))
                        for t in range(TILES):
                            for g in range(GROUPS):
                                dve.max(best[:, t, g, :], sfc[:, t, g * 8:(g + 1) * 8]).then_inc(step, 1)
                        count[0] += TILES * GROUPS
                        dve.wait_ge(step, count[0])
                        then(dve.tensor_tensor(pair[:], best[:, :, :, 0], best[:, :, :, 1], ALU.add))
                        mine = pair[:].unsqueeze(3).broadcast_to([P, TILES, GROUPS, GROUPS])
                        other = pair[:].unsqueeze(2).broadcast_to([P, TILES, GROUPS, GROUPS])
                        dve.tensor_tensor(wins[:], other, mine, ALU.is_gt)
                        then(dve.tensor_tensor(ties[:], other, mine, ALU.is_equal))
                        then(dve.tensor_tensor(ties[:], ties[:], before[:].unsqueeze(1).broadcast_to(
                            [P, TILES, GROUPS, GROUPS]), ALU.mult))
                        then(dve.tensor_tensor(wins[:], wins[:], ties[:], ALU.add))
                        then(dve.reduce_sum(rank[:], wins[:], axis=AX.X))
                        then(dve.tensor_scalar(rank[:], rank[:], float(TOP_GROUPS), None, ALU.is_lt))
                        by_group = sfc[:].rearrange("p t (g e) -> p t g e", g=GROUPS)
                        then(dve.tensor_tensor(by_group, by_group, rank[:].unsqueeze(3).broadcast_to(
                            [P, TILES, GROUPS, EXPERTS // GROUPS]), ALU.mult))
                        then(dve.tensor_scalar(sfc[:], sfc[:], 0.0, None, ALU.add))
                        for t in range(TILES):
                            dve.max(top8[:, t, :], sfc[:, t, :]).then_inc(step, 1)
                        count[0] += TILES
                        dve.wait_ge(step, count[0])
                        for t in range(TILES):
                            dve.max_index(where[:, t, :], top8[:, t, :], sfc[:, t, :]).then_inc(step, 1)
                        count[0] += TILES
                        dve.wait_ge(step, count[0])
                        then(dve.tensor_copy(where_f[:], where[:]))
                        for k in range(TOP_K):
                            dve.tensor_tensor(hit[:, k], index[:].unsqueeze(1).broadcast_to([P, TILES, EXPERTS]),
                                              where_f[:, :, k:k + 1].broadcast_to([P, TILES, EXPERTS]), ALU.is_equal
                                              ).then_inc(step, 1)
                        count[0] += TOP_K
                        dve.wait_ge(step, count[0])
                        for k in range(1, TOP_K):
                            then(dve.tensor_tensor(hit[:, 0], hit[:, 0], hit[:, k], ALU.add))
                        then(dve.tensor_tensor(hit[:, 0], hit[:, 0], score[:], ALU.mult))
                        then(dve.reduce_sum(norm_w[:], hit[:, 0], axis=AX.X))
                        then(dve.tensor_scalar(norm_w[:], norm_w[:], 1e-20, None, ALU.add))
                        then(dve.reciprocal(norm_w[:], norm_w[:]))
                        then(dve.tensor_tensor(cw[:, :, 0:EXPERTS], hit[:, 0], norm_w[:].unsqueeze(2).broadcast_to(
                            [P, TILES, EXPERTS]), ALU.mult))
                        dve.tensor_scalar(cw[:, :, 0:EXPERTS], cw[:, :, 0:EXPERTS], ROUTE_SCALE, None, ALU.mult
                                          ).then_inc(cw_ready, 1)
                        dve.memset(cw[:, :, EXPERTS:ALL_EXPERTS], 1.0).then_inc(cw_ready, 1)

            w = sb(st, "p5_w", [P, 2, 2 * CC * INNER + C])
            silu = sb(st, "p5_silu", [P, 2, S])
            hT = sb(st, "p5_hT", [P, 2, S])
            w_loaded = [sem("p5_w_loaded0"), sem("p5_w_loaded1")]
            gate_made, up_made, silu_done, hT_ready, down_made, added, stored = [sem("p5_" + k) for k in (
                "gate_made", "up_made", "silu_done", "hT_ready", "down_made", "added", "stored")]
            G_BANKS, U_BANKS, D_BANKS = (0, 1), (2, 3), (4, 5, 6, 7)

            def experts(eng, body):
                for e in range(2):
                    body(e, e)
                with eng.Fori(1, ALL_EXPERTS // 2 - 1) as i:
                    for u in range(2):
                        body(2 * i + u, u)
                for u in range(2):
                    body(ALL_EXPERTS - 2 + u, u)

            def wait_count(eng, semaphore, count):
                if not isinstance(count, int) or count > 0:
                    eng.wait_ge(semaphore, count)

            with nc.Block() as block:
                @block.sync
                def _(sp):
                    def load(e, u):
                        wait_count(sp, down_made, 2 * B * (e - 1))
                        sp.dma_start(w[:, u, :], a["experts"][ds(e, 1)].rearrange("e p n -> p (e n)")
                                     ).then_inc(w_loaded[u], 16)
                    experts(sp, load)
                    for b in range(B):
                        sp.wait_ge(added, TILES * (ALL_EXPERTS - 1) + TPB * (b + 1))
                        sp.dma_start(out[b].rearrange("(s p) c -> p s c", p=P), residual[:, b * TPB:(b + 1) * TPB, :]
                                     ).then_inc(stored, 16)
                    sp.wait_ge(stored, 16 * B)

                @block.tensor
                def _(pe):
                    def body(e, u):
                        pe.wait_ge(w_loaded[u], 16 * (e // 2 + 1) if isinstance(e, int) else 8 * (e - u) + 16)

                        def down(b):
                            pe.wait_ge(hT_ready, B * e + b + 1)
                            for j in range(2):
                                bk = D_BANKS[2 * (b % 2) + j]
                                wait_count(pe, added, TILES * e + TPB * b + 2 * j - 6)
                                for s in (2 * j, 2 * j + 1):
                                    last = pe.matmul(bank[bk][:, (s % 2) * C:(s % 2 + 1) * C],
                                                     hT[:, b % 2, s * P:(s + 1) * P], w[:, u, 2 * CC * INNER:],
                                                     start=True, stop=True)
                                last.then_inc(down_made, 1)
                        for b in range(B):
                            for first, banks, made, used in ((0, G_BANKS, gate_made, silu_done),
                                                             (CC * INNER, U_BANKS, up_made, hT_ready)):
                                wait_count(pe, used, B * e + b - 1)
                                for c in range(CC):
                                    last = pe.matmul(bank[banks[b % 2]][:],
                                                     w[:, u, first + c * INNER:first + (c + 1) * INNER],
                                                     yT[:, c, b * S:(b + 1) * S], start=c == 0, stop=c == CC - 1)
                                last.then_inc(made, 1)
                            if b:
                                down(b - 1)
                        down(B - 1)
                    experts(pe, body)

                @block.scalar
                def _(act):
                    def body(e, u):
                        for b in range(B):
                            act.wait_ge(gate_made, B * e + b + 1)
                            wait_count(act, hT_ready, B * e + b - 1)
                            act.activation(silu[:, b % 2, :], bank[G_BANKS[b % 2]][:], ACT.Silu).then_inc(silu_done, 1)
                    experts(act, body)

                @block.vector
                def _(dve):
                    def body(e, u):
                        def add(b):
                            for s in range(TPB):
                                t = b * TPB + s
                                if s % 2 == 0:
                                    dve.wait_ge(down_made, 2 * (B * e + b) + s // 2 + 1)
                                dve.scalar_tensor_tensor(
                                    residual[:, t, :], bank[D_BANKS[2 * (b % 2) + s // 2]][:, (s % 2) * C:(s % 2 + 1) * C],
                                    cw[:, t, ds(e, 1)], residual[:, t, :], op0=ALU.mult, op1=ALU.add).then_inc(added, 1)
                        for b in range(B):
                            dve.wait_ge(silu_done, B * e + b + 1)
                            dve.wait_ge(up_made, B * e + b + 1)
                            wait_count(dve, down_made, 2 * (B * e + b - 1))
                            dve.tensor_tensor(hT[:, b % 2, :], bank[U_BANKS[b % 2]][:], silu[:, b % 2, :], ALU.mult
                                              ).then_inc(hT_ready, 1)
                            if b:
                                add(b - 1)
                        add(B - 1)
                    experts(dve, body)


PLAIN = {
    "x": "L0_attn_hidden_states", "wq": "L0_attn_Wq", "wk": "L0_attn_Wk", "wv": "L0_attn_Wv", "bk": "L0_attn_bk",
    "bv": "L0_attn_bv", "wo": "L0_attn_Wo", "bo": "L0_attn_bo", "ln_scale": "L0_attn_ln_scale",
    "ln_bias": "L0_attn_ln_bias", "b2": "L0_ffn_b2",
    "bqkv": "L1_attn_bqkv", "bproj": "L1_attn_bproj", "router_bias": "L1_ffn_router_bias",
}
COLUMNS = {"bq_col": "L0_attn_bq", "bk_col": "L0_attn_bk", "b1_col": "L0_ffn_b1"}
TRANSPOSED = {"relT": "L0_attn_rel_embeddings", "w1T": "L0_ffn_W1", "w2T": "L0_ffn_W2", "wqkvT": "L1_attn_Wqkv",
              "wprojT": "L1_attn_Wproj", "routerT": "L1_ffn_router_weight"}


def expert_weights(inputs):
    def by_row(w):
        e, n, k = w.shape
        return w.transpose(0, 2, 1).reshape(e, k // P, P, n).transpose(0, 2, 1, 3).reshape(e, P, -1)
    gate, up, down = (np.asarray(inputs["L1_ffn_" + k]) for k in ("gate_w", "up_w", "down_w"))
    s_gate, s_up, s_down = (np.asarray(inputs["L1_ffn_shared_" + k]) for k in ("gate_w", "up_w", "down_w"))
    gate = np.concatenate([gate, s_gate.reshape(SHARED, INNER, C)])
    up = np.concatenate([up, s_up.reshape(SHARED, INNER, C)])
    down = np.concatenate([down, s_down.reshape(C, SHARED, INNER).transpose(1, 0, 2)])
    return np.ascontiguousarray(np.concatenate([by_row(gate), by_row(up), by_row(down)], axis=2))


def kernel(**inputs):
    import concourse.bacc as bacc
    from concourse import mybir
    from concourse.bass_utils import run_bass_kernel_spmd

    nc = bacc.Bacc("TRN2", target_bir_lowering=False, num_devices=1)
    arrays = {k: np.ascontiguousarray(inputs[n]) for k, n in PLAIN.items()}
    arrays["scale"] = np.ascontiguousarray(inputs["L0_ffn_scale"]).reshape(1)
    arrays.update({k: np.ascontiguousarray(np.asarray(inputs[n]).T) for k, n in TRANSPOSED.items()})
    arrays.update({k: np.ascontiguousarray(np.asarray(inputs[n]).reshape(-1, P).T) for k, n in COLUMNS.items()})
    arrays["experts"] = expert_weights(inputs)
    arrays["hot_c2p"], arrays["hot_p2c"] = one_hot_tables()
    arrays["group_before"] = (np.arange(GROUPS)[None, :] < np.arange(GROUPS)[:, None]).astype(np.float32).reshape(-1)
    arrays["expert_index"] = np.arange(EXPERTS, dtype=np.float32)
    a = {k: nc.dram_tensor("in_" + k, v.shape, mybir.dt.from_np(v.dtype), kind="ExternalInput").ap()
         for k, v in arrays.items()}
    out = nc.dram_tensor("out", (B, S, C), mybir.dt.float32, kind="ExternalOutput").ap()
    build(nc, a, out)
    r = run_bass_kernel_spmd(nc, [{"in_" + k: v for k, v in arrays.items()}], core_ids=[0])
    return r.results[0]["out"]
```

```python
from contextlib import ExitStack

import numpy as np

B, S, C = 8, 512, 256
P = 128
H, D = 16, 16
TILES = B * S // P
TPB = S // P
CC = C // P
REL = 128
SPAN, MAX_POS = 64, 128
NEAR = 3 * P
DIST = 512
R = 8
KCHUNK = 64
STACK = 6
FFN = 1024
EXPERTS, INNER, TOP_K, GROUPS, TOP_GROUPS = 32, 128, 4, 4, 2
ROUTE_SCALE = 2.5
SHARED = 2
ALL_EXPERTS = EXPERTS + SHARED
SLOT_TILES = TILES * TOP_K + EXPERTS


def bucket_indices(delta):
    mid = SPAN // 2
    f = np.float32

    def bucket(rel):
        a = np.where((rel < mid) & (rel > -mid), mid - 1, np.abs(rel))
        log = np.ceil(np.log((a / f(mid)).astype(f)) / np.log(f((MAX_POS - 1) / mid)) * f(mid - 1)) + mid
        return np.where(a <= mid, a, log * np.sign(rel)).astype(np.int32)

    c2p = np.clip(bucket(delta) + SPAN, 0, 2 * SPAN - 1)
    p2c = np.clip(-bucket(-delta) + SPAN, 0, 2 * SPAN - 1)
    return c2p, p2c


def one_hot_tables():
    c2p, _ = bucket_indices(DIST // 2 - 1 - np.arange(DIST))
    _, p2c = bucket_indices(np.arange(DIST) - (DIST // 2 - 1))
    rows = np.arange(REL)[:, None]
    return (rows == c2p[None]).astype(np.float32), (rows == p2c[None]).astype(np.float32)


def build(nc, a, out, taps=None):
    import concourse.bass as bass
    from concourse import mybir

    F32, BF16 = mybir.dt.float32, mybir.dt.bfloat16
    U32, I32 = mybir.dt.uint32, mybir.dt.int32
    ACT, ALU, AX = mybir.ActivationFunctionType, mybir.AluOpType, mybir.AxisListType
    ds = bass.ds
    whole = ExitStack()
    with whole:
        stage_semaphores = []

        def sem(name):
            stage_semaphores.append(nc.alloc_semaphore(name))
            return stage_semaphores[-1]

        def end_stage():
            nc.clear_and_free_semaphores(list(stage_semaphores))
            nc.all_engine_barrier()
            stage_semaphores.clear()

        def sb(stack, name, shape, dt=F32):
            return stack.enter_context(nc.sbuf_tensor(name, shape, dt))

        def dram(name, shape, dt):
            return nc.dram_tensor(name, shape, dt, kind="Internal").ap()

        bank = [whole.enter_context(nc.psum_tensor(f"bank{i}", [P, 512], F32)) for i in range(8)]
        ident = sb(whole, "ident", [P, P])
        spacer, ident_zeroed, ident_ready = [nc.alloc_semaphore(n) for n in (
            "spacer", "ident_zeroed", "ident_ready")]

        normed_d = dram("normed_d", [B, P, TPB, C], F32)
        q_stack_d = dram("q_stack_d", [H, STACK, D, B * S], BF16)
        qf_stack_d = dram("qf_stack_d", [H, STACK, D, B * S], BF16)
        k_stack_d = dram("k_stack_d", [H, STACK, D, B * S], BF16)
        c2p_stack_d = dram("c2p_stack_d", [H, STACK, D, DIST], BF16)
        k_by_r_d = dram("k_by_r_d", [C, 3, R, B, S // R], BF16)
        p2c_parts_d = dram("p2c_parts_d", [C, 3, DIST], BF16)
        c2p_d = dram("c2p_d", [2, B, P, DIST], F32)
        ctxT_d = dram("ctxT_d", [C, B, S], F32)

        def batches(eng, body):
            for b in range(2):
                body(b, b)
            with eng.Fori(1, B // 2 - 1) as i:
                for u in range(2):
                    body(2 * i + u, u)
            for u in range(2):
                body(B - 2 + u, u)

        def each_batch(eng, body):
            with eng.Fori(0, B // 2 - 1) as i:
                for u in range(2):
                    body(2 * i + u, u)
            for u in range(2):
                body(B - 2 + u, u)

        def exists(b, ahead):
            return not isinstance(b, int) or b + ahead < B

        def apart(eng):
            eng.sem_inc(spacer, 1)

        def layer_norm(name, stack, tiles):
            n = {"tiles": tiles}
            n["stats"] = sb(stack, name + "_stats", [P, tiles, 6])
            n["mv"] = sb(stack, name + "_mv", [P, tiles, 2])
            for k in ("var", "std", "rstd", "tmp"):
                n[k] = sb(stack, f"{name}_{k}", [P, tiles])
            for k in ("stats_done", "mv_done", "var_done", "std_done", "rstd_step", "normed"):
                n[k] = sem(f"{name}_{k}")
            return n

        def ln_moments(dve, n, k, source, eps):
            T = n["tiles"]
            for s in range(T):
                dve.bn_stats(n["stats"][:, s, :], source(s)).then_inc(n["stats_done"], 1)
            dve.wait_ge(n["stats_done"], T * k + T)
            apart(dve)
            for s in range(T):
                dve.bn_aggr(n["mv"][:, s, :], n["stats"][:, s, :]).then_inc(n["mv_done"], 1)
            dve.wait_ge(n["mv_done"], T * k + T)
            dve.tensor_scalar(n["var"][:], n["mv"][:, :, 1], eps, None, ALU.add).then_inc(n["var_done"], 1)

        def ln_std(act, n, k):
            act.wait_ge(n["var_done"], k + 1)
            act.activation(n["std"][:], n["var"][:], ACT.Sqrt).then_inc(n["std_done"], 1)

        def ln_normalize(dve, n, k, source, dest):
            T, step = n["tiles"], n["rstd_step"]
            dve.wait_ge(n["std_done"], k + 1)
            dve.reciprocal(n["rstd"][:], n["std"][:]).then_inc(step, 1)
            dve.wait_ge(step, 5 * k + 1)
            dve.tensor_tensor(n["tmp"][:], n["rstd"][:], n["rstd"][:], ALU.mult).then_inc(step, 1)
            dve.wait_ge(step, 5 * k + 2)
            dve.tensor_tensor(n["tmp"][:], n["tmp"][:], n["var"][:], ALU.mult).then_inc(step, 1)
            dve.wait_ge(step, 5 * k + 3)
            dve.tensor_scalar(n["tmp"][:], n["tmp"][:], -0.5, 1.5, ALU.mult, ALU.add).then_inc(step, 1)
            dve.wait_ge(step, 5 * k + 4)
            dve.tensor_tensor(n["rstd"][:], n["rstd"][:], n["tmp"][:], ALU.mult).then_inc(step, 1)
            dve.wait_ge(step, 5 * k + 5)
            for s in range(T):
                dve.tensor_scalar(dest(s), source(s), n["mv"][:, s, 0:1], n["rstd"][:, s:s + 1],
                                  ALU.subtract, ALU.mult).then_inc(n["normed"], 1)

        attn = ExitStack()
        v_all = sb(attn, "v_all", [P, TILES, C])

        CH = 3 * CC
        with ExitStack() as st:
            x_in = sb(st, "p1_x", [P, 2, TPB, C])
            normed = sb(st, "p1_normed", [P, 2, TPB, C])
            nT = sb(st, "p1_nT", [P, CC, S])
            wq, wk, wv = [sb(st, n, [P, CC, C]) for n in ("p1_wq", "p1_wk", "p1_wv")]
            bq, bk = sb(st, "p1_bq", [P, CC]), sb(st, "p1_bk", [P, CC])
            bq_far = sb(st, "p1_bq_far", [P, CC, 2])
            bk_row, bv_row = sb(st, "p1_bk_row", [P, C]), sb(st, "p1_bv_row", [P, 2, C])
            relT = sb(st, "p1_relT", [P, CC, REL])
            hot = sb(st, "p1_hot", [P, 2, DIST])
            pos_k = sb(st, "p1_pos_k", [P, C])
            full = sb(st, "p1_full", [P, CH, S])
            rest = sb(st, "p1_rest", [P, CH, S])
            parts = sb(st, "p1_parts", [P, CH, 3, S], BF16)
            k_by_r = sb(st, "p1_k_by_r", [P, CC, 3, R, S // R], BF16)
            tab = sb(st, "p1_tab", [P, 2 * CC, DIST])
            tab_rest = sb(st, "p1_tab_rest", [P, 2 * CC, DIST])
            tab_parts = sb(st, "p1_tab_parts", [P, 2 * CC, 3, DIST], BF16)
            ln = layer_norm("ln1", st, TPB)
            w_loaded, tables_loaded = sem("p1_w_loaded"), sem("p1_tables_loaded")
            x_loaded = [sem("p1_x_loaded0"), sem("p1_x_loaded1")]
            n_stored = [sem("p1_n_stored0"), sem("p1_n_stored1")]
            nT_made, nT_ready, projected, v_projected, v_ready = [sem("p1_" + n) for n in (
                "nT_made", "nT_ready", "projected", "v_projected", "v_ready")]
            full_ready, part1_ready, rest_ready, part2_ready, parts_ready = [sem("p1_" + n) for n in (
                "full_ready", "part1_ready", "rest_ready", "part2_ready", "parts_ready")]
            parts_stored = [sem(f"p1_parts_stored{m}") for m in range(CH)]
            by_r_ready, by_r_stored = sem("p1_by_r_ready"), sem("p1_by_r_stored")
            pos_made, pos_ready, tab_made, tab_ready, tab_part1, tab_left, tab_part2, tab_split, far_bias = [
                sem("p1_" + n) for n in ("pos_made", "pos_ready", "tab_made", "tab_ready", "tab_part1",
                                         "tab_left", "tab_part2", "tab_split", "far_bias")]
            tab_stored = sem("p1_tab_stored")

            def store_stack(eng, stack_d, part_sb, m, cols, done, order):
                heads = H // CC
                for slot, part in enumerate(order):
                    eng.dma_start(stack_d[m * heads:(m + 1) * heads, slot, :, cols], part_sb[:, part, :]
                                  ).then_inc(done, 16)
            Q_ORDER, K_ORDER = (0, 1, 2, 0, 1, 0), (0, 0, 0, 1, 1, 2)

            with nc.Block() as block:
                @block.sync
                def _(sp):
                    for b in range(2):
                        sp.dma_start(x_in[:, b], a["x"][b].rearrange("(s p) c -> p s c", p=P)).then_inc(x_loaded[b], 16)

                    def body(b, u):
                        sp.wait_ge(ln["normed"], TPB * b + TPB)
                        sp.dma_start(normed_d[ds(b, 1)].rearrange("a p s c -> p (a s) c"), normed[:, u]
                                     ).then_inc(n_stored[u], 16)
                        if exists(b, 2):
                            sp.dma_start(x_in[:, u], a["x"][ds(b + 2, 1)].rearrange("a (s p) c -> p (a s) c", p=P)
                                         ).then_inc(x_loaded[u], 16)
                        for m in range(4):
                            sp.wait_ge(parts_ready, CH * b + m + 1)
                            store_stack(sp, (q_stack_d, qf_stack_d)[m // 2], parts[:, m], m % 2,
                                        ds(b * S, S), parts_stored[m], Q_ORDER)
                        for c in range(CC):
                            sp.wait_ge(by_r_ready, CC * (b + 1) + c + 1)
                            sp.dma_start(k_by_r_d[c * P:(c + 1) * P, :, :, ds(b, 1), :].rearrange("p t r b k -> p (t r) (b k)"),
                                         k_by_r[:, c].rearrange("p t r k -> p (t r) k")).then_inc(by_r_stored, 16)
                    each_batch(sp, body)
                    for u in range(2):
                        sp.wait_ge(n_stored[u], 16 * (B // 2 + 1))
                    for m in range(4):
                        sp.wait_ge(parts_stored[m], 16 * STACK * (B + 1))
                    sp.wait_ge(by_r_stored, 16 * CC * (B + 1))

                @block.gpsimd
                def _(pool):
                    pool.memset(ident[:], 0.0).then_inc(ident_zeroed, 1)
                    pool.wait_ge(ident_zeroed, 1)
                    pool.affine_select(out=ident[:], in_=ident[:], compare_op=ALU.not_equal, fill=1.0, base=0,
                                       pattern=[[-1, P]], channel_multiplier=1).then_inc(ident_ready, 1)
                    pool.sem_inc(by_r_stored, 16 * CC)
                    pool.sem_inc(by_r_ready, CC)
                    for w, n in ((wk, "wk"), (wq, "wq"), (wv, "wv")):
                        pool.dma_start(w[:], a[n].rearrange("(c p) n -> p c n", p=P)).then_inc(w_loaded, 16)
                    for w, n in ((bq, "bq_col"), (bk, "bk_col")):
                        pool.dma_start(w[:], a[n]).then_inc(w_loaded, 16)
                    for j in range(2):
                        pool.dma_start(bv_row[:, j, :], a["bv"].rearrange("(o n) -> o n", o=1).broadcast_to([P, C])
                                       ).then_inc(w_loaded, 16)
                    pool.dma_start(bk_row[:], a["bk"].rearrange("(o n) -> o n", o=1).broadcast_to([P, C])
                                   ).then_inc(tables_loaded, 16)
                    pool.dma_start(relT[:], a["relT"].rearrange("(c p) n -> p c n", p=P)).then_inc(tables_loaded, 16)
                    pool.dma_start(hot[:, 0], a["hot_c2p"]).then_inc(tables_loaded, 16)
                    pool.dma_start(hot[:, 1], a["hot_p2c"]).then_inc(tables_loaded, 16)
                    for m in range(2 * CC):
                        pool.wait_ge(tab_split, m + 1)
                        if m < CC:
                            store_stack(pool, c2p_stack_d, tab_parts[:, m], m, slice(0, DIST), tab_stored, K_ORDER)
                        else:
                            pool.dma_start(p2c_parts_d[(m - CC) * P:(m - CC + 1) * P], tab_parts[:, m]
                                           ).then_inc(tab_stored, 16)

                    def body(b, u):
                        for m in range(4, CH):
                            pool.wait_ge(parts_ready, CH * b + m + 1)
                            store_stack(pool, k_stack_d, parts[:, m], m % 2, ds(b * S, S), parts_stored[m], K_ORDER)
                    each_batch(pool, body)
                    for m in range(4, CH):
                        pool.wait_ge(parts_stored[m], 16 * STACK * B)
                    pool.wait_ge(tab_stored, 16 * CC * (1 + STACK))

                @block.tensor
                def _(pe):
                    pe.sem_inc(v_projected, 2)
                    pe.wait_ge(ident_ready, 1)
                    pe.wait_ge(w_loaded, 16 * 7)
                    pe.wait_ge(tables_loaded, 16 * 4)
                    for c in range(CC):
                        last = pe.matmul(bank[6][:, 0:C], relT[:, c, :], wk[:, c, :], start=c == 0, stop=c == CC - 1)
                    last.then_inc(pos_made, 1)
                    pe.wait_ge(pos_ready, 1)
                    for m in range(2 * CC):
                        c = m % CC
                        pe.matmul(bank[2 + m][:], pos_k[:, c * P:(c + 1) * P], hot[:, m // CC], start=True, stop=True
                                  ).then_inc(tab_made, 1)
                    pe.wait_ge(tab_ready, 2 * CC)

                    def body(b, u):
                        pe.wait_ge(ln["normed"], TPB * b + TPB)
                        pe.wait_ge(nT_ready, CC * (b + 1))
                        for c in range(CC):
                            for s in range(TPB):
                                last = pe.transpose(bank[c][:, s * P:(s + 1) * P], normed[:, u, s, c * P:(c + 1) * P],
                                                    ident[:])
                            last.then_inc(nT_made, 1)
                        pe.wait_ge(nT_ready, CC * (b + 2))
                        for m in range(4):
                            w = (wq, wk)[m // 2]
                            pe.wait_ge(full_ready, CH * b + m + 3)
                            for c in range(CC):
                                last = pe.matmul(bank[2 + m][:], w[:, c, (m % 2) * P:(m % 2 + 1) * P], nT[:, c, :],
                                                 start=c == 0, stop=c == CC - 1)
                            last.then_inc(projected, 1)
                        for j in range(2):
                            pe.wait_ge(v_ready, 2 * b + j + 1)
                            for s in (2 * j, 2 * j + 1):
                                for c in range(CC):
                                    last = pe.matmul(bank[6 + j][:, (s % 2) * C:(s % 2 + 1) * C],
                                                     nT[:, c, s * P:(s + 1) * P], wv[:, c, :],
                                                     start=c == 0, stop=c == CC - 1)
                            last.then_inc(v_projected, 1)
                    each_batch(pe, body)

                @block.scalar
                def _(act):
                    act.sem_inc(nT_ready, CC)
                    act.sem_inc(full_ready, CH)
                    for m in range(4):
                        act.sem_inc(parts_stored[m], 16 * STACK)
                    for m in range(2 * CC):
                        act.wait_ge(tab_made, m + 1)
                        act.copy(tab[:, m, :], bank[2 + m][:]).then_inc(tab_ready, 1)
                    ln_std(act, ln, 0)
                    act.wait_ge(far_bias, 1)

                    def body(b, u):
                        if exists(b, 1):
                            ln_std(act, ln, b + 1)
                        for c in range(CC):
                            act.wait_ge(nT_made, CC * b + c + 1)
                            if c == 0:
                                act.wait_ge(v_projected, 2 * b + 2)
                            act.copy(nT[:, c, :], bank[c][:]).then_inc(nT_ready, 1)
                        for m in range(CH):
                            kind, c = m // 2, m % 2
                            source = bank[(2, 2, 4)[kind] + c]
                            act.wait_ge(projected, 4 * b + (0, 0, 2)[kind] + c + 1)
                            act.wait_ge(rest_ready, CH * b + m + 1)
                            if kind == 1:
                                act.activation(full[:, m, 0:S // 2], source[:, 0:S // 2], ACT.Identity,
                                               bias=bq_far[:, c, 0:1])
                                act.activation(full[:, m, S // 2:S], source[:, S // 2:S], ACT.Identity,
                                               bias=bq_far[:, c, 1:2]).then_inc(full_ready, 1)
                            else:
                                act.activation(full[:, m, :], source[:], ACT.Identity,
                                               bias=(bq if kind == 0 else bk)[:, c:c + 1]).then_inc(full_ready, 1)
                            act.wait_ge(full_ready, CH * (b + 1) + m + 1)
                            if kind < 2:
                                act.wait_ge(parts_stored[m], 16 * STACK * (b + 1))
                            elif not isinstance(b, int) or b > 0:
                                act.wait_ge(parts_stored[m], 16 * STACK * b)
                            if kind == 2:
                                act.wait_ge(by_r_ready, CC * b + c + 1)
                            act.copy(parts[:, m, 0, :], full[:, m, :]).then_inc(part1_ready, 1)
                    batches(act, body)

                @block.vector
                def _(dve):
                    dve.sem_inc(v_ready, 2)
                    dve.sem_inc(rest_ready, CH)
                    for u in range(2):
                        dve.sem_inc(n_stored[u], 16)
                    dve.wait_ge(tables_loaded, 16 * 4)
                    dve.wait_ge(pos_made, 1)
                    dve.tensor_tensor(pos_k[:], bank[6][:, 0:C], bk_row[:], ALU.add).then_inc(pos_ready, 1)

                    def norm(b, u, half):
                        dve.wait_ge(x_loaded[u], 16 * half + 16)
                        ln_moments(dve, ln, b, lambda s: x_in[:, u, s, :], 1e-5)
                        dve.wait_ge(n_stored[u], 16 * half + 16)
                        ln_normalize(dve, ln, b, lambda s: x_in[:, u, s, :], lambda s: normed[:, u, s, :])

                    dve.wait_ge(tab_ready, 2 * CC)
                    for c in range(CC):
                        for side, x in ((0, 0), (1, DIST - 2)):
                            last = dve.tensor_tensor(bq_far[:, c, side:side + 1], bq[:, c:c + 1],
                                                     tab[:, CC + c, x:x + 1], ALU.add)
                    last.then_inc(far_bias, 1)
                    norm(0, 0, 0)
                    for m in range(2 * CC):
                        dve.tensor_copy(tab_parts[:, m, 0, :], tab[:, m, :]).then_inc(tab_part1, 1)
                        dve.wait_ge(tab_part1, m + 1)
                        dve.tensor_tensor(tab_rest[:, m, :], tab[:, m, :], tab_parts[:, m, 0, :], ALU.subtract
                                          ).then_inc(tab_left, 1)
                        dve.wait_ge(tab_left, m + 1)
                        dve.tensor_copy(tab_parts[:, m, 1, :], tab_rest[:, m, :]).then_inc(tab_part2, 1)
                        dve.wait_ge(tab_part2, m + 1)
                        dve.tensor_tensor(tab_parts[:, m, 2, :], tab_rest[:, m, :], tab_parts[:, m, 1, :],
                                          ALU.subtract).then_inc(tab_split, 1)

                    def body(b, u, half):
                        if exists(b, 1):
                            dve.wait_ge(nT_made, CC * b + 1)
                            norm(b + 1, 1 - u, half + u)
                        for m in range(CH):
                            dve.wait_ge(part1_ready, CH * b + m + 1)
                            dve.tensor_tensor(rest[:, m, :], full[:, m, :], parts[:, m, 0, :], ALU.subtract
                                              ).then_inc(rest_ready, 1)
                            dve.wait_ge(rest_ready, CH * (b + 1) + m + 1)
                            dve.tensor_copy(parts[:, m, 1, :], rest[:, m, :]).then_inc(part2_ready, 1)
                            dve.wait_ge(part2_ready, CH * b + m + 1)
                            dve.tensor_tensor(parts[:, m, 2, :], rest[:, m, :], parts[:, m, 1, :], ALU.subtract
                                              ).then_inc(parts_ready, 1)
                            if m >= 4:
                                c = m - 4
                                dve.wait_ge(by_r_stored, 16 * CC * (b + 1))
                                dve.wait_ge(parts_ready, CH * b + m + 1)
                                dve.tensor_copy(k_by_r[:, c].rearrange("p t r k -> p t k r"),
                                                parts[:, m].rearrange("p t (k r) -> p t k r", r=R)
                                                ).then_inc(by_r_ready, 1)
                        for j in range(2):
                            dve.wait_ge(v_projected, 2 * (b + 1) + j + 1)
                            dve.tensor_tensor(v_all[:, ds(b * TPB + 2 * j, 2), :],
                                              bank[6 + j][:].rearrange("p (s c) -> p s c", s=2), bv_row[:], ALU.add
                                              ).then_inc(v_ready, 1)
                    with dve.Fori(0, B // 2 - 1) as i:
                        for u in range(2):
                            body(2 * i + u, u, i)
                    for u in range(2):
                        body(B - 2 + u, u, B // 2 - 1)
        end_stage()

        UNITS = H * TPB
        SCALE = float(1.0 / np.sqrt(np.float32(D * 3)))
        WINDOW = DIST - R
        ZERO_X = DIST // 2 - R

        def is_far(t, j):
            return abs(j // 2 - t) > 1

        LEAD = 2
        with ExitStack() as st:
            q6 = sb(st, "q6", [STACK * D, TPB, 2, B, P], BF16)
            k6 = sb(st, "k6", [STACK * D, 2, B * S], BF16)
            tab6 = sb(st, "tab6", [STACK * D, 2, DIST], BF16)
            p2c8 = sb(st, "p2c8", [P, 2, 3, WINDOW], BF16)
            kbd = sb(st, "kbd", [P, 2, 3, R, B, S // R], BF16)
            v_h = sb(st, "v_h", [P, 2, TILES, D])
            c2p_out = sb(st, "c2p_out", [P, 2, 2, DIST])
            c2p = sb(st, "c2p", [P, 2, B, NEAR])
            c2p_far = sb(st, "c2p_far", [P, 2, 2, B])
            probs = sb(st, "probs", [P, 2, B, S])
            probsT = sb(st, "probsT", [P, 2, TPB, P])
            ctxT = sb(st, "ctxT", [D, B, P])
            sums, inv_sums = sb(st, "sums", [P, 2, B]), sb(st, "inv_sums", [P, 2, B])
            row_max, neg_max = sb(st, "row_max", [P, 2, B]), sb(st, "neg_max", [P, 2, B])
            q_loaded = [sem(f"q_loaded{t}") for t in range(TPB)]
            head_loaded = [sem("head_loaded0"), sem("head_loaded1")]
            kbd_loaded = [sem("kbd_loaded0"), sem("kbd_loaded1")]
            HEAD_DMAS, KBD_DMAS = 2, 2 * R
            kbd_zeroed = sem("kbd_zeroed")
            v_copied, far_copied = sem("v_copied"), sem("far_copied")
            c2p_made, c2p_copied = sem("c2p_made"), sem("c2p_copied")
            c2p_written = [sem("c2p_written0"), sem("c2p_written1")]
            c2p_loaded = [sem("c2p_loaded0"), sem("c2p_loaded1")]
            scores_made, scores_added = sem("scores_made"), sem("scores_added")
            max_done, neg_max_done, exp_done = sem("max_done"), sem("neg_max_done"), sem("exp_done")
            inv_done, probs_ready, probs_transposed = sem("inv_done"), sem("probs_ready"), sem("probs_transposed")
            late_probs_ready = sem("late_probs_ready")
            EARLY = 5
            probsT_copied = [sem("probsT_even_copied"), sem("probsT_odd_copied")]
            pv_made, ctx_copied = sem("pv_made"), sem("ctx_copied")
            ctx_written = sem("ctx_written")
            SC, A_BANKS, T_BANKS, CTX_BANKS = 3, (3, 2), (4, 5), (6, 7)

            def each_step(eng, step):
                for w in range(8 - LEAD, 8):
                    step(-1, w)
                for w in range(8):
                    step(0, w)
                with eng.Fori(1, H // 2 - 1) as i:
                    for w in range(8):
                        step(i, w)
                for w in range(8):
                    step(H // 2 - 1, w)
                step(H // 2, 0)

            def is_unit(n):
                return not isinstance(n, int) or 0 <= n < UNITS

            def wait_count(eng, semaphore, count):
                if not isinstance(count, int) or count > 0:
                    eng.wait_ge(semaphore, count)

            with nc.Block() as block:
                @block.sync
                def _(sp):
                    def load_head(h, par):
                        rows = ds(h * D, D)
                        sp.dma_start(k6[:, par, :], k_stack_d[ds(h, 1)].rearrange("h k d n -> (h k d) n")
                                     ).then_inc(head_loaded[par], 16)
                        sp.dma_start(tab6[:, par, :], c2p_stack_d[ds(h, 1)].rearrange("h k d n -> (h k d) n")
                                     ).then_inc(head_loaded[par], 16)

                    def load_kbd(h, par, part):
                        rows = ds(h * D, D)
                        for g in range(part * R // 4, (part + 1) * R // 4):
                            sp.dma_start(kbd[g * D:(g + 1) * D, par, :, R - 1 - g, :, :].rearrange("p t b k -> p t (b k)"),
                                         k_by_r_d[rows, :, R - 1 - g, :, :].rearrange("p t b k -> p t (b k)")
                                         ).then_inc(kbd_loaded[par], 16)
                            sp.dma_start(p2c8[g * D:(g + 1) * D, par, :, :], p2c_parts_d[rows, :, g:g + WINDOW]
                                         ).then_inc(kbd_loaded[par], 16)

                    def load_q(h, t):
                        for far, stack_d in enumerate((q_stack_d, qf_stack_d)):
                            sp.dma_start(q6[:, t, far],
                                         stack_d[ds(h, 1)].rearrange("h k d (b t q) -> (h k d) t b q", t=TPB, q=P)[:, t]
                                         ).then_inc(q_loaded[t], 16)

                    def step(i, w):
                        n = 8 * i + w
                        if is_unit(n + 3) and is_unit(n):
                            wait_count(sp, scores_made, 8 * n)
                            load_q(2 * i + (w + 3) // 4, (w + 3) % 4)
                        if w in (0, 4) and is_unit(n) and is_unit(n + 4):
                            load_head(2 * i + 1 + w // 4, 1 - w // 4)
                        if is_unit(n) and is_unit(n + 4 - w % 4):
                            load_kbd(2 * i + 1 + w // 4, 1 - w // 4, w % 4)
                        if is_unit(n + LEAD):
                            par = w % 2
                            for q in range(4):
                                sp.wait_ge(c2p_copied, 8 * (n + LEAD) + 2 * q + 2)
                                sp.dma_start(c2p_d[par, 2 * q:2 * q + 2].rearrange("b p n -> p b n"),
                                             c2p_out[:, q % 2]).then_inc(c2p_written[q % 2], 16)
                            for q in range(2):
                                sp.wait_ge(c2p_written[q], 16 * 2 * (n + LEAD + 1))
                            wait_count(sp, scores_added, 8 * (n + 1))
                            skew = bass.AP(c2p_d.tensor, par * B * P * DIST + P - 1,
                                           [[DIST - 1, P], [P * DIST, B], [1, NEAR]])
                            sp.dma_start(c2p[:, par], skew).then_inc(c2p_loaded[par], 16)
                        if is_unit(n - 1):
                            t, h = (w - 1) % 4, 2 * i + w // 4 - (w % 4 == 0)
                            sp.wait_ge(ctx_copied, 2 * n)
                            sp.dma_start(ctxT_d[ds(h * D, D), :, t * P:(t + 1) * P], ctxT[:]
                                         ).then_inc(ctx_written, 16)
                    load_head(0, 0)
                    load_q(0, 0)
                    load_q(0, 1)
                    load_q(0, 2)
                    sp.wait_ge(kbd_zeroed, 2)
                    for part in range(4):
                        load_kbd(0, 0, part)
                    each_step(sp, step)
                    sp.wait_ge(ctx_written, 16 * UNITS)

                @block.gpsimd
                def _(pool):
                    pool.memset(kbd[:, 1], 0.0).then_inc(kbd_zeroed, 1)

                    def copy_v(h, par):
                        pool.tensor_copy(v_h[:, par], v_all[:, :, ds(h * D, D)]).then_inc(v_copied, 1)

                    def step(i, w):
                        n = 8 * i + w
                        if w in (1, 5) and is_unit(n) and is_unit(n + 3):
                            wait_count(pool, pv_made, 8 * (n - 1))
                            apart(pool)
                            copy_v(2 * i + 1 + w // 4, 1 - w // 4)
                        if is_unit(n + LEAD):
                            wait_count(pool, scores_added, 8 * (n + 1))
                            for q in range(4):
                                pool.wait_ge(c2p_copied, 8 * (n + LEAD) + 2 * q + 2)
                                apart(pool)
                                pool.tensor_copy(c2p_far[:, w % 2, :, 2 * q:2 * q + 2],
                                                 c2p_out[:, q % 2, :, 0:DIST - 1:DIST - 2].rearrange("p b s -> p s b")
                                                 ).then_inc(far_copied, 1)
                    copy_v(0, 0)
                    each_step(pool, step)

                @block.tensor
                def _(pe):
                    def step(i, w):
                        n = 8 * i + w
                        t, par = w % 4, w // 4
                        cur, nxt, prev = is_unit(n), is_unit(n + LEAD), is_unit(n - 1)
                        tn = (w + LEAD) % 4
                        i_n, par_n = (i + 1, 0) if w + LEAD > 7 else (i, (w + LEAD) // 4)
                        par_p = ((w - 1) % 8) // 4
                        if cur:
                            if t == 0:
                                pe.wait_ge(kbd_loaded[par], 16 * KBD_DMAS * (i + 1))
                            for j in range(8):
                                if j == A_BANKS[1]:
                                    wait_count(pe, c2p_copied, 8 * (n + min(LEAD, UNITS - n) if isinstance(n, int)
                                                                    else n + LEAD))
                                wait_count(pe, scores_added, 8 * n + j - 2 if j >= SC else 8 * (n - 1) + (7, 8, 6)[j])
                                sc, far = bank[j % SC], is_far(t, j)
                                for b in range(B):
                                    last = pe.matmul(sc[:, b * KCHUNK:(b + 1) * KCHUNK], q6[:, t, int(far), b, :],
                                                     k6[:, par, b * S + j * KCHUNK:b * S + (j + 1) * KCHUNK],
                                                     start=b == 0, stop=far and b == B - 1, skip_group_check=True)
                                cols = sc[:].rearrange("p (b k r) -> p b k r", b=B, r=R)
                                for k in range(0 if far else KCHUNK // R):
                                    x0 = t * P - (j * KCHUNK + k * R) + ZERO_X
                                    for tp, kp in ((0, 0), (0, 1), (0, 2), (1, 0), (1, 1), (2, 0)):
                                        last = pe.matmul(
                                            cols[:, :, k, :], p2c8[:, par, tp, x0:x0 + P],
                                            kbd[:, par, kp, :, :, j * (KCHUNK // R) + k].rearrange("p r b -> p b r"),
                                            start=False, stop=k == KCHUNK // R - 1 and tp == 2, skip_group_check=True)
                                last.then_inc(scores_made, 1)
                        if nxt:
                            pe.wait_ge(q_loaded[tn], 32 * (2 * i_n + par_n + 1))
                            if tn == 0:
                                pe.wait_ge(head_loaded[par_n], 16 * HEAD_DMAS * (i_n + 1))

                        def pv(j, k):
                            if k == 0:
                                pe.wait_ge(probsT_copied[j % 2], 4 * (n - 1) + j // 2 + 1)
                                if j % 4 == 0:
                                    wait_count(pe, ctx_copied, 2 * (n - 1) + j // 4 - 1)
                                if j == 0:
                                    pe.wait_ge(v_copied, 2 * i + w // 4 + (w % 4 > 0))
                            last = pe.matmul(bank[CTX_BANKS[j // 4]][0:D, (j % 4) * P:(j % 4 + 1) * P],
                                             v_h[:, par_p, j * TPB + k, :], probsT[:, j % 2, k, :],
                                             start=k == 0, stop=k == TPB - 1)
                            if k == TPB - 1:
                                last.then_inc(pv_made, 1)

                        for j in range(8 + 2):
                            if prev and j < 8:
                                if j < EARLY:
                                    pe.wait_ge(probs_ready, EARLY * (n - 1) + j + 1)
                                else:
                                    pe.wait_ge(late_probs_ready, (B - EARLY) * (n - 1) + j - EARLY + 1)
                                wait_count(pe, probsT_copied[j % 2], 4 * (n - 1) + j // 2)
                            for k in range(TPB if prev else 0):
                                if j < 8:
                                    last = pe.transpose(bank[T_BANKS[j % 2]][:, k * P:(k + 1) * P],
                                                        probs[:, (w - 1) % 2, j, k * P:(k + 1) * P], ident[:])
                                    if k == TPB - 1:
                                        last.then_inc(probs_transposed, 1)
                                if j >= 2:
                                    pv(j - 2, k)
                            if nxt and j < 8:
                                if j == 1 and cur:
                                    pe.wait_ge(scores_added, 8 * n + 6)
                                wait_count(pe, c2p_copied, 8 * (n + LEAD) + j - 1)
                                pe.matmul(bank[A_BANKS[j % 2]][:], q6[:, tn, 0, j, :], tab6[:, par_n, :], start=True, stop=True
                                          ).then_inc(c2p_made, 1)
                    each_step(pe, step)

                def copy_probsT(eng, copy, n, j):
                    eng.wait_ge(probs_transposed, 8 * n + j + 1)
                    wait_count(eng, pv_made, 8 * n + j - 1)
                    copy(probsT[:, j % 2], bank[T_BANKS[j % 2]][:].rearrange("p (k q) -> p k q", k=TPB)
                         ).then_inc(probsT_copied[j % 2], 1)

                @block.scalar
                def _(act):
                    def step(i, w):
                        n = 8 * i + w
                        nxt, prev = is_unit(n + LEAD), is_unit(n - 1)
                        pp = (w - 1) % 2
                        if prev:
                            act.wait_ge(neg_max_done, n)
                            wait_count(act, inv_done, 2 * (n - 2))
                            for j in range(B):
                                act.activation(probs[:, pp, j, :], probs[:, pp, j, :], ACT.Exp,
                                               bias=neg_max[:, pp, j:j + 1], scale=SCALE,
                                               accum_out=sums[:, pp, j:j + 1]).then_inc(exp_done, 1)
                            for j in range(EARLY, B):
                                act.wait_ge(inv_done, 2 * (n - 1) + 2)
                                act.activation(probs[:, pp, j, :], probs[:, pp, j, :], ACT.Copy,
                                               scale=inv_sums[:, pp, j:j + 1]).then_inc(late_probs_ready, 1)
                        for j in range(8):
                            if prev and j % 2 == 0:
                                copy_probsT(act, act.copy, n - 1, j)
                            if nxt:
                                act.wait_ge(c2p_made, 8 * (n + LEAD) + j + 1)
                                if j % 2 == 0:
                                    q = j // 2
                                    wait_count(act, c2p_written[q % 2], 16 * (2 * (n + LEAD) + q // 2))
                                    wait_count(act, far_copied, 4 * (n + LEAD) + q - 1)
                                act.copy(c2p_out[:, (j // 2) % 2, j % 2, :], bank[A_BANKS[j % 2]][:]).then_inc(c2p_copied, 1)
                    each_step(act, step)

                @block.vector
                def _(dve):
                    def step(i, w):
                        n = 8 * i + w
                        t, cp, pp = w % 4, w % 2, (w - 1) % 2
                        cur, prev = is_unit(n), is_unit(n - 1)
                        if cur:
                            dve.wait_ge(c2p_loaded[cp], 16 * (4 * i + w // 2 + 1))
                            dve.wait_ge(far_copied, 4 * (n + 1))
                            wait_count(dve, probs_transposed, 8 * (n - 1))
                        for j in range(8):
                            if cur:
                                if is_far(t, j):
                                    side = 0 if j // 2 < t else 1
                                    bias = c2p_far[:, cp, side, :].unsqueeze(2).broadcast_to([P, B, KCHUNK])
                                else:
                                    first = j * KCHUNK - (t - 1) * P
                                    bias = c2p[:, cp, :, first:first + KCHUNK]
                                dve.wait_ge(scores_made, 8 * n + j + 1)
                                dve.tensor_tensor(probs[:, cp, :, j * KCHUNK:(j + 1) * KCHUNK],
                                                  bank[j % SC][:].rearrange("p (b k) -> p b k", b=B), bias, ALU.add
                                                  ).then_inc(scores_added, 1)
                            if j == 1 and is_unit(n - 2):
                                copy_ctx(n - 2, 1)
                            if prev and j in (1, 3):
                                lo, hi = ((0, 2), (2, B))[j // 2]
                                dve.wait_ge(exp_done, 8 * (n - 1) + hi)
                                dve.reciprocal(inv_sums[:, pp, lo:hi], sums[:, pp, lo:hi]).then_inc(inv_done, 1)
                                dve.wait_ge(inv_done, 2 * (n - 1) + j // 2 + 1)
                            if prev and j % 2:
                                for b in range(j - 1, min(j + 1, EARLY)):
                                    dve.tensor_scalar(probs[:, pp, b, :], probs[:, pp, b, :], inv_sums[:, pp, b:b + 1],
                                                      None, ALU.mult).then_inc(probs_ready, 1)
                        if cur:
                            dve.wait_ge(scores_added, 8 * n + 8)
                        for j in range(B):
                            if cur:
                                dve.reduce_max(row_max[:, cp, j:j + 1], probs[:, cp, j, :], axis=AX.X).then_inc(max_done, 1)
                            if prev and j % 2:
                                copy_probsT(dve, dve.tensor_copy, n - 1, j)
                            if prev and j == 6:
                                copy_ctx(n - 1, 0)
                        if cur:
                            dve.wait_ge(max_done, 8 * n + 8)
                            dve.tensor_scalar(neg_max[:, cp, :], row_max[:, cp, :], -SCALE, None, ALU.mult
                                              ).then_inc(neg_max_done, 1)
                        if not cur and prev:
                            copy_ctx(n - 1, 1)

                    def copy_ctx(n, half):
                        dve.wait_ge(pv_made, 8 * n + 4 * half + 4)
                        if half == 0:
                            wait_count(dve, ctx_written, 16 * n)
                        dve.tensor_copy(ctxT[:, 4 * half:4 * half + 4, :],
                                        bank[CTX_BANKS[half]][0:D, :].rearrange("p (b q) -> p b q", b=4)
                                        ).then_inc(ctx_copied, 1)
                    dve.memset(kbd[:, 0], 0.0).then_inc(kbd_zeroed, 1)
                    each_step(dve, step)
        attn.close()
        end_stage()

        residual = sb(whole, "residual", [P, TILES, C])

        def row(name):
            return a[name].rearrange("(o n) -> o n", o=1).broadcast_to([P, a[name].shape[0]])

        HID = FFN // P
        LOW = 4
        with ExitStack() as st:
            ctx_in = sb(st, "p3_ctx", [P, 2, CC, S])
            n_in = sb(st, "p3_n", [P, 2, TPB, C])
            x_in = sb(st, "p3_x", [P, 2, TPB, C])
            n_bo, x_lb = sb(st, "p3_n_bo", [P, TPB, C]), sb(st, "p3_x_lb", [P, TPB, C])
            o = sb(st, "p3_o", [P, TPB, C])
            o_norm = sb(st, "p3_o_norm", [P, TPB, C])
            x1 = sb(st, "p3_x1", [P, TPB, C])
            x1_b2 = sb(st, "p3_x1_b2", [P, 2, TPB, C])
            y = sb(st, "p3_y", [P, TPB, C])
            yT = sb(st, "p3_yT", [P, 2, CC, S])
            hT = sb(st, "p3_hT", [P, HID, S])
            wo = sb(st, "p3_wo", [P, CC, C])
            w1, w2 = sb(st, "p3_w1", [P, CC, FFN]), sb(st, "p3_w2", [P, HID, C])
            w1_b, w2_b = sb(st, "p3_w1_b", [P, 2, CC, FFN]), sb(st, "p3_w2_b", [P, 2, HID, C])
            rows3 = sb(st, "p3_rows", [P, 4, C])
            b1 = sb(st, "p3_b1", [P, HID])
            scale = sb(st, "p3_scale", [P, 1])
            pick = sb(st, "p3_pick", [P, 2 * LOW, P])
            odd = sb(st, "p3_odd", [P, CC, 2 * LOW])
            lnA, lnB = layer_norm("ln2", st, TPB), layer_norm("ln3", st, TPB)
            w_loaded, pick_zeroed, pick_ready = sem("p3_w_loaded"), sem("p3_pick_zeroed"), sem("p3_pick_ready")
            in_loaded = [sem("p3_in_loaded0"), sem("p3_in_loaded1")]
            wo_made, n_bo_ready, x_lb_ready, o_ready, scaled, x1_ready, x1_b2_ready = [sem("p3_" + k) for k in (
                "wo_made", "n_bo_ready", "x_lb_ready", "o_ready", "scaled", "x1_ready", "x1_b2_ready")]
            yT_made, yT_ready, even_made, odd_ready, w1_ready, w_ready = [sem("p3_" + k) for k in (
                "yT_made", "yT_ready", "even_made", "odd_ready", "w1_ready", "w_ready")]
            ffn1_made, gelu_done, ffn2_made, x2_ready = [sem("p3_" + k) for k in (
                "ffn1_made", "gelu_done", "ffn2_made", "x2_ready")]
            O_BANKS, Y_BANKS, F_BANKS, G_BANKS = (0, 1), (2, 3), (4, 5), (6, 7)
            EVEN_BANKS = O_BANKS + Y_BANKS
            W_OPS = CC * LOW + HID * LOW

            def wait_count(eng, semaphore, count):
                if not isinstance(count, int) or count > 0:
                    eng.wait_ge(semaphore, count)

            with nc.Block() as block:
                @block.sync
                def _(sp):
                    def load(b, u):
                        wait_count(sp, wo_made, 2 * (b - 1))
                        wait_count(sp, n_bo_ready, b - 1)
                        wait_count(sp, x_lb_ready, b - 1)
                        sp.dma_start(ctx_in[:, u], ctxT_d[:, ds(b, 1), :].rearrange("(c p) b s -> p c (b s)", p=P)
                                     ).then_inc(in_loaded[u], 16)
                        sp.dma_start(n_in[:, u], normed_d[ds(b, 1)].rearrange("b p s c -> p (b s) c")
                                     ).then_inc(in_loaded[u], 16)
                        sp.dma_start(x_in[:, u], a["x"][ds(b, 1)].rearrange("b (s p) c -> p (b s) c", p=P)
                                     ).then_inc(in_loaded[u], 16)
                    batches(sp, load)

                @block.gpsimd
                def _(pool):
                    for k, n in enumerate(("bo", "ln_scale", "ln_bias", "b2")):
                        pool.dma_start(rows3[:, k, :], row(n)).then_inc(w_loaded, 16)
                    pool.dma_start(wo[:], a["wo"].rearrange("(c p) n -> p c n", p=P)).then_inc(w_loaded, 16)
                    pool.dma_start(w1[:], a["w1T"].rearrange("(c p) n -> p c n", p=P)).then_inc(w_loaded, 16)
                    pool.dma_start(w2[:], a["w2T"].rearrange("(c p) n -> p c n", p=P)).then_inc(w_loaded, 16)
                    pool.dma_start(b1[:], a["b1_col"]).then_inc(w_loaded, 16)
                    pool.dma_start(scale[:], row("scale")).then_inc(w_loaded, 16)
                    pool.memset(pick[:], 0.0).then_inc(pick_zeroed, 1)
                    pool.wait_ge(pick_zeroed, 1)
                    pool.affine_select(out=pick[:], in_=pick[:], compare_op=ALU.not_equal, fill=1.0, base=-1,
                                       pattern=[[-2, 2 * LOW], [0, P]], channel_multiplier=1).then_inc(pick_ready, 1)
                    pool.wait_ge(w_loaded, 16 * 9)

                    def across(k):
                        return rows3[:, k, :].unsqueeze(1).broadcast_to([P, TPB, C])

                    def body(b, u):
                        if isinstance(b, int):
                            pool.wait_ge(in_loaded[u], 48 * (b // 2 + 1))
                        else:
                            pool.wait_ge(in_loaded[u], 24 * (b - u) + 48)
                        wait_count(pool, o_ready, 2 * b)
                        apart(pool)
                        pool.tensor_tensor(n_bo[:], n_in[:, u], across(0), ALU.add).then_inc(n_bo_ready, 1)
                        wait_count(pool, x1_ready, b)
                        apart(pool)
                        pool.tensor_tensor(x_lb[:], x_in[:, u], across(2), ALU.add).then_inc(x_lb_ready, 1)
                        wait_count(pool, x2_ready, 2 * (b - 1))
                        pool.wait_ge(x1_ready, b + 1)
                        apart(pool)
                        pool.tensor_tensor(x1_b2[:, u], x1[:], across(3), ALU.add).then_inc(x1_b2_ready, 1)
                    batches(pool, body)

                @block.tensor
                def _(pe):
                    def project(b, u):
                        if isinstance(b, int):
                            pe.wait_ge(in_loaded[u], 48 * (b // 2 + 1))
                        else:
                            pe.wait_ge(in_loaded[u], 24 * (b - u) + 48)
                        wait_count(pe, w_ready, W_OPS * b)
                        for j in range(2):
                            for s in (2 * j, 2 * j + 1):
                                for c in range(CC):
                                    last = pe.matmul(bank[O_BANKS[j]][:, (s % 2) * C:(s % 2 + 1) * C],
                                                     ctx_in[:, u, c, s * P:(s + 1) * P], wo[:, c, :],
                                                     start=c == 0, stop=c == CC - 1)
                            last.then_inc(wo_made, 1)

                    def transpose(b, u):
                        pe.wait_ge(lnB["normed"], TPB * b + TPB)
                        for c in range(CC):
                            for s in range(TPB):
                                last = pe.transpose(bank[Y_BANKS[c]][:, s * P:(s + 1) * P], y[:, s, c * P:(c + 1) * P],
                                                    ident[:])
                            last.then_inc(yT_made, 1)
                        pe.wait_ge(yT_ready, CC * b + CC)
                        pe.wait_ge(o_ready, 2 * b + 2)
                        for i in range(2 * LOW):
                            last = pe.matmul(bank[EVEN_BANKS[i // 2]][:, (i % 2) * C:(i % 2 + 1) * C], pick[:, i, :],
                                             y[:, 0, :], start=True, stop=True)
                        last.then_inc(even_made, 1)

                    pe.wait_ge(w_loaded, 16 * 9)
                    pe.wait_ge(pick_ready, 1)
                    project(0, 0)
                    transpose(0, 0)
                    project(1, 1)

                    def body(b, u):
                        pe.wait_ge(w_ready, W_OPS * b + W_OPS)
                        for m in range(HID):
                            wait_count(pe, gelu_done, HID * b + m - 1)
                            for c in range(CC):
                                last = pe.matmul(bank[F_BANKS[m % 2]][:], w1_b[:, u, c, m * P:(m + 1) * P],
                                                 yT[:, u, c, :], start=c == 0, stop=c == CC - 1)
                            last.then_inc(ffn1_made, 1)
                        if exists(b, 1):
                            transpose(b + 1, 1 - u)
                        pe.wait_ge(gelu_done, HID * b + HID)
                        for j in range(2):
                            wait_count(pe, x2_ready, 2 * b + j - 1)
                            for s in (2 * j, 2 * j + 1):
                                for m in range(HID):
                                    last = pe.matmul(bank[G_BANKS[j]][:, (s % 2) * C:(s % 2 + 1) * C],
                                                     hT[:, m, s * P:(s + 1) * P], w2_b[:, u, m, :],
                                                     start=m == 0, stop=m == HID - 1)
                            last.then_inc(ffn2_made, 1)
                        if exists(b, 2):
                            project(b + 2, u)
                    batches(pe, body)

                @block.scalar
                def _(act):
                    def copy_yT(b, u):
                        wait_count(act, ffn1_made, HID * (b - 1))
                        for c in range(CC):
                            act.wait_ge(yT_made, CC * b + c + 1)
                            act.copy(yT[:, u, c, :], bank[Y_BANKS[c]][:]).then_inc(yT_ready, 1)

                    def gelu(b, m):
                        act.wait_ge(ffn1_made, HID * b + m + 1)
                        if m == 0:
                            wait_count(act, ffn2_made, 2 * b)
                        act.activation(hT[:, m, :], bank[F_BANKS[m % 2]][:], ACT.Gelu, bias=b1[:, m:m + 1]
                                       ).then_inc(gelu_done, 1)
                    ln_std(act, lnA, 0)
                    ln_std(act, lnB, 0)
                    copy_yT(0, 0)
                    act.wait_ge(w_loaded, 16 * 9)

                    def body(b, u):
                        if exists(b, 1):
                            ln_std(act, lnA, b + 1)
                        for m in range(HID // 2):
                            gelu(b, m)
                        if exists(b, 1):
                            ln_std(act, lnB, b + 1)
                        for m in range(HID // 2, HID):
                            gelu(b, m)
                        if exists(b, 1):
                            copy_yT(b + 1, 1 - u)
                    batches(act, body)

                @block.vector
                def _(dve):
                    def norms(b, u):
                        dve.wait_ge(n_bo_ready, b + 1)
                        for j in range(2):
                            dve.wait_ge(wo_made, 2 * b + j + 1)
                            dve.tensor_tensor(o[:, 2 * j:2 * j + 2, :],
                                              bank[O_BANKS[j]][:].rearrange("p (s c) -> p s c", s=2),
                                              n_bo[:, 2 * j:2 * j + 2, :], ALU.add).then_inc(o_ready, 1)
                        dve.wait_ge(o_ready, 2 * b + 2)
                        ln_moments(dve, lnA, b, lambda s: o[:, s, :], 1e-7)
                        ln_normalize(dve, lnA, b, lambda s: o[:, s, :], lambda s: o_norm[:, s, :])
                        dve.wait_ge(lnA["normed"], TPB * b + TPB)
                        dve.tensor_tensor(o_norm[:], o_norm[:], rows3[:, 1, :].unsqueeze(1).broadcast_to([P, TPB, C]),
                                          ALU.mult).then_inc(scaled, 1)
                        dve.wait_ge(scaled, b + 1)
                        dve.wait_ge(x_lb_ready, b + 1)
                        wait_count(dve, x1_b2_ready, b)
                        dve.tensor_tensor(x1[:], o_norm[:], x_lb[:], ALU.add).then_inc(x1_ready, 1)
                        dve.wait_ge(x1_ready, b + 1)
                        ln_moments(dve, lnB, b, lambda s: x1[:, s, :], 1e-5)
                        wait_count(dve, even_made, b)
                        ln_normalize(dve, lnB, b, lambda s: x1[:, s, :], lambda s: y[:, s, :])

                    def weights(b, u):
                        dve.wait_ge(yT_ready, CC * b + CC)
                        dve.tensor_scalar(odd[:], yT[:, u, :, 2:2 + 4 * LOW:2], scale[:], None, ALU.mult
                                          ).then_inc(odd_ready, 1)
                        dve.wait_ge(odd_ready, b + 1)
                        dve.wait_ge(even_made, b + 1)
                        wait_count(dve, ffn2_made, 2 * (b - 1))

                        def even(i):
                            return bank[EVEN_BANKS[i // 2]][:, (i % 2) * C:(i % 2 + 1) * C]
                        for c in range(CC):
                            for i in range(LOW):
                                dve.scalar_tensor_tensor(
                                    w1_b[:, u, c, i * C:(i + 1) * C], even(i), odd[:, c, i:i + 1],
                                    w1[:, c, i * C:(i + 1) * C], op0=ALU.mult, op1=ALU.add).then_inc(w_ready, 1)
                        for m in range(HID):
                            for i in range(LOW):
                                cols = slice(i * C // LOW, (i + 1) * C // LOW)
                                dve.scalar_tensor_tensor(
                                    w2_b[:, u, m, cols], even(LOW + i)[:, m // CC:C:LOW],
                                    odd[:, m % CC, LOW + i:LOW + i + 1], w2[:, m, cols],
                                    op0=ALU.mult, op1=ALU.add).then_inc(w_ready, 1)

                    dve.wait_ge(w_loaded, 16 * 9)
                    norms(0, 0)
                    weights(0, 0)

                    def body(b, u):
                        if exists(b, 1):
                            norms(b + 1, 1 - u)
                            weights(b + 1, 1 - u)
                        dve.wait_ge(x1_b2_ready, b + 1)
                        for j in range(2):
                            dve.wait_ge(ffn2_made, 2 * b + j + 1)
                            dve.tensor_tensor(residual[:, ds(b * TPB + 2 * j, 2), :],
                                              bank[G_BANKS[j]][:].rearrange("p (s c) -> p s c", s=2),
                                              x1_b2[:, u, 2 * j:2 * j + 2, :], ALU.add).then_inc(x2_ready, 1)
                    batches(dve, body)
        end_stage()


        def tile_of(n, g):
            return n * TPB + g

        TASK = 4
        QKV = 3 * C
        with ExitStack() as st:
            y = sb(st, "p4_y", [P, B, C])
            yT = sb(st, "p4_yT", [P, CC, B, P])
            qkv = sb(st, "p4_qkv", [P, 2, B, QKV])
            prod = sb(st, "p4_prod", [P, 2, B, C])
            score = sb(st, "p4_score", [P, B, H, B])
            top = sb(st, "p4_top", [P, B, H])
            total = sb(st, "p4_total", [P, B, H])
            attn_out = sb(st, "p4_attn", [P, 2, B, C])
            attnT = sb(st, "p4_attnT", [P, CC, B, P])
            wqkv, wproj = sb(st, "p4_wqkv", [P, CC, QKV]), sb(st, "p4_wproj", [P, CC, C])
            bqkv, bproj = sb(st, "p4_bqkv", [1, QKV]), sb(st, "p4_bproj", [1, C])
            ones = sb(st, "p4_ones", [1, P])
            ln = layer_norm("ln4", st, B)
            w_loaded, ones_ready = sem("p4_w_loaded"), sem("p4_ones_ready")
            yT_made, yT_ready, qkv_made, qkv_ready = [sem("p4_" + k) for k in (
                "yT_made", "yT_ready", "qkv_made", "qkv_ready")]
            q_times_k, scores_ready, top_ready, shifted, exp_done, total_ready, inv_ready, p_ready = [
                sem("p4_" + k) for k in ("q_times_k", "scores_ready", "top_ready", "shifted", "exp_done",
                                         "total_ready", "inv_ready", "p_ready")]
            p_times_v, out_ready, aT_made, aT_ready, proj_made, x3_ready = [sem("p4_" + k) for k in (
                "p_times_v", "out_ready", "aT_made", "aT_ready", "proj_made", "x3_ready")]
            Y_BANKS, QKV_BANKS, PROJ_BANK = (0, 1), ((2, 3), (4, 5)), 6
            BLOCKS = ((slice(0, TASK), slice(0, TASK)), (slice(TASK, B), slice(0, B)))

            def seen(n):
                return TASK if n < TASK else B

            with nc.Block() as block:
                @block.sync
                def _(sp):
                    sp.dma_start(wqkv[:], a["wqkvT"].rearrange("(c p) n -> p c n", p=P)).then_inc(w_loaded, 16)
                    sp.dma_start(wproj[:], a["wprojT"].rearrange("(c p) n -> p c n", p=P)).then_inc(w_loaded, 16)
                    sp.dma_start(bqkv[:], a["bqkv"].rearrange("(o n) -> o n", o=1)).then_inc(w_loaded, 16)
                    sp.dma_start(bproj[:], a["bproj"].rearrange("(o n) -> o n", o=1)).then_inc(w_loaded, 16)
                    sp.wait_ge(w_loaded, 64)

                @block.gpsimd
                def _(pool):
                    pool.memset(ones[:], 1.0).then_inc(ones_ready, 1)

                @block.tensor
                def _(pe):
                    def transposes(source, g, made, ready):
                        for q in range(4):
                            if 4 * g + q >= 2:
                                pe.wait_ge(ready, 4 * g + q - 1)
                            for k in range(4):
                                n, c = 4 * (q % 2) + k, q // 2
                                last = pe.transpose(bank[Y_BANKS[q % 2]][:, k * P:(k + 1) * P],
                                                    source[:, n, c * P:(c + 1) * P], ident[:])
                            last.then_inc(made, 1)

                    def qkv_of(g):
                        pe.wait_ge(ln["normed"], B * g + B)
                        if g:
                            pe.wait_ge(aT_ready, 4 * g - 4)
                        transposes(y, g, yT_made, yT_ready)
                        pe.wait_ge(yT_ready, 4 * g + 4)
                        for n in range(B):
                            if B * g + n >= 2:
                                pe.wait_ge(qkv_ready, 2 * (B * g + n) - 2)
                            for h, (lo, hi) in enumerate(((0, 512), (512, QKV))):
                                dst = bank[QKV_BANKS[n % 2][h]][:, 0:hi - lo]
                                for c in range(CC):
                                    pe.matmul(dst, yT[:, c, n, :], wqkv[:, c, lo:hi], start=c == 0, stop=False)
                                pe.matmul(dst, ones[:], bqkv[:, lo:hi], start=False, stop=True).then_inc(qkv_made, 1)

                    def project(g):
                        pe.wait_ge(out_ready, B * g + B)
                        pe.wait_ge(yT_ready, 4 * min(g + 2, TPB))
                        transposes(attn_out[:, g % 2], g, aT_made, aT_ready)
                        pe.wait_ge(aT_ready, 4 * g + 4)
                        for n in range(B):
                            half = bank[PROJ_BANK + n % 2][:, 0:C]
                            if B * g + n >= 2:
                                pe.wait_ge(x3_ready, B * g + n - 1)
                            for c in range(CC):
                                pe.matmul(half, attnT[:, c, n, :], wproj[:, c, :], start=c == 0, stop=False)
                            pe.matmul(half, ones[:], bproj[:], start=False, stop=True).then_inc(proj_made, 1)

                    pe.wait_ge(w_loaded, 64)
                    pe.wait_ge(ones_ready, 1)
                    qkv_of(0)
                    for g in range(TPB):
                        if g + 1 < TPB:
                            qkv_of(g + 1)
                        project(g)

                @block.scalar
                def _(act):
                    def copy_T(dst, g, made, ready):
                        for q in range(4):
                            act.wait_ge(made, 4 * g + q + 1)
                            act.copy(dst[:, q // 2, 4 * (q % 2):4 * (q % 2) + 4, :],
                                     bank[Y_BANKS[q % 2]][:].rearrange("p (n s) -> p n s", n=4)).then_inc(ready, 1)

                    def qkv_of(g):
                        ln_std(act, ln, g)
                        if g:
                            act.wait_ge(qkv_made, 2 * B * g)
                        copy_T(yT, g, yT_made, yT_ready)
                        if g >= 2:
                            act.wait_ge(out_ready, B * (g - 1))
                        for n in range(B):
                            for h, (lo, hi) in enumerate(((0, 512), (512, QKV))):
                                act.wait_ge(qkv_made, 2 * (B * g + n) + h + 1)
                                act.copy(qkv[:, g % 2, n, lo:hi], bank[QKV_BANKS[n % 2][h]][:, 0:hi - lo]
                                         ).then_inc(qkv_ready, 1)

                    def exponentials(g):
                        for k, (ns, ms) in enumerate(BLOCKS):
                            act.wait_ge(shifted, 2 * g + k + 1)
                            act.activation(score[:, ns, :, ms], score[:, ns, :, ms], ACT.Exp, scale=float(D) ** -0.5
                                           ).then_inc(exp_done, 1)

                    qkv_of(0)
                    for g in range(TPB):
                        exponentials(g)
                        if g + 1 < TPB:
                            qkv_of(g + 1)
                        if g:
                            act.wait_ge(proj_made, B * g)
                        copy_T(attnT, g, aT_made, aT_ready)

                @block.vector
                def _(dve):
                    def norm(g):
                        def source(n):
                            return residual[:, tile_of(n, g), :]
                        ln_moments(dve, ln, g, source, 1e-5)
                        if g:
                            dve.wait_ge(yT_made, 4 * g)
                        ln_normalize(dve, ln, g, source, lambda n: y[:, n, :])

                    def heads(x, m):
                        return x.rearrange("p m (h d) -> p m h d", h=H)

                    def attention(g):
                        u = g % 2
                        dve.wait_ge(qkv_ready, 2 * B * (g + 1))
                        q, k, v = (qkv[:, u, :, i * C:(i + 1) * C] for i in range(3))
                        for n in range(B):
                            m = seen(n)
                            if B * g + n >= 2:
                                dve.wait_ge(scores_ready, B * g + n - 1)
                            dve.tensor_tensor(prod[:, n % 2, 0:m, :], k[:, 0:m, :],
                                              q[:, n, :].unsqueeze(1).broadcast_to([P, m, C]), ALU.mult
                                              ).then_inc(q_times_k, 1)
                            dve.wait_ge(q_times_k, B * g + n + 1)
                            dve.reduce_sum(score[:, n, :, 0:m].rearrange("p h m -> p m h"),
                                           heads(prod[:, n % 2, 0:m, :], m), axis=AX.X).then_inc(scores_ready, 1)
                        dve.wait_ge(scores_ready, B * g + B)
                        for j, (ns, ms) in enumerate(BLOCKS):
                            size = [P, TASK, H, ms.stop]
                            dve.reduce_max(top[:, ns, :], score[:, ns, :, ms], axis=AX.X).then_inc(top_ready, 1)
                            dve.wait_ge(top_ready, 2 * g + j + 1)
                            dve.tensor_tensor(score[:, ns, :, ms], score[:, ns, :, ms],
                                              top[:, ns, :].unsqueeze(3).broadcast_to(size), ALU.subtract
                                              ).then_inc(shifted, 1)
                        if g:
                            add(g - 1)
                        if g + 1 < TPB:
                            norm(g + 1)
                        for j, (ns, ms) in enumerate(BLOCKS):
                            size = [P, TASK, H, ms.stop]
                            dve.wait_ge(exp_done, 2 * g + j + 1)
                            dve.reduce_sum(total[:, ns, :], score[:, ns, :, ms], axis=AX.X).then_inc(total_ready, 1)
                            dve.wait_ge(total_ready, 2 * g + j + 1)
                            dve.reciprocal(total[:, ns, :], total[:, ns, :]).then_inc(inv_ready, 1)
                            dve.wait_ge(inv_ready, 2 * g + j + 1)
                            dve.tensor_tensor(score[:, ns, :, ms], score[:, ns, :, ms],
                                              total[:, ns, :].unsqueeze(3).broadcast_to(size), ALU.mult
                                              ).then_inc(p_ready, 1)
                        dve.wait_ge(p_ready, 2 * g + 2)
                        if g >= 2:
                            dve.wait_ge(aT_made, 4 * (g - 1))
                        for n in range(B):
                            m = seen(n)
                            dve.tensor_tensor(heads(prod[:, n % 2, 0:m, :], m), heads(v[:, 0:m, :], m),
                                              score[:, n, :, 0:m].rearrange("p h m -> p m h").unsqueeze(3)
                                              .broadcast_to([P, m, H, D]), ALU.mult).then_inc(p_times_v, 1)
                            dve.wait_ge(p_times_v, B * g + n + 1)
                            dve.reduce_sum(attn_out[:, u, n, :], prod[:, n % 2, 0:m, :].rearrange("p m c -> p c m"),
                                           axis=AX.X).then_inc(out_ready, 1)

                    def add(g):
                        for n in range(B):
                            t = tile_of(n, g)
                            dve.wait_ge(proj_made, B * g + n + 1)
                            dve.tensor_tensor(residual[:, t, :], bank[PROJ_BANK + n % 2][:, 0:C], residual[:, t, :],
                                              ALU.add).then_inc(x3_ready, 1)
                    norm(0)
                    for g in range(TPB):
                        attention(g)
                    add(TPB - 1)
        end_stage()

        o_sorted_d = dram("o_sorted_d", [SLOT_TILES * P, C], F32)
        y_d = dram("y_d", [TILES * P, C], F32)
        HALF = TILES // 2
        WIDTH = 2 * CC * INNER + C
        with ExitStack() as st:
            slot = sb(st, "p5_slot", [P, TILES, TOP_K], U32)
            route_w = sb(st, "p5_route_w", [P, TILES, TOP_K])
            slot_tile = sb(st, "p5_slot_tile", [P, TILES, TOP_K])
            slot_row = sb(st, "p5_slot_row", [P, TILES, TOP_K])
            last_tile = sb(st, "p5_last_tile", [P, EXPERTS])
            tile_index = sb(st, "p5_tile_index", [P, SLOT_TILES])
            tile_expert = sb(st, "p5_tile_expert", [1, SLOT_TILES], I32)
            token = sb(st, "p5_token", [P, SLOT_TILES], U32)
            numbers = sb(st, "p5_numbers", [P, SLOT_TILES], BF16)
            tile_number = sb(st, "p5_tile_number", [P, TILES])
            own_number = sb(st, "p5_own_number", [P, 1])
            yT = sb(st, "p5_yT", [P, CC, B * S])
            with ExitStack() as pre:
                y = sb(pre, "p5_y", [P, 2, TPB, C])
                router = sb(pre, "p5_router", [P, CC, EXPERTS])
                bias = sb(pre, "p5_bias", [P, EXPERTS])
                before = sb(pre, "p5_before", [P, GROUPS, GROUPS])
                index = sb(pre, "p5_index", [P, EXPERTS])
                tile_start = sb(pre, "p5_tile_start", [P, TILES])
                score = sb(pre, "p5_score", [P, TILES, EXPERTS])
                sfc = sb(pre, "p5_sfc", [P, TILES, EXPERTS])
                best = sb(pre, "p5_best", [P, TILES, GROUPS, 8])
                pair = sb(pre, "p5_pair", [P, TILES, GROUPS])
                wins, ties = [sb(pre, n, [P, TILES, GROUPS, GROUPS]) for n in ("p5_wins", "p5_ties")]
                rank = sb(pre, "p5_rank", [P, TILES, GROUPS])
                top8 = sb(pre, "p5_top8", [P, TILES, 8])
                where = sb(pre, "p5_where", [P, TILES, 8], U32)
                where_f = sb(pre, "p5_where_f", [P, TILES, 8])
                hit = sb(pre, "p5_hit", [P, TOP_K, TILES, EXPERTS])
                picked = sb(pre, "p5_picked", [P, TOP_K, TILES, EXPERTS])
                norm_w = sb(pre, "p5_norm_w", [P, TILES])
                taken = sb(pre, "p5_taken", [P, EXPERTS, TILES])
                goes_on = sb(pre, "p5_goes_on", [P, EXPERTS, TILES])
                rank_e = sb(pre, "p5_rank_e", [P, EXPERTS, TILES])
                full = sb(pre, "p5_full", [P, EXPERTS, TILES])
                tiles_of, first = [sb(pre, n, [P, EXPERTS]) for n in ("p5_tiles_of", "p5_first")]
                slot_f = sb(pre, "p5_slot_f", [P, TILES, TOP_K])
                place = sb(pre, "p5_place", [P, 2, TILES, TOP_K], U32)
                earlier, ones = sb(pre, "p5_earlier", [P, P]), sb(pre, "p5_ones", [P, P])
                ln = layer_norm("ln5", pre, TPB)
                c_loaded, yT_made, yT_ready, logits_made, score_ready, step = [
                    sem("p5_" + k) for k in ("c_loaded", "yT_made", "yT_ready", "logits_made", "score_ready",
                                             "route_step")]
                y_stored = [sem(f"p5_y_stored{u}") for u in range(2)]
                ones_made, earlier_ready, counts_made = [sem("p5_" + k) for k in (
                    "ones_made", "earlier_ready", "counts_made")]
                ranked = sem("p5_ranked")
                Y_BANKS, L_BANKS, COUNT_BANK = ((0, 1), (2, 3)), (4, 5), 6

                with nc.Block() as block:
                    @block.vector
                    def _(dve):
                        dve.memset(goes_on[:], 1.0).then_inc(step, 1)
                        dve.wait_ge(step, 1)
                        dve.memset(goes_on[:, :, 0:1], 0.0).then_inc(step, 1)
                        for b in range(B):
                            def source(s):
                                return residual[:, b * TPB + s, :]
                            ln_moments(dve, ln, b, source, 1e-5)
                            if b >= 2:
                                dve.wait_ge(yT_made, CC * (b - 1))
                                dve.wait_ge(y_stored[b % 2], 16 * (b // 2))
                            ln_normalize(dve, ln, b, source, lambda s: y[:, b % 2, s, :])
                        dve.wait_ge(c_loaded, 16 * 8)
                        dve.wait_ge(score_ready, 2)
                        count = [2]

                        def signal(ins):
                            ins.then_inc(step, 1)
                            count[0] += 1

                        def wait_own():
                            dve.wait_ge(step, count[0])

                        def then(ins):
                            signal(ins)
                            wait_own()
                        then(dve.tensor_tensor(sfc[:], score[:], bias[:].unsqueeze(1).broadcast_to([P, TILES, EXPERTS]),
                                               ALU.add))
                        for t in range(TILES):
                            for g in range(GROUPS):
                                signal(dve.max(best[:, t, g, :], sfc[:, t, g * 8:(g + 1) * 8]))
                        wait_own()
                        then(dve.tensor_tensor(pair[:], best[:, :, :, 0], best[:, :, :, 1], ALU.add))
                        mine = pair[:].unsqueeze(3).broadcast_to([P, TILES, GROUPS, GROUPS])
                        other = pair[:].unsqueeze(2).broadcast_to([P, TILES, GROUPS, GROUPS])
                        dve.tensor_tensor(wins[:], other, mine, ALU.is_gt)
                        then(dve.tensor_tensor(ties[:], other, mine, ALU.is_equal))
                        then(dve.tensor_tensor(ties[:], ties[:], before[:].unsqueeze(1).broadcast_to(
                            [P, TILES, GROUPS, GROUPS]), ALU.mult))
                        then(dve.tensor_tensor(wins[:], wins[:], ties[:], ALU.add))
                        then(dve.reduce_sum(rank[:], wins[:], axis=AX.X))
                        then(dve.tensor_scalar(rank[:], rank[:], float(TOP_GROUPS), None, ALU.is_lt))
                        by_group = sfc[:].rearrange("p t (g e) -> p t g e", g=GROUPS)
                        then(dve.tensor_tensor(by_group, by_group, rank[:].unsqueeze(3).broadcast_to(
                            [P, TILES, GROUPS, EXPERTS // GROUPS]), ALU.mult))
                        then(dve.tensor_scalar(sfc[:], sfc[:], 0.0, None, ALU.add))
                        for t in range(TILES):
                            signal(dve.max(top8[:, t, :], sfc[:, t, :]))
                        wait_own()
                        for t in range(TILES):
                            signal(dve.max_index(where[:, t, :], top8[:, t, :], sfc[:, t, :]))
                        wait_own()
                        then(dve.tensor_copy(where_f[:], where[:]))
                        for k in range(TOP_K):
                            signal(dve.tensor_tensor(hit[:, k], index[:].unsqueeze(1).broadcast_to([P, TILES, EXPERTS]),
                                                     where_f[:, :, k:k + 1].broadcast_to([P, TILES, EXPERTS]),
                                                     ALU.is_equal))
                        wait_own()
                        by_tile = taken[:].rearrange("p e t -> p t e")
                        then(dve.tensor_tensor(by_tile, hit[:, 0], hit[:, 1], ALU.add))
                        for k in range(2, TOP_K):
                            then(dve.tensor_tensor(by_tile, by_tile, hit[:, k], ALU.add))
                        dve.tensor_tensor_scan(rank_e[:].rearrange("p e t -> p (e t)"),
                                               goes_on[:].rearrange("p e t -> p (e t)"),
                                               taken[:].rearrange("p e t -> p (e t)"), 0.0, ALU.mult, ALU.add
                                               ).then_inc(ranked, 1)
                        then(dve.tensor_tensor(picked[:], hit[:], score[:].unsqueeze(1).broadcast_to(
                            [P, TOP_K, TILES, EXPERTS]), ALU.mult))
                        then(dve.reduce_sum(route_w[:].rearrange("p t k -> p k t"), picked[:], axis=AX.X))
                        then(dve.reduce_sum(norm_w[:], route_w[:], axis=AX.X))
                        then(dve.tensor_scalar(norm_w[:], norm_w[:], 1e-20, None, ALU.add))
                        then(dve.reciprocal(norm_w[:], norm_w[:]))
                        then(dve.tensor_tensor(route_w[:], route_w[:], norm_w[:].unsqueeze(2).broadcast_to(
                            [P, TILES, TOP_K]), ALU.mult))
                        then(dve.tensor_scalar(route_w[:], route_w[:], ROUTE_SCALE, None, ALU.mult))
                        dve.wait_ge(counts_made, 2)
                        in_earlier, in_all = [bank[COUNT_BANK][:, k * EXPERTS:(k + 1) * EXPERTS] for k in range(2)]
                        then(dve.tensor_tensor(full[:], in_all.unsqueeze(2).broadcast_to([P, EXPERTS, TILES]),
                                               tile_start[:].unsqueeze(1).broadcast_to([P, EXPERTS, TILES]), ALU.is_gt))
                        then(dve.reduce_sum(tiles_of[:], full[:], axis=AX.X))
                        then(dve.tensor_tensor_scan(last_tile[:], ones[:, 0:EXPERTS], tiles_of[:], 0.0,
                                                    ALU.mult, ALU.add))
                        then(dve.tensor_tensor(first[:], last_tile[:], tiles_of[:], ALU.subtract))
                        then(dve.tensor_scalar(first[:], first[:], float(P), -1.0, ALU.mult, ALU.add))
                        then(dve.tensor_tensor(first[:], first[:], in_earlier, ALU.add))
                        then(dve.tensor_tensor(rank_e[:], rank_e[:], first[:].unsqueeze(2).broadcast_to(
                            [P, EXPERTS, TILES]), ALU.add))
                        then(dve.tensor_tensor(picked[:], hit[:], rank_e[:].rearrange("p e t -> p t e").unsqueeze(1)
                                               .broadcast_to([P, TOP_K, TILES, EXPERTS]), ALU.mult))
                        then(dve.reduce_sum(slot_f[:].rearrange("p t k -> p k t"), picked[:], axis=AX.X))
                        then(dve.tensor_copy(slot[:], slot_f[:]))
                        signal(dve.tensor_scalar(place[:, 0], slot[:], P.bit_length() - 1, None, ALU.logical_shift_right))
                        then(dve.tensor_scalar(place[:, 1], slot[:], P - 1, None, ALU.bitwise_and))
                        signal(dve.tensor_copy(slot_tile[:], place[:, 0]))
                        signal(dve.tensor_copy(slot_row[:], place[:, 1]))
                        signal(dve.tensor_copy(numbers[:], tile_index[:]))

                    @block.sync
                    def _(sp):
                        sp.dma_start(router[:], a["routerT"].rearrange("(c p) n -> p c n", p=P)).then_inc(c_loaded, 16)
                        sp.dma_start(bias[:], row("router_bias")).then_inc(c_loaded, 16)
                        sp.dma_start(before[:].rearrange("p g h -> p (g h)"), row("group_before")).then_inc(c_loaded, 16)
                        sp.dma_start(index[:], row("expert_index")).then_inc(c_loaded, 16)
                        sp.dma_start(tile_start[:], row("tile_start")).then_inc(c_loaded, 16)
                        sp.dma_start(tile_index[:], row("tile_index")).then_inc(c_loaded, 16)
                        sp.dma_start(tile_number[:], a["tile_index"][0:TILES].rearrange("(o n) -> o n", o=1)
                                     .broadcast_to([P, TILES])).then_inc(c_loaded, 16)
                        sp.dma_start(own_number[:], a["tile_index"][0:P].rearrange("(p o) -> p o", o=1)
                                     ).then_inc(c_loaded, 16)
                        for b in range(B):
                            sp.wait_ge(ln["normed"], TPB * b + TPB)
                            sp.dma_start(y_d[b * S:(b + 1) * S, :].rearrange("(t p) c -> p t c", p=P), y[:, b % 2]
                                         ).then_inc(y_stored[b % 2], 16)
                        for u in range(2):
                            sp.wait_ge(y_stored[u], 16 * B // 2)
                        sp.wait_ge(c_loaded, 16 * 8)

                    @block.gpsimd
                    def _(pool):
                        pool.memset(ones[:], 1.0).then_inc(ones_made, 1)
                        pool.wait_ge(ones_made, 1)
                        pool.affine_select(out=earlier[:], in_=ones[:], compare_op=ALU.is_gt, fill=0.0, base=0,
                                           pattern=[[1, P]], channel_multiplier=-1).then_inc(earlier_ready, 1)

                    @block.tensor
                    def _(pe):
                        pe.wait_ge(c_loaded, 16 * 8)
                        for b in range(B + 1):
                            if b < B:
                                u = b % 2
                                pe.wait_ge(ln["normed"], TPB * b + TPB)
                                if b >= 2:
                                    pe.wait_ge(yT_ready, CC * (b - 1))
                                for c in range(CC):
                                    for s in range(TPB):
                                        last = pe.transpose(bank[Y_BANKS[u][c]][:, s * P:(s + 1) * P],
                                                            y[:, u, s, c * P:(c + 1) * P], ident[:])
                                    last.then_inc(yT_made, 1)
                            if b:
                                pe.wait_ge(yT_ready, CC * b)
                                for t in range((b - 1) * TPB, b * TPB):
                                    for c in range(CC):
                                        last = pe.matmul(bank[L_BANKS[t // HALF]][:, (t % HALF) * EXPERTS:
                                                                                  (t % HALF + 1) * EXPERTS],
                                                         yT[:, c, t * P:(t + 1) * P], router[:, c, :],
                                                         start=c == 0, stop=c == CC - 1)
                                last.then_inc(logits_made, 1)
                        pe.wait_ge(earlier_ready, 1)
                        pe.wait_ge(ranked, 1)
                        for k, which in enumerate((earlier, ones)):
                            pe.matmul(bank[COUNT_BANK][:, k * EXPERTS:(k + 1) * EXPERTS], which[:],
                                      rank_e[:, :, TILES - 1], start=True, stop=True).then_inc(counts_made, 1)

                    @block.scalar
                    def _(act):
                        for b in range(B):
                            ln_std(act, ln, b)
                            for c in range(CC):
                                act.wait_ge(yT_made, CC * b + c + 1)
                                act.copy(yT[:, c, b * S:(b + 1) * S], bank[Y_BANKS[b % 2][c]][:]).then_inc(yT_ready, 1)
                        for half in range(2):
                            act.wait_ge(logits_made, B // 2 * (half + 1))
                            act.activation(score[:, half * HALF:(half + 1) * HALF, :],
                                           bank[L_BANKS[half]][:].rearrange("p (t e) -> p t e", e=EXPERTS), ACT.Sigmoid
                                           ).then_inc(score_ready, 1)

            w_all = sb(st, "p5_w_all", [P, EXPERTS, WIDTH])
            all_loaded = sem("p5_all_loaded")

            def tiles(eng, body):
                for u in range(2):
                    body(u, u, 0)
                with eng.Fori(1, TILES // 2) as i:
                    for u in range(2):
                        body(2 * i + u, u, i)

            def wait_count(eng, semaphore, count):
                if not isinstance(count, int) or count > 0:
                    eng.wait_ge(semaphore, count)

            with ExitStack() as tb:
                row_hot = sb(tb, "p5_row_hot", [P, 2, TOP_K, P], BF16)
                tile_hot = sb(tb, "p5_tile_hot", [P, 2, TOP_K, SLOT_TILES], BF16)
                scaled_hot = sb(tb, "p5_scaled_hot", [P, 2, 2, TOP_K, SLOT_TILES], BF16)
                token_f = sb(tb, "p5_token_f", [P, 2, SLOT_TILES])
                passed = sb(tb, "p5_passed", [P, 2, EXPERTS])
                experts_passed = sb(tb, "p5_experts_passed", [P, 2])
                expert_f = sb(tb, "p5_expert_f", [1, SLOT_TILES])
                hot_ready, scaled_ready, hot_used, token_step, expert_step = [sem("p5_" + k) for k in (
                    "hot_ready", "scaled_ready", "hot_used", "token_step", "expert_step")]
                experts_made = sem("p5_experts_made")
                TABLE_BANK, EXPERT_BANK = 0, 1

                with nc.Block() as block:
                    @block.tensor
                    def _(pe):
                        pe.wait_ge(expert_step, 3)
                        for half, n in enumerate((P, SLOT_TILES - P)):
                            pe.matmul(bank[EXPERT_BANK][0:1, half * P:half * P + n], experts_passed[:, half:half + 1],
                                      ident[:, 0:n], start=True, stop=True).then_inc(experts_made, 1)

                        def table(t, u, first=False, last_one=False):
                            pe.wait_ge(scaled_ready, t + 1)
                            for k in range(TOP_K):
                                last = pe.matmul(bank[TABLE_BANK][:, 0:2 * SLOT_TILES], row_hot[:, u, k, :],
                                                 scaled_hot[:, u, :, k, :], start=first and k == 0,
                                                 stop=last_one and k == TOP_K - 1)
                            last.then_inc(hot_used, 1)
                        for u in range(2):
                            table(u, u, first=u == 0)
                        with pe.Fori(1, TILES // 2 - 1) as i:
                            for u in range(2):
                                table(2 * i + u, u)
                        for u in range(2):
                            table(TILES - 2 + u, u, last_one=u == 1)

                    @block.scalar
                    def _(act):
                        for k in range(4):
                            n = EXPERTS // 4
                            act.dma_start(w_all[:, k * n:(k + 1) * n, :],
                                          a["experts"][k * n:(k + 1) * n].rearrange("e p n -> p e n")
                                          ).then_inc(all_loaded, 16)

                        def scale(t, u, i):
                            wait_count(act, hot_used, t - 1)
                            act.wait_ge(hot_ready, t + 1)
                            act.activation(scaled_hot[:, u, 0], tile_hot[:, u], ACT.Copy, scale=own_number[:])
                            act.activation(scaled_hot[:, u, 1], tile_hot[:, u], ACT.Copy, scale=tile_number[:, ds(t, 1)]
                                           ).then_inc(scaled_ready, 1)
                        tiles(act, scale)

                    @block.vector
                    def _(dve):
                        for half in range(2):
                            dve.tensor_scalar(passed[:, half, :], last_tile[:], float(-P * half), own_number[:],
                                              ALU.add, ALU.is_le).then_inc(expert_step, 1)
                        dve.wait_ge(expert_step, 2)
                        dve.reduce_sum(experts_passed[:], passed[:], axis=AX.X).then_inc(expert_step, 1)

                        def one_hots(t, u, i):
                            wait_count(dve, hot_used, t - 1)
                            for k in range(TOP_K):
                                its_row, its_tile = [x[:, ds(t, 1), k:k + 1].rearrange("p t k -> p (t k)")
                                                     for x in (slot_row, slot_tile)]
                                dve.tensor_scalar(row_hot[:, u, k, :], numbers[:, 0:P], its_row, None, ALU.is_equal)
                                last = dve.tensor_scalar(tile_hot[:, u, k, :], numbers[:], its_tile, None, ALU.is_equal)
                            last.then_inc(hot_ready, 1)
                        tiles(dve, one_hots)
                        dve.wait_ge(experts_made, 2)
                        dve.tensor_scalar(expert_f[:], bank[EXPERT_BANK][0:1, 0:SLOT_TILES], float(EXPERTS - 1), None,
                                          ALU.min).then_inc(expert_step, 1)
                        dve.wait_ge(expert_step, 4)
                        dve.tensor_copy(tile_expert[:], expert_f[:])
                        dve.wait_ge(hot_used, TILES)
                        dve.tensor_scalar(token_f[:, 0], bank[TABLE_BANK][:, SLOT_TILES:2 * SLOT_TILES], float(P), None,
                                          ALU.mult).then_inc(token_step, 1)
                        dve.wait_ge(token_step, 1)
                        dve.tensor_tensor(token_f[:, 1], token_f[:, 0], bank[TABLE_BANK][:, 0:SLOT_TILES], ALU.add
                                          ).then_inc(token_step, 1)
                        dve.wait_ge(token_step, 2)
                        dve.tensor_copy(token[:], token_f[:, 1])

            with ExitStack() as ex:
                w = sb(ex, "p5_w", [P, SHARED, WIDTH])
                s_silu = sb(ex, "p5_s_silu", [P, SHARED, S])
                s_hT = sb(ex, "p5_s_hT", [P, 2, SHARED, S])
                w_loaded = sem("p5_w_loaded")
                s_gate_made, s_up_made, s_silu_done, s_hT_ready, s_down_made, added = [sem("p5_s_" + k) for k in (
                    "gate_made", "up_made", "silu_done", "hT_ready", "down_made", "added")]
                G_BANKS, U_BANKS, D_BANKS = (0, 1), (2, 3), (4, 5)
                x_tile = sb(ex, "p5_x_tile", [P, 4, C])
                x_at = sb(ex, "p5_x_at", [P, 4, 1], U32)
                xT = sb(ex, "p5_xT", [P, 2, CC, P])
                silu = sb(ex, "p5_e_silu", [P, 2, INNER])
                h = sb(ex, "p5_h", [P, 2, INNER])
                hT = sb(ex, "p5_e_hT", [P, 2, P])
                o_pair = sb(ex, "p5_o_pair", [P, 2, 2, C])
                gathered = sb(ex, "p5_gathered", [P, 2, TOP_K, C])
                at = sb(ex, "p5_g_at", [P, 2, TOP_K], U32)
                x_loaded, x_at_ready = [sem(f"p5_x_loaded{w}") for w in range(4)], sem("p5_x_at_ready")
                o_stored = [sem(f"p5_o_stored{u}") for u in range(2)]
                all_computed, g_at_ready = sem("p5_all_computed"), sem("p5_g_at_ready")
                g_loaded, stored = [sem(f"p5_g_loaded{u}") for u in range(2)], sem("p5_stored")
                xT_made, xT_ready, gu_made, silu_done, h_ready, hT_made, hT_ready, o_made, o_ready, summed = [
                    sem("p5_e_" + k) for k in ("xT_made", "xT_ready", "gu_made", "silu_done", "h_ready", "hT_made",
                                               "hT_ready", "o_made", "o_ready", "summed")]
                X_BANKS, GU_BANKS, H_BANKS, O_BANKS = (0, 1), (2, 3), (4, 5), (6, 7)
                ROUNDS = SLOT_TILES // 4

                def each_step(eng, step):
                    step(-1, 3)
                    for w in range(4):
                        step(0, w)
                    with eng.Fori(1, ROUNDS - 1) as q:
                        for w in range(4):
                            step(q, w)
                    for w in range(4):
                        step(ROUNDS - 1, w)
                    for w in range(2):
                        step(ROUNDS, w)

                def is_tile(n):
                    return not isinstance(n, int) or 0 <= n < SLOT_TILES

                with nc.Block() as block:
                    @block.sync
                    def _(sp):
                        def rows(d, q, w):
                            return d[ds((4 * q + w) * P, 2 * P), :].rearrange("(s p) c -> p s c", p=P)

                        def step(q, w):
                            n = 4 * q + w
                            if w % 2 == 0 and is_tile(n - 2):
                                sp.wait_ge(o_ready, n)
                                sp.dma_start(rows(o_sorted_d, q - 1 + w // 2, 2 - w), o_pair[:, 1 - w // 2]
                                             ).then_inc(o_stored[1 - w // 2], 16)
                        for e in range(SHARED):
                            sp.dma_start(w[:, e, :], a["experts"][EXPERTS + e]).then_inc(w_loaded, 16)
                        each_step(sp, step)
                        for u in range(2):
                            sp.wait_ge(o_stored[u], 16 * ROUNDS)
                        sp.sem_inc(all_computed, 1)

                        def store(t, u, i):
                            sp.wait_ge(summed, TOP_K * (t + 1))
                            sp.dma_start(out.rearrange("b (s p) c -> (b s) p c", p=P)[ds(t, 1)].rearrange(
                                "t p c -> p (t c)"), residual[:, ds(t, 1), :].rearrange("p t c -> p (t c)")
                                         ).then_inc(stored, 16)
                        tiles(sp, store)
                        sp.wait_ge(stored, 16 * TILES)

                    @block.tensor
                    def _(pe):
                        def expert_of(n):
                            return nc.values_load(tile_expert[0:1, ds(n, 1)], engines=[mybir.EngineType.PE], min_val=0,
                                                  max_val=EXPERTS - 1,
                                                  skip_runtime_bounds_check_because="the router limits it")

                        def weights(e, lo, hi):
                            return w_all[:, ds(e, 1), lo:hi].rearrange("p e n -> p (e n)")

                        of_round = {}

                        def step(q, w):
                            n = 4 * q + w
                            if w == 0:
                                of_round.clear()
                            if is_tile(n + 1):
                                w1 = (w + 1) % 4
                                pe.wait_ge(x_loaded[w1], 16 * (q + 1 + (w == 3)))
                                for c in range(CC):
                                    last = pe.transpose(bank[X_BANKS[w1 % 2]][:, c * P:(c + 1) * P],
                                                        x_tile[:, w1, c * P:(c + 1) * P], ident[:])
                                last.then_inc(xT_made, 1)
                            if is_tile(n):
                                of_round[w] = expert_of(n)
                                pe.wait_ge(xT_ready, n + 1)
                                for c in range(CC):
                                    last = pe.matmul(bank[GU_BANKS[w % 2]][:, 0:2 * INNER], xT[:, w % 2, c, :],
                                                     weights(of_round[w], 2 * c * INNER, 2 * (c + 1) * INNER),
                                                     start=c == 0, stop=c == CC - 1)
                                last.then_inc(gu_made, 1)
                            if is_tile(n - 1):
                                pe.wait_ge(h_ready, n)
                                pe.transpose(bank[H_BANKS[(w + 1) % 2]][:, 0:P], h[:, (w + 1) % 2, :], ident[:]
                                             ).then_inc(hT_made, 1)
                            if is_tile(n - 2):
                                e = of_round[w - 2] if w >= 2 and w - 2 in of_round else expert_of(n - 2)
                                pe.wait_ge(hT_ready, n - 1)
                                wait_count(pe, o_ready, n - 3)
                                pe.matmul(bank[O_BANKS[w % 2]][:, 0:C], hT[:, w % 2, :],
                                          weights(e, 2 * CC * INNER, WIDTH), start=True, stop=True).then_inc(o_made, 1)
                        pe.wait_ge(all_loaded, 16 * 4)
                        each_step(pe, step)

                        pe.wait_ge(o_ready, SLOT_TILES)

                        def down(b, u):
                            pe.wait_ge(s_hT_ready, SHARED * (b + 1))
                            for j in range(2):
                                wait_count(pe, added, 2 * b + j - 1)
                                for s in (2 * j, 2 * j + 1):
                                    for e in range(SHARED):
                                        last = pe.matmul(bank[D_BANKS[j]][:, (s % 2) * C:(s % 2 + 1) * C],
                                                         s_hT[:, u, e, s * P:(s + 1) * P], w[:, e, 2 * CC * INNER:],
                                                         start=e == 0, stop=e == SHARED - 1)
                                last.then_inc(s_down_made, 1)

                        def shared(b, u):
                            for e in range(SHARED):
                                for first_w, banks, made, used in ((0, G_BANKS, s_gate_made, s_silu_done),
                                                                   (INNER, U_BANKS, s_up_made, s_hT_ready)):
                                    wait_count(pe, used, SHARED * (b - 1) + e + 1)
                                    for c in range(CC):
                                        at_w = 2 * c * INNER + first_w
                                        last = pe.matmul(bank[banks[e]][:], w[:, e, at_w:at_w + INNER],
                                                         yT[:, c, ds(b * S, S)], start=c == 0, stop=c == CC - 1)
                                    last.then_inc(made, 1)
                            if not isinstance(b, int) or b > 0:
                                down(b - 1, 1 - u)
                        pe.wait_ge(w_loaded, 16 * SHARED)
                        batches(pe, shared)
                        down(B - 1, 1)

                    @block.scalar
                    def _(act):
                        def step(q, w):
                            n = 4 * q + w
                            if is_tile(n + 1):
                                act.wait_ge(xT_made, n + 2)
                                wait_count(act, gu_made, n)
                                act.copy(xT[:, (w + 1) % 2].rearrange("p c s -> p (c s)"),
                                         bank[X_BANKS[(w + 1) % 2]][:, 0:CC * P]).then_inc(xT_ready, 1)
                            if is_tile(n):
                                act.wait_ge(gu_made, n + 1)
                                wait_count(act, h_ready, n - 1)
                                act.activation(silu[:, w % 2, :], bank[GU_BANKS[w % 2]][:, 0:INNER], ACT.Silu
                                               ).then_inc(silu_done, 1)
                        each_step(act, step)

                        def shared(b, u):
                            for e in range(SHARED):
                                act.wait_ge(s_gate_made, SHARED * b + e + 1)
                                wait_count(act, s_hT_ready, SHARED * (b - 1) + e + 1)
                                act.activation(s_silu[:, e, :], bank[G_BANKS[e]][:], ACT.Silu).then_inc(s_silu_done, 1)
                        batches(act, shared)

                    @block.vector
                    def _(dve):
                        def step(q, w):
                            n = 4 * q + w
                            if is_tile(n):
                                dve.wait_ge(silu_done, n + 1)
                                wait_count(dve, hT_made, n - 1)
                                dve.tensor_tensor(h[:, w % 2, :], bank[GU_BANKS[w % 2]][:, INNER:2 * INNER],
                                                  silu[:, w % 2, :], ALU.mult).then_inc(h_ready, 1)
                            if is_tile(n - 1):
                                dve.wait_ge(hT_made, n)
                                wait_count(dve, o_made, n - 2)
                                dve.tensor_copy(hT[:, (w + 1) % 2, :], bank[H_BANKS[(w + 1) % 2]][:, 0:P]
                                                ).then_inc(hT_ready, 1)
                            if is_tile(n - 2):
                                dve.wait_ge(o_made, n - 1)
                                u, q2 = 1 - w // 2, q - 1 + w // 2
                                if w % 2 == 0:
                                    wait_count(dve, o_stored[u], 16 * q2)
                                dve.tensor_copy(o_pair[:, u, w % 2, :], bank[O_BANKS[w % 2]][:, 0:C]
                                                ).then_inc(o_ready, 1)
                        each_step(dve, step)

                        def total(t, u, i):
                            dve.wait_ge(g_loaded[u], 16 * TOP_K * (i + 1))
                            for k in range(TOP_K):
                                if k:
                                    dve.wait_ge(summed, TOP_K * t + k)
                                x = residual[:, ds(t, 1), :].rearrange("p t c -> p (t c)")
                                dve.scalar_tensor_tensor(
                                    x, gathered[:, u, k, :], route_w[:, ds(t, 1), k:k + 1].rearrange("p t k -> p (t k)"),
                                    x, op0=ALU.mult, op1=ALU.add).then_inc(summed, 1)

                        def gather_sums(b):
                            for j in range(2):
                                dve.wait_ge(s_down_made, 2 * b + j + 1)
                                x = residual[:, ds(b * TPB + 2 * j, 2), :]
                                dve.tensor_tensor(x, x, bank[D_BANKS[j]][:].rearrange("p (s c) -> p s c", s=2),
                                                  ALU.add).then_inc(added, 1)
                            dve.wait_ge(added, 2 * b + 2)
                            for s in range(TPB):
                                total(b * TPB + s, s % 2, b * 2 + s // 2)

                        def finish(b, u):
                            for e in range(SHARED):
                                dve.wait_ge(s_silu_done, SHARED * b + e + 1)
                                dve.wait_ge(s_up_made, SHARED * b + e + 1)
                                if e == 0:
                                    wait_count(dve, s_down_made, 2 * (b - 1))
                                dve.tensor_tensor(s_hT[:, u, e, :], bank[U_BANKS[e]][:], s_silu[:, e, :], ALU.mult
                                                  ).then_inc(s_hT_ready, 1)
                            if not isinstance(b, int) or b > 0:
                                gather_sums(b - 1)
                        batches(dve, finish)
                        gather_sums(B - 1)

                    @block.gpsimd
                    def _(pool):
                        def load(q, w):
                            n = 4 * q + w
                            if not (isinstance(q, int) and q == 0):
                                pool.wait_ge(xT_made, n - 3)
                                apart(pool)
                            pool.tensor_copy(x_at[:, w, :], token[:, ds(n, 1)]).then_inc(x_at_ready, 1)
                            pool.wait_ge(x_at_ready, n + 1)
                            apart(pool)
                            pool.indirect_dma_start(x_tile[:, w, :], None, y_d,
                                                    bass.IndirectOffsetOnAxis(x_at[:, w, :], 0)
                                                    ).then_inc(x_loaded[w], 16)
                        for w in range(4):
                            load(0, w)
                        with pool.Fori(1, ROUNDS) as q:
                            for w in range(4):
                                load(q, w)
                        pool.wait_ge(all_computed, 1)

                        def gather(t, u, i):
                            if not isinstance(t, int):
                                pool.wait_ge(summed, TOP_K * (t - 1))
                                apart(pool)
                            pool.tensor_copy(at[:, u, :], slot[:, ds(t, 1), :].rearrange("p t k -> p (t k)")
                                             ).then_inc(g_at_ready, 1)
                            pool.wait_ge(g_at_ready, t + 1)
                            apart(pool)
                            for k in range(TOP_K):
                                pool.indirect_dma_start(
                                    gathered[:, u, k, :], None, o_sorted_d,
                                    bass.IndirectOffsetOnAxis(at[:, u, k:k + 1], 0)).then_inc(g_loaded[u], 16)
                        tiles(pool, gather)


PLAIN = {
    "x": "L0_attn_hidden_states", "wq": "L0_attn_Wq", "wk": "L0_attn_Wk", "wv": "L0_attn_Wv", "bk": "L0_attn_bk",
    "bv": "L0_attn_bv", "wo": "L0_attn_Wo", "bo": "L0_attn_bo", "ln_scale": "L0_attn_ln_scale",
    "ln_bias": "L0_attn_ln_bias", "b2": "L0_ffn_b2",
    "bqkv": "L1_attn_bqkv", "bproj": "L1_attn_bproj", "router_bias": "L1_ffn_router_bias",
}
COLUMNS = {"bq_col": "L0_attn_bq", "bk_col": "L0_attn_bk", "b1_col": "L0_ffn_b1"}
TRANSPOSED = {"relT": "L0_attn_rel_embeddings", "w1T": "L0_ffn_W1", "w2T": "L0_ffn_W2", "wqkvT": "L1_attn_Wqkv",
              "wprojT": "L1_attn_Wproj", "routerT": "L1_ffn_router_weight"}


def expert_weights(inputs):
    def by_row(w):
        e, n, k = w.shape
        return w.transpose(0, 2, 1).reshape(e, k // P, P, n).transpose(0, 2, 1, 3).reshape(e, P, -1)
    gate, up, down = (np.asarray(inputs["L1_ffn_" + k]) for k in ("gate_w", "up_w", "down_w"))
    s_gate, s_up, s_down = (np.asarray(inputs["L1_ffn_shared_" + k]) for k in ("gate_w", "up_w", "down_w"))
    gate = np.concatenate([gate, s_gate.reshape(SHARED, INNER, C)])
    up = np.concatenate([up, s_up.reshape(SHARED, INNER, C)])
    down = np.concatenate([down, s_down.reshape(C, SHARED, INNER).transpose(1, 0, 2)])
    ingoing = np.stack([by_row(gate).reshape(-1, P, CC, INNER), by_row(up).reshape(-1, P, CC, INNER)], axis=3)
    return np.ascontiguousarray(np.concatenate([ingoing.reshape(-1, P, 2 * CC * INNER), by_row(down)], axis=2))


def kernel(**inputs):
    import concourse.bacc as bacc
    from concourse import mybir
    from concourse.bass_utils import run_bass_kernel_spmd

    nc = bacc.Bacc("TRN2", target_bir_lowering=False, num_devices=1)
    arrays = {k: np.ascontiguousarray(inputs[n]) for k, n in PLAIN.items()}
    arrays["scale"] = np.ascontiguousarray(inputs["L0_ffn_scale"]).reshape(1)
    arrays.update({k: np.ascontiguousarray(np.asarray(inputs[n]).T) for k, n in TRANSPOSED.items()})
    arrays.update({k: np.ascontiguousarray(np.asarray(inputs[n]).reshape(-1, P).T) for k, n in COLUMNS.items()})
    arrays["experts"] = expert_weights(inputs)
    arrays["hot_c2p"], arrays["hot_p2c"] = one_hot_tables()
    arrays["group_before"] = (np.arange(GROUPS)[None, :] < np.arange(GROUPS)[:, None]).astype(np.float32).reshape(-1)
    arrays["expert_index"] = np.arange(EXPERTS, dtype=np.float32)
    arrays["tile_index"] = np.arange(SLOT_TILES, dtype=np.float32)
    arrays["tile_start"] = np.arange(TILES, dtype=np.float32) * P
    a = {k: nc.dram_tensor("in_" + k, v.shape, mybir.dt.from_np(v.dtype), kind="ExternalInput").ap()
         for k, v in arrays.items()}
    out = nc.dram_tensor("out", (B, S, C), mybir.dt.float32, kind="ExternalOutput").ap()
    build(nc, a, out)
    r = run_bass_kernel_spmd(nc, [{"in_" + k: v for k, v in arrays.items()}], core_ids=[0])
    return r.results[0]["out"]
```
